# Optimizing a Trainium2 kernel written in Bass

```python
import numpy as np
import jax
import jax.numpy as jnp

def _softmax(x, axis=-1):
    return jax.nn.softmax(x, axis=axis)

def _gelu(x):
    return jax.nn.gelu(x, approximate=True)

def _silu(x):
    return jax.nn.silu(x)

def _sigmoid(x):
    return jax.nn.sigmoid(x)

def _layernorm(x, axis=-1, eps=1e-05):
    m = jnp.mean(x, axis=axis, keepdims=True)
    v = jnp.var(x, axis=axis, keepdims=True)
    return (x - m) / jnp.sqrt(v + eps)

def _scatter_add(tgt, idx, src, axis=0):
    return tgt.at[idx].add(src)

def _segment_sum(src, seg, n):
    return jax.ops.segment_sum(src, seg, n)
kernel_name = 'mk_decoder_postln_d2_seqx_r8_3a3897'

def setup_inputs(seed: int=0):
    np.random.seed(seed)
    _w = jnp.asarray

    def _rec_inputs():
        import jax
        import jax.numpy as jnp
        _rk = jax.random.key(seed)
        x = -0.0005207 + 1.001 * jax.random.normal(jax.random.fold_in(_rk, 1), (32, 128, 128), jnp.float32)
        _lenS = 128 - jax.random.randint(jax.random.fold_in(_rk, 7), (32,), 0, max(1, 128 // 4) + 1, jnp.int32)
        _lenS2 = 77 - jax.random.randint(jax.random.fold_in(_rk, 8), (32,), 0, max(1, 77 // 4) + 1, jnp.int32)
        _ctx_1024P = jax.random.normal(jax.random.fold_in(_rk, 11), (32, 16, 128), jnp.float32)
        _ctx_1024c = jax.random.dirichlet(jax.random.fold_in(_rk, 511), 0.3 * jnp.ones((16,), jnp.float32), (32, 77))
        _ctx_1024t = jnp.einsum('bsk,bkd->bsd', _ctx_1024c, _ctx_1024P)
        _ctx_1024t = _ctx_1024t * jax.lax.rsqrt(jnp.mean(jnp.square(_ctx_1024t)) + 1e-12) * 0.953939
        ctx_1024 = -0.000514642 + 1.00011 * (_ctx_1024t + 0.3 * jax.random.normal(jax.random.fold_in(_rk, 611), (32, 77, 128), jnp.float32))
        _validS = jnp.arange(128)[None, :] < _lenS[:, None]
        _validS2 = jnp.arange(77)[None, :] < _lenS2[:, None]
        _causal = jnp.tril(jnp.ones((128, 128), dtype=bool))
        mask_Bx1x1xS2_if1 = jnp.where(jnp.ones((32, 1, 1, 77), dtype=bool), 1, 0).astype(jnp.int32)
        return (x, ctx_1024, mask_Bx1x1xS2_if1)
    x, ctx_1024, mask_Bx1x1xS2_if1 = _rec_inputs()

    def _L0_attn_setup():
        import jax, jax.numpy as jnp
        import numpy as np
        B, S, D = (2, 256, 128)
        H, DQ, DV = (16, 64, 64)
        key = jax.random.key(seed)
        k1, k2, k3, k4, k5 = jax.random.split(key, 5)
        scale = 0.02
        return {'x': jax.random.normal(k1, (B, S, D), dtype=jnp.float32), 'w_q': jax.random.normal(k2, (H, DQ, D), dtype=jnp.float32) * scale, 'w_k': jax.random.normal(k3, (H, DQ, D), dtype=jnp.float32) * scale, 'w_v': jax.random.normal(k4, (H, DV, D), dtype=jnp.float32) * scale, 'w_o': jax.random.normal(k5, (D, H * DV), dtype=jnp.float32) * scale}
    _L0_attn_all = _L0_attn_setup()
    _L0_attn_in = {k: v for k, v in _L0_attn_all.items() if k in ('w_q', 'w_k', 'w_v', 'w_o')}
    del _L0_attn_all

    def _L0_xattn_setup():
        import jax, jax.numpy as jnp
        import numpy as np
        import math
        B, S, D, H = (1, 256, 128, 16)
        DK = D // H
        DH = 64
        LOG_T_MIN = math.log(0.1)
        LOG_T_MAX = math.log(10.0)

        def _linear(x, W, b):
            return x @ W.T + b
        key = jax.random.key(seed)
        ks = jax.random.split(key, 20)
        p = 0.02
        return {'query': jax.random.normal(ks[0], (B, S, D), jnp.float32), 'key': jax.random.normal(ks[1], (B, S, D), jnp.float32), 'value': jax.random.normal(ks[2], (B, S, D), jnp.float32), 'Wq': jax.random.normal(ks[3], (D, D), jnp.float32) * p, 'bq': jax.random.normal(ks[4], (D,), jnp.float32) * p, 'Wk': jax.random.normal(ks[5], (D, D), jnp.float32) * p, 'bk': jax.random.normal(ks[6], (D,), jnp.float32) * p, 'Wv': jax.random.normal(ks[7], (D, D), jnp.float32) * p, 'bv': jax.random.normal(ks[8], (D,), jnp.float32) * p, 'Wo': jax.random.normal(ks[9], (D, D), jnp.float32) * p, 'bo': jax.random.normal(ks[10], (D,), jnp.float32) * p, 'w1': jax.random.normal(ks[11], (DH, 3), jnp.float32) * 0.3, 'b1': jax.random.normal(ks[12], (DH,), jnp.float32) * 0.1, 'w2': jax.random.normal(ks[13], (DH, DH), jnp.float32) * 0.1, 'b2': jax.random.normal(ks[14], (DH,), jnp.float32) * 0.1, 'w3': jax.random.normal(ks[15], (1, DH), jnp.float32) * 0.1, 'b3': jnp.full((1,), (LOG_T_MIN + LOG_T_MAX) / 2, jnp.float32)}
    _L0_xattn_all = _L0_xattn_setup()
    _L0_xattn_in = {k: v for k, v in _L0_xattn_all.items() if k in ('Wq', 'bq', 'Wk', 'bk', 'Wv', 'bv', 'Wo', 'bo', 'w1', 'b1', 'w2', 'b2', 'w3', 'b3')}
    del _L0_xattn_all

    def _L0_ffn_setup():
        import jax, jax.numpy as jnp
        import numpy as np
        K_TOP = 2
        key = jax.random.key(seed)
        k1, k2, k3 = jax.random.split(key, 3)
        B, S, H, E = (4, 256, 128, 8)
        hidden_states = jax.random.normal(k1, (B, S, H), dtype=jnp.float32)
        router_w = jax.random.normal(k2, (E, H), dtype=jnp.float32) * 0.02
        expert_weights = jax.random.normal(k3, (E, H, H), dtype=jnp.float32) * 0.02
        return {'hidden_states': hidden_states, 'router_w': router_w, 'expert_weights': expert_weights}
    _L0_ffn_all = _L0_ffn_setup()
    _L0_ffn_in = {k: v for k, v in _L0_ffn_all.items() if k in ('router_w', 'expert_weights')}
    del _L0_ffn_all

    def _L1_attn_setup():
        import jax, jax.numpy as jnp
        import numpy as np
        B_, L_, D_MODEL = (2, 256, 128)
        D_INNER, D_STATE, D_CONV, DT_RANK = (256, 16, 4, 64)

        def _mamba(hidden_states, in_proj_w, conv_w, conv_b, x_proj_w, dt_proj_w, dt_proj_b, A_log, D, out_proj_w):
            B, L, _ = hidden_states.shape
            xz = jnp.einsum('bld,ed->bel', hidden_states, in_proj_w)
            x, z = jnp.split(xz, 2, axis=1)
            xp = jnp.pad(x, ((0, 0), (0, 0), (D_CONV - 1, 0)))
            xc = jax.lax.conv_general_dilated(xp, conv_w, (1,), 'VALID', dimension_numbers=('NCH', 'OIH', 'NCH'), feature_group_count=D_INNER)
            x = jax.nn.silu(xc + conv_b[None, :, None])
            x_dbl = jnp.einsum('bdl,kd->bkl', x, x_proj_w)
            dt_in = x_dbl[:, :DT_RANK]
            Bm = x_dbl[:, DT_RANK:DT_RANK + D_STATE]
            Cm = x_dbl[:, DT_RANK + D_STATE:]
            delta = jnp.einsum('brl,dr->bdl', dt_in, dt_proj_w)
            delta = jax.nn.softplus(delta + dt_proj_b[None, :, None])
            A = -jnp.exp(A_log)
            dA = jnp.exp(jnp.einsum('bdl,dn->lbdn', delta, A))
            dBu = jnp.einsum('bdl,bnl,bdl->lbdn', delta, Bm, x)
            C_t = jnp.transpose(Cm, (2, 0, 1))

            def step(h, inp):
                dA_t, dBu_t, c_t = inp
                h = dA_t * h + dBu_t
                y = jnp.einsum('bdn,bn->bd', h, c_t)
                return (h, y)
            h0 = jnp.zeros((B, D_INNER, D_STATE), delta.dtype)
            _, ys = jax.lax.scan(step, h0, (dA, dBu, C_t))
            y = jnp.transpose(ys, (1, 2, 0))
            y = y + x * D[None, :, None]
            y = y * jax.nn.silu(z)
            return jnp.einsum('bdl,od->blo', y, out_proj_w)
        key = jax.random.key(seed)
        ks = jax.random.split(key, 8)
        hidden_states = jax.random.normal(ks[0], (B_, L_, D_MODEL), jnp.float32)
        in_proj_w = jax.random.normal(ks[1], (2 * D_INNER, D_MODEL), jnp.float32) * D_MODEL ** (-0.5)
        conv_w = jax.random.normal(ks[2], (D_INNER, 1, D_CONV), jnp.float32) * D_CONV ** (-0.5)
        conv_b = jnp.zeros((D_INNER,), jnp.float32)
        x_proj_w = jax.random.normal(ks[3], (DT_RANK + 2 * D_STATE, D_INNER), jnp.float32) * D_INNER ** (-0.5)
        dt_std = DT_RANK ** (-0.5)
        dt_proj_w = jax.random.uniform(ks[4], (D_INNER, DT_RANK), jnp.float32, -dt_std, dt_std)
        dt = jnp.exp(jax.random.uniform(ks[5], (D_INNER,), jnp.float32) * (np.log(0.1) - np.log(0.001)) + np.log(0.001))
        dt_proj_b = dt + jnp.log(-jnp.expm1(-dt))
        A_log = jnp.log(jnp.broadcast_to(jnp.arange(1, D_STATE + 1, dtype=jnp.float32), (D_INNER, D_STATE)))
        D = jnp.ones((D_INNER,), jnp.float32)
        out_proj_w = jax.random.normal(ks[6], (D_MODEL, D_INNER), jnp.float32) * D_INNER ** (-0.5)
        return dict(hidden_states=hidden_states, in_proj_w=in_proj_w, conv_w=conv_w, conv_b=conv_b, x_proj_w=x_proj_w, dt_proj_w=dt_proj_w, dt_proj_b=dt_proj_b, A_log=A_log, D=D, out_proj_w=out_proj_w)
    _L1_attn_all = _L1_attn_setup()
    _L1_attn_in = {k: v for k, v in _L1_attn_all.items() if k in ('in_proj_w', 'conv_w', 'conv_b', 'x_proj_w', 'dt_proj_w', 'dt_proj_b', 'A_log', 'D', 'out_proj_w')}
    del _L1_attn_all

    def _L1_xattn_setup():
        import jax, jax.numpy as jnp
        import numpy as np
        N, S, E, H = (4, 256, 128, 16)
        D = E // H
        SCALE = E ** 0.5
        key = jax.random.key(seed)
        ks = jax.random.split(key, 8)
        return {'values': jax.random.normal(ks[0], (N, S, E), dtype=jnp.float32), 'keys': jax.random.normal(ks[1], (N, S, E), dtype=jnp.float32), 'queries': jax.random.normal(ks[2], (N, S, E), dtype=jnp.float32), 'mask': jnp.ones((N, 1, 1, S), dtype=jnp.int32), 'Wv': jax.random.normal(ks[3], (D, D), dtype=jnp.float32) * D ** (-0.5), 'Wk': jax.random.normal(ks[4], (D, D), dtype=jnp.float32) * D ** (-0.5), 'Wq': jax.random.normal(ks[5], (D, D), dtype=jnp.float32) * D ** (-0.5), 'Wo': jax.random.normal(ks[6], (E, E), dtype=jnp.float32) * E ** (-0.5), 'bo': jnp.zeros((E,), dtype=jnp.float32)}
    _L1_xattn_all = _L1_xattn_setup()
    _L1_xattn_in = {k: v for k, v in _L1_xattn_all.items() if k in ('Wv', 'Wk', 'Wq', 'Wo', 'bo')}
    del _L1_xattn_all

    def _L1_ffn_setup():
        import jax, jax.numpy as jnp
        import numpy as np
        D = 128
        H = 128
        E = 8
        K = 2
        I = 2 * 128
        ROUTE_SCALE = 1.0
        key = jax.random.key(seed)
        ks = jax.random.split(key, 12)
        s = lambda *sh: 1.0 / np.sqrt(sh[-1])
        return {'x': jax.random.normal(ks[0], (1, 256, D), jnp.float32), 'gate_w': jax.random.normal(ks[1], (E, D), jnp.float32) * s(E, D), 'w1': jax.random.normal(ks[2], (E, H, D), jnp.float32) * s(H, D), 'b1': jax.random.normal(ks[3], (E, H), jnp.float32) * 0.01, 'w2': jax.random.normal(ks[4], (E, D, H), jnp.float32) * s(D, H), 'b2': jax.random.normal(ks[5], (E, D), jnp.float32) * 0.01, 'w3': jax.random.normal(ks[6], (E, H, D), jnp.float32) * s(H, D), 'b3': jax.random.normal(ks[7], (E, H), jnp.float32) * 0.01, 'sw1': jax.random.normal(ks[8], (I, D), jnp.float32) * s(I, D), 'sw2': jax.random.normal(ks[9], (I, D), jnp.float32) * s(I, D), 'sw3': jax.random.normal(ks[10], (D, I), jnp.float32) * s(D, I)}
    _L1_ffn_all = _L1_ffn_setup()
    _L1_ffn_in = {k: v for k, v in _L1_ffn_all.items() if k in ('gate_w', 'w1', 'b1', 'w2', 'b2', 'w3', 'b3', 'sw1', 'sw2', 'sw3')}
    del _L1_ffn_all
    return {'x': x, 'ctx_1024': ctx_1024, 'mask_Bx1x1xS2_if1': mask_Bx1x1xS2_if1, 'L0_attn_w_q': _L0_attn_in['w_q'], 'L0_attn_w_k': _L0_attn_in['w_k'], 'L0_attn_w_v': _L0_attn_in['w_v'], 'L0_attn_w_o': _L0_attn_in['w_o'], 'L0_xattn_Wq': _L0_xattn_in['Wq'], 'L0_xattn_bq': _L0_xattn_in['bq'], 'L0_xattn_Wk': _L0_xattn_in['Wk'], 'L0_xattn_bk': _L0_xattn_in['bk'], 'L0_xattn_Wv': _L0_xattn_in['Wv'], 'L0_xattn_bv': _L0_xattn_in['bv'], 'L0_xattn_Wo': _L0_xattn_in['Wo'], 'L0_xattn_bo': _L0_xattn_in['bo'], 'L0_xattn_w1': _L0_xattn_in['w1'], 'L0_xattn_b1': _L0_xattn_in['b1'], 'L0_xattn_w2': _L0_xattn_in['w2'], 'L0_xattn_b2': _L0_xattn_in['b2'], 'L0_xattn_w3': _L0_xattn_in['w3'], 'L0_xattn_b3': _L0_xattn_in['b3'], 'L0_ffn_router_w': _L0_ffn_in['router_w'], 'L0_ffn_expert_weights': _L0_ffn_in['expert_weights'], 'L1_attn_in_proj_w': _L1_attn_in['in_proj_w'], 'L1_attn_conv_w': _L1_attn_in['conv_w'], 'L1_attn_conv_b': _L1_attn_in['conv_b'], 'L1_attn_x_proj_w': _L1_attn_in['x_proj_w'], 'L1_attn_dt_proj_w': _L1_attn_in['dt_proj_w'], 'L1_attn_dt_proj_b': _L1_attn_in['dt_proj_b'], 'L1_attn_A_log': _L1_attn_in['A_log'], 'L1_attn_D': _L1_attn_in['D'], 'L1_attn_out_proj_w': _L1_attn_in['out_proj_w'], 'L1_xattn_Wv': _L1_xattn_in['Wv'], 'L1_xattn_Wk': _L1_xattn_in['Wk'], 'L1_xattn_Wq': _L1_xattn_in['Wq'], 'L1_xattn_Wo': _L1_xattn_in['Wo'], 'L1_xattn_bo': _L1_xattn_in['bo'], 'L1_ffn_gate_w': _L1_ffn_in['gate_w'], 'L1_ffn_w1': _L1_ffn_in['w1'], 'L1_ffn_b1': _L1_ffn_in['b1'], 'L1_ffn_w2': _L1_ffn_in['w2'], 'L1_ffn_b2': _L1_ffn_in['b2'], 'L1_ffn_w3': _L1_ffn_in['w3'], 'L1_ffn_b3': _L1_ffn_in['b3'], 'L1_ffn_sw1': _L1_ffn_in['sw1'], 'L1_ffn_sw2': _L1_ffn_in['sw2'], 'L1_ffn_sw3': _L1_ffn_in['sw3']}

def reference(x, ctx_1024, mask_Bx1x1xS2_if1, L0_attn_w_q, L0_attn_w_k, L0_attn_w_v, L0_attn_w_o, L0_xattn_Wq, L0_xattn_bq, L0_xattn_Wk, L0_xattn_bk, L0_xattn_Wv, L0_xattn_bv, L0_xattn_Wo, L0_xattn_bo, L0_xattn_w1, L0_xattn_b1, L0_xattn_w2, L0_xattn_b2, L0_xattn_w3, L0_xattn_b3, L0_ffn_router_w, L0_ffn_expert_weights, L1_attn_in_proj_w, L1_attn_conv_w, L1_attn_conv_b, L1_attn_x_proj_w, L1_attn_dt_proj_w, L1_attn_dt_proj_b, L1_attn_A_log, L1_attn_D, L1_attn_out_proj_w, L1_xattn_Wv, L1_xattn_Wk, L1_xattn_Wq, L1_xattn_Wo, L1_xattn_bo, L1_ffn_gate_w, L1_ffn_w1, L1_ffn_b1, L1_ffn_w2, L1_ffn_b2, L1_ffn_w3, L1_ffn_b3, L1_ffn_sw1, L1_ffn_sw2, L1_ffn_sw3):
    import jax
    import jax.numpy as jnp

    def _L0_attn_ref(x, w_q, w_k, w_v, w_o):
        import jax, jax.numpy as jnp
        import numpy as np
        B, S, D = (2, 256, 128)
        H, DQ, DV = (16, 64, 64)
        b, s, d = x.shape
        q = jnp.einsum('bsd,hqd->bhsq', x, w_q)
        k = jnp.einsum('bsd,hqd->bhsq', x, w_k)
        v = jnp.einsum('bsd,hvd->bhsv', x, w_v)
        scores = jnp.einsum('bhsq,bhtq->bhst', q, k)
        causal = jnp.triu(jnp.ones((s, s), dtype=bool), k=1)
        masked = jnp.where(causal, -jnp.inf, scores)
        dq = w_q.shape[1]
        weights = jax.nn.softmax(masked / jnp.sqrt(jnp.float32(dq)), axis=-1)
        out = jnp.einsum('bhst,bhtv->bhsv', weights, v)
        cat = out.transpose(0, 2, 1, 3).reshape(b, s, -1)
        return jnp.einsum('bsf,df->bsd', cat, w_o)

    def _L0_xattn_ref(query, key, value, Wq, bq, Wk, bk, Wv, bv, Wo, bo, w1, b1, w2, b2, w3, b3):
        import jax, jax.numpy as jnp
        import numpy as np
        import math
        B, S, D, H = (1, 256, 128, 16)
        DK = D // H
        DH = 64
        LOG_T_MIN = math.log(0.1)
        LOG_T_MAX = math.log(10.0)

        def _linear(x, W, b):
            return x @ W.T + b
        b, sq, d = query.shape
        sk = key.shape[1]
        h, dk = (H, DK)
        Q = _linear(query, Wq, bq).reshape(b, sq, h, dk).transpose(0, 2, 1, 3)
        K = _linear(key, Wk, bk).reshape(b, sk, h, dk).transpose(0, 2, 1, 3)
        V = _linear(value, Wv, bv).reshape(b, sk, h, dk).transpose(0, 2, 1, 3)
        qk = jnp.einsum('bhqd,bhkd->bhqk', Q, K)
        scores = qk / math.sqrt(dk)
        mean_sim = scores.mean(axis=(-2, -1))
        max_sim = scores.max(axis=-1).mean(axis=-1)
        probs = jax.nn.softmax(scores, axis=-1)
        entropy_proxy = jnp.var(probs, axis=-1, ddof=1).mean(axis=-1)
        feats = jnp.stack([mean_sim, max_sim, entropy_proxy], axis=-1)
        hidden = jax.nn.gelu(_linear(feats, w1, b1), approximate=False)
        hidden = jax.nn.gelu(_linear(hidden, w2, b2), approximate=False)
        log_t = jnp.clip(_linear(hidden, w3, b3), LOG_T_MIN, LOG_T_MAX)
        t = jnp.exp(log_t)[..., None]
        attn_scores = qk / (2.0 * t)
        attn = jax.nn.softmax(attn_scores, axis=-1)
        attn = jnp.nan_to_num(attn, nan=0.0)
        out = jnp.einsum('bhqk,bhkd->bhqd', attn, V)
        out = out.transpose(0, 2, 1, 3).reshape(b, sq, d)
        return _linear(out, Wo, bo)

    def _L0_ffn_ref(hidden_states, router_w, expert_weights):
        import jax, jax.numpy as jnp
        import numpy as np
        K_TOP = 2
        B, S, H = hidden_states.shape
        x = hidden_states.reshape(-1, H)
        logits = x @ router_w.T
        probs = jax.nn.softmax(logits, axis=-1)
        topk_vals, topk_idx = jax.lax.top_k(probs, K_TOP)
        topk_w = topk_vals / (topk_vals.sum(-1, keepdims=True) + 1e-06)
        expert_out = jnp.einsum('nh,eho->eno', x, expert_weights)
        combined = jnp.take_along_axis(expert_out.transpose(1, 0, 2), topk_idx[:, :, None], axis=1)
        combined = combined.transpose(1, 0, 2)
        remap_bias = jnp.take_along_axis(probs, topk_idx, axis=1).T[:, :, None]
        weights = topk_w.T[:, :, None]
        out = ((combined + remap_bias) * weights).sum(axis=0)
        return out.reshape(B, S, H)

    def _L1_attn_ref(hidden_states, in_proj_w, conv_w, conv_b, x_proj_w, dt_proj_w, dt_proj_b, A_log, D, out_proj_w):
        import jax, jax.numpy as jnp
        import numpy as np
        B_, L_, D_MODEL = (2, 256, 128)
        D_INNER, D_STATE, D_CONV, DT_RANK = (256, 16, 4, 64)

        def _mamba(hidden_states, in_proj_w, conv_w, conv_b, x_proj_w, dt_proj_w, dt_proj_b, A_log, D, out_proj_w):
            B, L, _ = hidden_states.shape
            xz = jnp.einsum('bld,ed->bel', hidden_states, in_proj_w)
            x, z = jnp.split(xz, 2, axis=1)
            xp = jnp.pad(x, ((0, 0), (0, 0), (D_CONV - 1, 0)))
            xc = jax.lax.conv_general_dilated(xp, conv_w, (1,), 'VALID', dimension_numbers=('NCH', 'OIH', 'NCH'), feature_group_count=D_INNER)
            x = jax.nn.silu(xc + conv_b[None, :, None])
            x_dbl = jnp.einsum('bdl,kd->bkl', x, x_proj_w)
            dt_in = x_dbl[:, :DT_RANK]
            Bm = x_dbl[:, DT_RANK:DT_RANK + D_STATE]
            Cm = x_dbl[:, DT_RANK + D_STATE:]
            delta = jnp.einsum('brl,dr->bdl', dt_in, dt_proj_w)
            delta = jax.nn.softplus(delta + dt_proj_b[None, :, None])
            A = -jnp.exp(A_log)
            dA = jnp.exp(jnp.einsum('bdl,dn->lbdn', delta, A))
            dBu = jnp.einsum('bdl,bnl,bdl->lbdn', delta, Bm, x)
            C_t = jnp.transpose(Cm, (2, 0, 1))

            def step(h, inp):
                dA_t, dBu_t, c_t = inp
                h = dA_t * h + dBu_t
                y = jnp.einsum('bdn,bn->bd', h, c_t)
                return (h, y)
            h0 = jnp.zeros((B, D_INNER, D_STATE), delta.dtype)
            _, ys = jax.lax.scan(step, h0, (dA, dBu, C_t))
            y = jnp.transpose(ys, (1, 2, 0))
            y = y + x * D[None, :, None]
            y = y * jax.nn.silu(z)
            return jnp.einsum('bdl,od->blo', y, out_proj_w)
        return _mamba(hidden_states, in_proj_w, conv_w, conv_b, x_proj_w, dt_proj_w, dt_proj_b, A_log, D, out_proj_w)

    def _L1_xattn_ref(values, keys, queries, mask, Wv, Wk, Wq, Wo, bo):
        import jax, jax.numpy as jnp
        import numpy as np
        N, S, E, H = (4, 256, 128, 16)
        D = E // H
        SCALE = E ** 0.5
        n = queries.shape[0]
        v = values.reshape(n, -1, H, D)
        k = keys.reshape(n, -1, H, D)
        q = queries.reshape(n, -1, H, D)
        v = jnp.einsum('nshd,od->nsho', v, Wv)
        k = jnp.einsum('nshd,od->nsho', k, Wk)
        q = jnp.einsum('nshd,od->nsho', q, Wq)
        energy = jnp.einsum('nqhd,nkhd->nhqk', q, k)
        energy = jnp.where(mask == 0, jnp.float32(-1e+20), energy)
        attn = jax.nn.softmax(energy / SCALE, axis=3)
        out = jnp.einsum('nhqk,nkhd->nqhd', attn, v).reshape(n, -1, H * D)
        return out @ Wo.T + bo

    def _L1_ffn_ref(x, gate_w, w1, b1, w2, b2, w3, b3, sw1, sw2, sw3):
        import jax, jax.numpy as jnp
        import numpy as np
        D = 128
        H = 128
        E = 8
        K = 2
        I = 2 * 128
        ROUTE_SCALE = 1.0
        B, S, _ = x.shape
        xt = x.reshape(-1, D)
        logits = xt @ gate_w.T
        scores = jax.nn.softmax(logits.astype(jnp.float32), axis=-1)
        top_vals, idx = jax.lax.top_k(scores, K)
        weights = jnp.take_along_axis(scores, idx, axis=1).astype(x.dtype) * ROUTE_SCALE
        xs = xt[:, None, :] * weights[:, :, None]
        y = jnp.zeros_like(xt)
        for e in range(E):
            mask = (idx == e).astype(x.dtype)
            h = jax.nn.silu(jnp.einsum('tkd,hd->tkh', xs, w1[e]) + b1[e])
            x2 = jnp.einsum('tkh,dh->tkd', h, w2[e]) + b2[e]
            x3 = jnp.einsum('tkd,hd->tkh', xs, w3[e]) + b3[e]
            y = y + jnp.sum(x2 * x3 * mask[:, :, None], axis=1)
        z = jax.nn.silu(xt @ sw1.T) * (xt @ sw2.T) @ sw3.T
        return (y + z).reshape(B, S, D)
    x = _layernorm(x + _L0_attn_ref(x, L0_attn_w_q, L0_attn_w_k, L0_attn_w_v, L0_attn_w_o), axis=-1)
    x = _layernorm(x + _L0_xattn_ref(x, ctx_1024, ctx_1024, L0_xattn_Wq, L0_xattn_bq, L0_xattn_Wk, L0_xattn_bk, L0_xattn_Wv, L0_xattn_bv, L0_xattn_Wo, L0_xattn_bo, L0_xattn_w1, L0_xattn_b1, L0_xattn_w2, L0_xattn_b2, L0_xattn_w3, L0_xattn_b3), axis=-1)
    x = _layernorm(x + _L0_ffn_ref(x, L0_ffn_router_w, L0_ffn_expert_weights), axis=-1)
    x = _layernorm(x + _L1_attn_ref(x, L1_attn_in_proj_w, L1_attn_conv_w, L1_attn_conv_b, L1_attn_x_proj_w, L1_attn_dt_proj_w, L1_attn_dt_proj_b, L1_attn_A_log, L1_attn_D, L1_attn_out_proj_w), axis=-1)
    x = _layernorm(x + _L1_xattn_ref(ctx_1024, ctx_1024, x, mask_Bx1x1xS2_if1, L1_xattn_Wv, L1_xattn_Wk, L1_xattn_Wq, L1_xattn_Wo, L1_xattn_bo), axis=-1)
    x = _layernorm(x + _L1_ffn_ref(x, L1_ffn_gate_w, L1_ffn_w1, L1_ffn_b1, L1_ffn_w2, L1_ffn_b2, L1_ffn_w3, L1_ffn_b3, L1_ffn_sw1, L1_ffn_sw2, L1_ffn_sw3), axis=-1)
    return x

_drawn_inputs = setup_inputs


def setup_inputs(seed=0):
    import zlib

    import numpy as np

    out = dict(_drawn_inputs(seed))
    spreads = {'L1_attn_conv_b': (0.0, 0.1), 'L1_attn_D': (1.0, 0.2), 'L1_xattn_bo': (0.0, 0.1)}
    factors = {'L0_attn_w_q': 8.0,
     'L0_attn_w_k': 7.878,
     'L0_xattn_Wq': 8.0,
     'L0_xattn_bq': 8.0,
     'L0_xattn_Wk': 8.0,
     'L0_xattn_bk': 64.0,
     'L0_xattn_bv': 5.181,
     'L0_xattn_w1': 8.0,
     'L0_xattn_b1': 8.0,
     'L0_xattn_w2': 8.0,
     'L0_xattn_b2': 8.0,
     'L0_xattn_w3': 8.0,
     'L1_attn_dt_proj_w': 4.0,
     'L1_attn_A_log': 2.777,
     'L1_ffn_b1': 28.663,
     'L1_ffn_b2': 8.0,
     'L1_ffn_b3': 24.819}
    for name, (base, spread) in spreads.items():
        noise = np.random.default_rng([zlib.crc32(name.encode()), seed]).standard_normal(out[name].shape)
        drawn = base * np.exp(spread * noise) if base else spread * noise
        out[name] = jnp.asarray(drawn.astype(out[name].dtype))
    for name, factor in factors.items():
        out[name] = (out[name] * factor).astype(out[name].dtype)
    return out
```

```python
from contextlib import ExitStack

import concourse.bass as bass
from concourse import mybir

F32 = mybir.dt.float32
BF16 = mybir.dt.bfloat16
I32 = mybir.dt.int32
ALU = mybir.AluOpType
ACT = mybir.ActivationFunctionType
X = mybir.AxisListType.X

P = 128
B = 32
G = 4
NG = B // G
W = G * P
SC = 77
EPS = 1e-5

AH, AD = 16, 64
XH, XD = 16, 8
E = 8
DI, NS, DR, KC = 256, 16, 64, 4
LOG_T_MIN, LOG_T_MAX = -2.302585092994046, 2.302585092994046


def stage_memory(nc, memory):
    return lambda name, shape, dtype=F32: memory.enter_context(nc.sbuf_tensor(name, shape, dtype))


class Core:
    pass


def ones_credit(engine, pairs):
    for semaphore, count in pairs:
        engine.sem_inc(semaphore, count)



def tail_dve(c, dve, n):
    dve.wait_ge(c.xs_loaded, (n + 1) * 16)
    dve.tensor_tensor(c.resid[:, :, :], c.y_bank[:, :].rearrange("p (j d) -> p j d", j=G), c.xs[:, :, :],
                      ALU.add).then_inc(c.resid_done, 1)
    dve.drain()
    for j in range(G):
        dve.bn_stats(c.bn[:, j, :], c.resid[:, j, :])
    dve.drain()
    for j in range(G):
        dve.bn_aggr(c.meanvar[:, j, :], c.bn[:, j, :])
    dve.drain()
    dve.tensor_scalar(c.var_eps[:, :], c.meanvar[:, :, 1], EPS, None, ALU.add).then_inc(c.var_done, 1)
    dve.wait_ge(c.rstd_done, n + 1)
    dve.wait_ge(c.y_stored, (n + 1) * 16)
    if not c.last:
        dve.wait_ge(c.y_transposed, n + 1)
    for j in range(G):
        last = dve.tensor_scalar(c.ys[:, j, :], c.resid[:, j, :], c.meanvar[:, j, 0:1], c.rstd[:, j:j + 1],
                                 ALU.subtract, ALU.mult)
    last.then_inc(c.y_normed, 1)


def tail_pool(c, pool, n):
    pool.wait_ge(c.var_done, n + 1)
    pool.tensor_tensor(c.rstd[:, :], c.var_eps[:, :], c.w["minus_half"][:, :], ALU.pow).then_inc(c.rstd_done, 1)


def tail_pe(c, pe, n, bank):
    if c.last:
        return
    pe.wait_ge(c.y_normed, n + 1)
    for j in range(G):
        last = pe.transpose(bank[:, j * P:(j + 1) * P], c.ys[:, j, :], c.w["ident"][:, :])
    last.then_inc(c.y_transposed, 1)


def tail_act(c, act, n, bank):
    if c.last:
        return
    act.wait_ge(c.y_transposed, n + 2)
    act.wait_ge(c.yT_stored, (n + 1) * 16)
    act.activation(c.yTs[:, :], bank[:, :], ACT.Copy).then_inc(c.yT_copied, 1)


def load_x(c, sp, n, g, source, source_T, with_ctx):
    sp.wait_ge(c.xTs_used, n + 1)
    sp.dma_start(c.xTs[:, :], source_T[:, bass.ds(g * W, W)]).then_inc(c.xTs_loaded, 16)
    if with_ctx:
        sp.dma_start(c.ctxTs[:, :], c.dram["ctxT"][:, bass.ds(g * (G * SC), G * SC)]).then_inc(c.ctx_loaded, 16)
    sp.wait_ge(c.resid_done, n + 1)
    sp.dma_start(c.xs[:, :, :], source[:, bass.ds(g * G, G), :]).then_inc(c.xs_loaded, 16)


def store_x(c, sp, n, g, target, target_T):
    sp.wait_ge(c.y_normed, n + 1)
    sp.dma_start(target[:, bass.ds(g * G, G), :], c.ys[:, :, :]).then_inc(c.y_stored, 16)
    if target_T is not None:
        sp.wait_ge(c.yT_copied, n + 2)
        sp.dma_start(target_T[:, bass.ds(g * W, W)], c.yTs[:, :]).then_inc(c.yT_stored, 16)


def sp_stage(c, sp, stage, with_ctx=False):
    n0 = c.n0
    source, source_T = (c.x_dram, c.xT_dram) if c.n0 == 0 else (c.x_all, c.xT_all)
    target, target_T = (c.out_dram, None) if c.last else (c.x_all, c.xT_all)
    load_x(c, sp, n0, 0, source, source_T, with_ctx)
    with sp.Fori(0, NG - 1) as g:
        load_x(c, sp, g + n0 + 1, g + 1, source, source_T, with_ctx)
        store_x(c, sp, g + n0, g, target, target_T)
    store_x(c, sp, n0 + NG - 1, NG - 1, target, target_T)
    sp.wait_ge(c.y_stored, (n0 + NG) * 16 + 16)
    if target_T is not None:
        sp.wait_ge(c.yT_stored, (n0 + NG) * 16 + 16)



def causal_attention(c, nc, stage):
    n0 = c.n0
    NQ = AH // 4
    CH = 6
    sem, bank = c.sem, c.bank
    memory = ExitStack()
    sb = stage_memory(nc, memory)

    qT = sb("qT", [P, 2, 8, P])
    kT = sb("kT", [P, 2, 8, P])
    v = sb("v", [P, 2, AH, AD])
    probs = sb("probs", [P, 4, 4, P])
    probsT = sb("probsT", [P, 2, 4, P])
    row_max = sb("row_max", [P, 2, 4])
    row_sum, row_inv = sb("row_sum", [P, 2, 4]), sb("row_inv", [P, 2, 4])
    heads_outT = sb("heads_outT", [P, 2, 4, P])

    proj_bank = [bank(0), bank(1)]
    score_bank = [bank(2), bank(3)]
    probsT_bank, outT_bank = bank(4), [bank(5), bank(6)]

    proj_done, proj_copied = sem("a_proj_done"), sem("a_proj_copied")
    scores_done, scores_shifted = sem("a_scores_done"), sem("a_scores_shifted")
    probs_done, transposed = sem("a_probs_done"), sem("a_transposed")
    probsT_copied, pv_done = sem("a_probsT_copied"), sem("a_pv_done")
    normed, outT_copied = sem("a_normed"), sem("a_outT_copied")
    outT_used = sem("a_outT_used")

    def quad_heads(q):
        return [8 * (q // 2) + q % 2 + 2 * m for m in range(4)]

    with nc.Block() as block:
        @block.sync
        def _(sp):
            sp_stage(c, sp, stage)

        @block.gpsimd
        def _(pool):
            with pool.Fori(0, NG) as g:
                tail_pool(c, pool, g + n0)

        @block.tensor
        def _(pe):
            def project(g, j, chunks):
                for ch in chunks:
                    t = g * (G * CH) + (j * CH + ch)
                    out = proj_bank[ch % 2]
                    if ch == 0 and j == 0:
                        pe.wait_ge(c.xTs_loaded, (g + n0 + 1) * 16)
                    pe.wait_ge(proj_copied, t + 1)
                    xj = c.xTs[:, j * P:(j + 1) * P]
                    if ch < 4:
                        w = (c.w["a_wq"], c.w["a_wk"])[ch // 2]
                        for m in range(4):
                            hp = 4 * (ch % 2) + m
                            last = pe.matmul(out[:, m * P:(m + 1) * P], w[:, hp * P:(hp + 1) * P], xj,
                                             start=True, stop=True)
                    else:
                        last = pe.matmul(out[:, :], xj, c.w["a_wv"][:, (ch - 4) * 512:(ch - 3) * 512],
                                         start=True, stop=True)
                    last.then_inc(proj_done, 1)

            def scores(g, q):
                j, r = q // NQ, (q // NQ) % 2
                if q % NQ == 0:
                    pe.wait_ge(proj_copied, g * (G * CH) + (j * CH + 4 + 2))
                pe.wait_ge(scores_shifted, g * (G * NQ) + (q + 1))
                out = score_bank[q % 2]
                mask = pe.matmul(out[:, :], c.ident16[:, :], c.causal16[:, :], start=True, stop=False)
                if q == (G - 2) * NQ + 3:
                    mask.then_inc(c.xTs_used, 1)
                for m, h in enumerate(quad_heads(q % NQ)):
                    rows = slice(64 * (h % 2), 64 * (h % 2) + 64)
                    last = pe.matmul(out[:, m * P:(m + 1) * P], qT[rows, r, h // 2, :], kT[rows, r, h // 2, :],
                                     start=False, stop=(m == 3))
                last.then_inc(scores_done, 1)

            def transpose_probs(g, q):
                pe.wait_ge(normed, g * (G * NQ) + (q + 1))
                pe.wait_ge(probsT_copied, g * (G * NQ) + (q + 1))
                for m in range(4):
                    last = pe.transpose(probsT_bank[:, m * P:(m + 1) * P], probs[:, q % 4, m, :],
                                        c.w["ident"][:, :])
                last.then_inc(transposed, 1)

            def times_v(g, q):
                j, half = q // NQ, q // 2
                pe.wait_ge(probsT_copied, g * (G * NQ) + (q + 2))
                if q % NQ == 0:
                    pe.wait_ge(proj_copied, g * (G * CH) + (j * CH + CH + 2))
                if q % 2 == 0:
                    pe.wait_ge(outT_copied, g * (G * 2) + (half + 1))
                if q == 0 and not c.last:
                    pe.wait_ge(c.yT_copied, g + n0 + 1)
                for m, h in enumerate(quad_heads(q % NQ)):
                    rows = slice(64 * (h % 2), 64 * (h % 2) + 64)
                    last = pe.matmul(outT_bank[half % 2][rows, m * P:(m + 1) * P], v[:, j % 2, h, :],
                                     probsT[:, q % 2, m, :], start=True, stop=True)
                last.then_inc(pv_done, 1)

            def project_out(g, half):
                j = half // 2
                pe.wait_ge(outT_copied, g * (G * 2) + (half + 3))
                if half == 0:
                    pe.wait_ge(c.resid_done, g + n0 + 1)
                for m in range(4):
                    hp = 4 * (half % 2) + m
                    last = pe.matmul(c.y_bank[:, j * P:(j + 1) * P], heads_outT[:, half % 2, m, :],
                                     c.w["a_wo"][:, hp, :], start=(hp == 0), stop=(hp == 7))
                last.then_inc(outT_used, 1)

            with pe.Fori(0, NG) as g:
                project(g, 0, range(CH))
                for s in range(G * NQ + 5):
                    if s < G * NQ:
                        scores(g, s)
                    if 2 <= s < G * NQ + 2:
                        transpose_probs(g, s - 2)
                    if s % NQ < 3 and s // NQ + 1 < G:
                        project(g, s // NQ + 1, range(2 * (s % NQ), 2 * (s % NQ) + 2))
                    if 3 <= s < G * NQ + 3:
                        times_v(g, s - 3)
                    if s >= 6 and s % 2 == 0:
                        project_out(g, (s - 6) // 2)
                tail_pe(c, pe, g + n0, outT_bank[0])

        @block.scalar
        def _(act):
            def copy_projection(g, j, chunks):
                for ch in chunks:
                    t = g * (G * CH) + (j * CH + ch)
                    r = j % 2
                    act.wait_ge(proj_done, t + 1)
                    if ch == 0:
                        act.wait_ge(scores_done, g * (G * NQ) + ((j - 2) * NQ + NQ + 8))
                    if ch == 4:
                        act.wait_ge(pv_done, g * (G * NQ) + ((j - 2) * NQ + NQ + 8))
                    src = proj_bank[ch % 2]
                    if ch < 4:
                        dst = (qT, kT)[ch // 2][:, r, 4 * (ch % 2):4 * (ch % 2) + 4, :]
                        act.activation(dst, src[:, :].rearrange("p (m t) -> p m t", m=4), ACT.Copy)\
                            .then_inc(proj_copied, 1)
                    else:
                        dst = v[:, r, 8 * (ch - 4):8 * (ch - 3), :]
                        act.activation(dst, src[:, :].rearrange("p (h d) -> p h d", h=8), ACT.Copy)\
                            .then_inc(proj_copied, 1)

            def exp(g, q):
                act.wait_ge(scores_shifted, g * (G * NQ) + (q + 1 + 2))
                act.activation(probs[:, q % 4, :, :], probs[:, q % 4, :, :], ACT.Exp, scale=float(AD) ** -0.5)\
                    .then_inc(probs_done, 1)

            def copy_probsT(g, q):
                act.wait_ge(transposed, g * (G * NQ) + (q + 1 + 4))
                act.wait_ge(pv_done, g * (G * NQ) + (q - 1 + 8))
                act.activation(probsT[:, q % 2, :, :], probsT_bank[:, :].rearrange("p (m t) -> p m t", m=4),
                               ACT.Copy).then_inc(probsT_copied, 1)

            def copy_outT(g, half):
                act.wait_ge(pv_done, g * (G * NQ) + (2 * half + 2 + 8))
                act.wait_ge(outT_used, g * (G * 2) + (half + 1))
                act.activation(heads_outT[:, half % 2, :, :], outT_bank[half % 2][:, :].rearrange("p (m t) -> p m t", m=4),
                               ACT.Copy).then_inc(outT_copied, 1)

            ones_credit(act, [(proj_copied, 2), (probsT_copied, 1), (outT_copied, 2)])
            with act.Fori(0, NG) as g:
                copy_projection(g, 0, range(CH))
                for s in range(G * NQ + 5):
                    if s < G * NQ:
                        exp(g, s)
                    if 2 <= s < G * NQ + 2:
                        copy_probsT(g, s - 2)
                    if s % NQ < 3 and s // NQ + 1 < G:
                        copy_projection(g, s // NQ + 1, range(2 * (s % NQ), 2 * (s % NQ) + 2))
                    if s >= 5 and s % 2 == 1:
                        copy_outT(g, (s - 5) // 2)
                tail_act(c, act, g + n0, outT_bank[0])

        @block.vector
        def _(dve):
            def shift(g, q):
                s = g * (G * NQ) + q
                dve.wait_ge(scores_done, s + (1 + 8))
                dve.wait_ge(transposed, s + 1)
                src = score_bank[q % 2][:, :].rearrange("p (m t) -> p m t", m=4)
                dve.tensor_reduce(row_max[:, q % 2, :], src, X, ALU.max)
                dve.drain()
                dve.tensor_tensor(probs[:, q % 4, :, :], src,
                                  row_max[:, q % 2, :].unsqueeze(2).broadcast_to([P, 4, P]),
                                  ALU.subtract).then_inc(scores_shifted, 1)

            def normalise(g, q):
                dve.wait_ge(probs_done, g * (G * NQ) + (q + 1))
                dve.tensor_reduce(row_sum[:, q % 2, :], probs[:, q % 4, :, :], X, ALU.add)
                dve.drain()
                dve.reciprocal(row_inv[:, q % 2, :], row_sum[:, q % 2, :])
                dve.drain()
                dve.tensor_tensor(probs[:, q % 4, :, :], probs[:, q % 4, :, :],
                                  row_inv[:, q % 2, :].unsqueeze(2).broadcast_to([P, 4, P]),
                                  ALU.mult).then_inc(normed, 1)

            ones_credit(dve, [(scores_shifted, 2), (transposed, 4), (scores_done, 8), (pv_done, 8), (outT_used, 2)])
            with dve.Fori(0, NG) as g:
                for s in range(G * NQ + 1):
                    if s < G * NQ:
                        shift(g, s)
                    if s >= 1:
                        normalise(g, s - 1)
                dve.wait_ge(outT_used, g * (2 * G) + (2 * G + 2))
                tail_dve(c, dve, g + n0)
    memory.close()



def cross_attention(c, nc, stage):
    n0 = c.n0
    tempered = stage == 1
    w = {k[3:]: v for k, v in c.w.items() if k.startswith("x0_" if tempered else "x1_")}
    NC = 4
    HC = XH // NC
    T = G * NC
    sem, bank = c.sem, c.bank
    memory = ExitStack()
    sb = stage_memory(nc, memory)
    pre = f"s{stage}_"

    keys = sb(pre + "keys", [P, G, XH, SC])
    v_spread = sb(pre + "v_spread", [P, G, XH * P])
    shifted = sb(pre + "shifted", [P, G, XH, SC])
    row_max = sb(pre + "row_max", [P, G, XH])
    row_sum, row_inv = sb(pre + "row_sum", [P, G, XH]), sb(pre + "row_inv", [P, G, XH])
    probsT = sb(pre + "probsT", [P, 2, HC, P])
    heads_outT = sb(pre + "heads_outT", [P, 2, P])
    score_banks = c.psum[:, 0:4, 0:HC * SC].rearrange("p q (m t) -> p q m t", m=HC)
    chunk_bank = [bank(4), bank(5)]
    q_bank, k_bank, misc = bank(4), bank(5), bank(6)
    v_diagonal = v_spread[:, :, :].rearrange("p j (h d) -> p j h d", h=XH)

    k_done, keys_done = sem(pre + "k_done"), sem(pre + "keys_done")
    v_done, v_copied = sem(pre + "v_done"), sem(pre + "v_copied")
    scores_done, shift_done = sem(pre + "scores_done"), sem(pre + "shift_done")
    probs_done, transposed, copied = sem(pre + "probs_done"), sem(pre + "transposed"), sem(pre + "copied")
    pv_done, normed, sum_inverted = sem(pre + "pv_done"), sem(pre + "normed"), sem(pre + "sum_inverted")
    outT_copied, out_done = sem(pre + "outT_copied"), sem(pre + "out_done")
    zeros_set, mask_ready = sem(pre + "zeros_set"), sem(pre + "mask_ready")
    if tempered:
        SCALE = XD ** -0.5
        qT = sb(pre + "qT", [P, W])
        exp1 = sb(pre + "exp1", [P, 2, 2, XH, SC])
        sum1, sum2 = sb(pre + "sum1", [P, G, XH]), sb(pre + "sum2", [P, G, XH])
        inv1 = sb(pre + "inv1", [P, G, XH])
        ksum, qsum, bk77 = sb(pre + "ksum", [P, G]), sb(pre + "qsum", [P, G]), sb(pre + "bk77", [P, 1])
        qk_sum = sb(pre + "qk_sum", [P, G])
        qk_heads = sb(pre + "qk_heads", [P, G, XH])
        feats = sb(pre + "feats", [3, G * XH])
        hidden1, hidden2 = sb(pre + "hidden1", [64, G * XH]), sb(pre + "hidden2", [64, G * XH])
        log_t = sb(pre + "log_t", [P, G * XH])
        inv_t = sb(pre + "inv_t", [P, G, XH])
        q_done, q_copied = sem(pre + "q_done"), sem(pre + "q_copied")
        exp1_done, sums_done = sem(pre + "exp1_done"), sem(pre + "sums_done")
        feats_ready, clipped = sem(pre + "feats_ready"), sem(pre + "clipped")
        mlp_pe, mlp_act, scaled = sem(pre + "mlp_pe"), sem(pre + "mlp_act"), sem(pre + "scaled")
        queries = qT
    else:
        SCALE = float(P) ** -0.5
        mask_int = sb(pre + "mask_int", [P, B * SC], I32)
        key_bias = sb(pre + "key_bias", [P, B, SC], BF16)
        w_qk = sb(pre + "w_qk", [P, P])
        mask_loaded, w_qk_done, w_qk_copied = sem(pre + "mask_loaded"), sem(pre + "w_qk_done"), sem(pre + "w_qk_copied")
        queries = c.xTs

    with nc.Block() as block:
        @block.sync
        def _(sp):
            if not tempered:
                sp.dma_start(mask_int[:, :], c.dram["mask"]).then_inc(mask_loaded, 16)
            sp_stage(c, sp, stage, with_ctx=True)

        @block.gpsimd
        def _(pool):
            pool.memset(v_spread[:, :, :], 0.0)
            pool.memset(probsT[:, :, :, :], 0.0).then_inc(zeros_set, 1)
            with pool.Fori(0, NG) as g:
                if tempered:
                    for j in range(G):
                        if j == 0:
                            pool.wait_ge(mlp_act, g * 4 + 4)
                        pool.tensor_tensor(shifted[:, j, :, :], shifted[:, j, :, :],
                                           inv_t[:, j, :].unsqueeze(2).broadcast_to([P, XH, SC]),
                                           ALU.mult).then_inc(scaled, 1)
                else:
                    for j in range(G):
                        pool.wait_ge(sum_inverted, g * G + (j + 1))
                        pool.tensor_tensor(shifted[:, j, :, :], shifted[:, j, :, :],
                                           row_inv[:, j, :].unsqueeze(2).broadcast_to([P, XH, SC]),
                                           ALU.mult).then_inc(normed, 1)
                tail_pool(c, pool, g + n0)

        @block.tensor
        def _(pe):
            def project(g):
                pe.wait_ge(c.xTs_loaded, (g + n0 + 1) * 16)
                pe.wait_ge(c.ctx_loaded, (g + c.ctx0 + 1) * 16)
                pe.wait_ge(copied, g * T + 2)
                if tempered:
                    pe.matmul(q_bank[:, :], w["wq"][:, :], c.xTs[:, :], start=True, stop=True).then_inc(q_done, 1)
                pe.matmul(k_bank[:, 0:G * SC], w["wk"][:, :] if tempered else w_qk[:, :], c.ctxTs[:, :],
                          start=True, stop=True).then_inc(k_done, 1)
                if not c.last:
                    pe.wait_ge(c.yT_copied, g + n0 + 1)
                for j in range(G):
                    last = pe.matmul(misc[0:SC, j * P:(j + 1) * P], c.ctxTs[:, j * SC:(j + 1) * SC],
                                     w["wv"][:, :], start=True, stop=True)
                last.then_inc(v_done, 1)

            def scores(g, j):
                if j == 0 and tempered:
                    pe.wait_ge(q_copied, g + 1)
                pe.wait_ge(keys_done, g * G + (j + 1))
                pe.wait_ge(shift_done, g * G + (j + 1))
                for q in range(4):
                    out = score_banks[:, q, :, :]
                    if not tempered:
                        bias = key_bias[:, bass.ds(g * G + j, 1), :].broadcast_to([P, HC, SC])
                        pe.matmul(out, c.ident16[:, :], bias, start=True, stop=False)
                    last = pe.matmul(out, queries[:, j * P:(j + 1) * P], keys[:, j, HC * q:HC * (q + 1), :],
                                     start=tempered, stop=True)
                    if tempered and j == 0 and q == 0:
                        last.then_inc(c.xTs_used, 1)
                last.then_inc(scores_done, 1)

            def temperature_mlp(g):
                pe.wait_ge(feats_ready, g + 1)
                for f, stat in enumerate((qk_heads, row_max, sum2)):
                    last = pe.matmul(misc[0:3, 0:G * XH], w["select"][:, f, :],
                                     stat[:, :, :].rearrange("p j h -> p (j h)"), start=(f == 0), stop=(f == 2))
                last.then_inc(mlp_pe, 1)
                pe.wait_ge(mlp_act, g * 4 + 1)
                pe.matmul(misc[0:64, 64:128], w["w1"][:, :], feats[:, :], start=True, stop=True).then_inc(mlp_pe, 1)
                pe.wait_ge(mlp_act, g * 4 + 2)
                pe.matmul(misc[:, 128:192], w["w2"][:, :], hidden1[:, :], start=True, stop=True)\
                    .then_inc(mlp_pe, 1)
                pe.wait_ge(mlp_act, g * 4 + 3)
                pe.matmul(misc[:, 192:256], w["w3"][:, :], hidden2[:, :], start=True, stop=True).then_inc(mlp_pe, 1)

            def transpose_chunk(g, u):
                j, k = u // NC, u % NC
                if k == 0:
                    pe.wait_ge(normed, g * G + (j + 1))
                pe.wait_ge(copied, g * T + (u + 1))
                for m in range(HC):
                    last = pe.transpose(chunk_bank[u % 2][0:SC, m * P:(m + 1) * P], shifted[:, j, k * HC + m, :],
                                        c.w["ident"][:, :])
                    if not tempered and u == 2 * NC and m == 0:
                        last.then_inc(c.xTs_used, 1)
                last.then_inc(transposed, 1)

            def times_v(g, u):
                j, k = u // NC, u % NC
                if u == 0:
                    pe.wait_ge(v_copied, g + 1)
                if k == 0:
                    pe.wait_ge(outT_copied, g * G + (j + 1))
                pe.wait_ge(copied, g * T + (u + 3))
                for m in range(HC):
                    h = k * HC + m
                    last = pe.matmul(misc[:, 0:P], v_diagonal[:, j, h, :], probsT[:, u % 2, m, :],
                                     start=(h == 0), stop=(h == XH - 1))
                last.then_inc(pv_done, 1)

            def project_out(g, j):
                pe.wait_ge(outT_copied, g * G + (j + 2))
                if j == 0:
                    pe.wait_ge(c.resid_done, g + n0 + 1)
                y = c.y_bank[:, j * P:(j + 1) * P]
                pe.matmul(y, heads_outT[:, j % 2, :], w["wo"][:, :], start=True, stop=False)
                pe.matmul(y, c.w["ones_row"][:, :], w["bo"][:, :], start=False, stop=True).then_inc(out_done, 1)

            pe.wait_ge(zeros_set, 1)
            if not tempered:
                pe.matmul(misc[:, 0:P], w["wk"][:, :], w["wq"][:, :], start=True, stop=True).then_inc(w_qk_done, 1)
                pe.wait_ge(w_qk_copied, 1)
                pe.wait_ge(mask_ready, 1)
            with pe.Fori(0, NG) as g:
                project(g)
                if tempered:
                    for j in range(G):
                        scores(g, j)
                    temperature_mlp(g)
                else:
                    scores(g, 0)
                for s in range(T + 3):
                    if not tempered and s % NC == 0 and s // NC + 1 < G:
                        scores(g, s // NC + 1)
                    if s < T:
                        transpose_chunk(g, s)
                    if 1 <= s <= T:
                        times_v(g, s - 1)
                    if s >= 6 and (s - 6) % NC == 0:
                        project_out(g, (s - 6) // NC)
                tail_pe(c, pe, g + n0, misc)

        @block.scalar
        def _(act):
            def first_exp(g, j):
                act.wait_ge(shift_done, g * G + (j + 2))
                act.wait_ge(sums_done, g * G + (j + 1))
                for power in (1, 2):
                    act.activation(exp1[:, j % 2, power - 1, :, :], shifted[:, j, :, :], ACT.Exp,
                                   scale=power * SCALE).then_inc(exp1_done, 1)

            def temperature_mlp(g):
                act.wait_ge(mlp_pe, g * 4 + 1)
                act.activation(feats[:, :], misc[0:3, 0:64], ACT.Identity, bias=w["feat_bias"][:, 0:1])\
                    .then_inc(mlp_act, 1)
                act.wait_ge(mlp_pe, g * 4 + 2)
                act.activation(hidden1[:, :], misc[0:64, 64:128], ACT.Gelu, bias=w["b1"][:, 0:1])\
                    .then_inc(mlp_act, 1)
                act.wait_ge(mlp_pe, g * 4 + 3)
                act.activation(hidden2[:, :], misc[0:64, 128:192], ACT.Gelu, bias=w["b2"][:, 0:1])\
                    .then_inc(mlp_act, 1)
                act.wait_ge(clipped, g + 1)
                act.activation(inv_t[:, :, :].rearrange("p j h -> p (j h)"), log_t[:, :], ACT.Exp, scale=-1.0)\
                    .then_inc(mlp_act, 1)

            def exp(g, j):
                if tempered:
                    act.wait_ge(scaled, g * G + (j + 1))
                else:
                    act.wait_ge(shift_done, g * G + (j + 2))
                act.activation(shifted[:, j, :, :], shifted[:, j, :, :], ACT.Exp,
                               scale=0.5 if tempered else SCALE).then_inc(probs_done, 1)

            def copy_chunk(g, u):
                act.wait_ge(transposed, g * T + (u + 1 + T))
                act.wait_ge(pv_done, g * T + (u + 3))
                act.activation(probsT[0:SC, u % 2, :, :],
                               chunk_bank[u % 2][0:SC, :].rearrange("p (m t) -> p m t", m=HC), ACT.Copy)\
                    .then_inc(copied, 1)

            def copy_outT(g, j):
                act.wait_ge(pv_done, (g * G + j) * NC + (NC + 4))
                act.wait_ge(out_done, g * G + (j + 1))
                act.activation(heads_outT[:, j % 2, :], misc[:, 0:P], ACT.Copy).then_inc(outT_copied, 1)

            ones_credit(act, [(copied, 2), (outT_copied, 1)])
            act.wait_ge(zeros_set, 1)
            if not tempered:
                act.wait_ge(w_qk_done, 1)
                act.activation(w_qk[:, :], misc[:, 0:P], ACT.Copy).then_inc(w_qk_copied, 1)
            with act.Fori(0, NG) as g:
                if tempered:
                    act.wait_ge(q_done, g + 1)
                    act.wait_ge(scores_done, g * G + 4)
                    act.activation(qT[:, :], q_bank[:, :], ACT.Identity, bias=w["bq"][:, 0:1]).then_inc(q_copied, 1)
                    for j in range(G):
                        first_exp(g, j)
                    temperature_mlp(g)
                exp(g, 0)
                for s in range(T + 3):
                    if s < T:
                        copy_chunk(g, s)
                    if s % NC == NC - 1 and s // NC + 1 < G:
                        exp(g, s // NC + 1)
                    if s >= 5 and (s - 5) % NC == 0:
                        copy_outT(g, (s - 5) // NC)
                tail_act(c, act, g + n0, misc)

        @block.vector
        def _(dve):
            def own_columns(j):
                blocks = v_spread[0:SC, j, :]
                return bass.AP(blocks.tensor, blocks.offset, [blocks.ap[0], [P + XD, XH], [1, XD]])

            def spread(g):
                dve.wait_ge(k_done, g + 1)
                dve.wait_ge(scores_done, g * G + 4)
                if tempered:
                    dve.tensor_reduce(ksum[:, :], k_bank[:, 0:G * SC].rearrange("p (j t) -> p j t", j=G), X, ALU.add)
                for j in range(G):
                    dve.scalar_tensor_tensor(
                        keys[:, j, :, :], k_bank[:, j * SC:(j + 1) * SC].unsqueeze(1).broadcast_to([P, XH, SC]),
                        w["bk"][:, 0:1] if tempered else 0.0,
                        c.w["head_of"][:, :].unsqueeze(2).broadcast_to([P, XH, SC]),
                        ALU.add, ALU.mult).then_inc(keys_done, 1)
                dve.wait_ge(v_done, g + 1)
                dve.wait_ge(pv_done, g * T + 4)
                for j in range(G):
                    src = misc[0:SC, j * P:(j + 1) * P].rearrange("p (h d) -> p h d", h=XH)
                    if tempered:
                        last = dve.tensor_tensor(own_columns(j), src,
                                                 w["bv"][:, :].rearrange("p (h d) -> p h d", h=XH), ALU.add)
                    else:
                        last = dve.tensor_copy(own_columns(j), src)
                last.then_inc(v_copied, 1)

            def shift(g, j):
                dve.wait_ge(scores_done, g * G + (j + 5))
                dve.wait_ge(transposed, (g * G + j) * NC + NC)
                dve.tensor_reduce(row_max[:, j, :].rearrange("p (q m) -> p q m", q=4), score_banks, X, ALU.max)
                dve.drain()
                dve.tensor_tensor(shifted[:, j, :, :].rearrange("p (q m) t -> p q m t", q=4), score_banks,
                                  row_max[:, j, :].rearrange("p (q m) -> p q m", q=4).unsqueeze(3)
                                  .broadcast_to([P, 4, HC, SC]), ALU.subtract).then_inc(shift_done, 1)

            def sums(g, j):
                dve.wait_ge(exp1_done, (g * G + j) * 2 + 2)
                dve.tensor_reduce(sum1[:, j, :], exp1[:, j % 2, 0, :, :], X, ALU.add)
                dve.tensor_reduce(sum2[:, j, :], exp1[:, j % 2, 1, :, :], X, ALU.add).then_inc(sums_done, 1)

            def statistics(g):
                dve.wait_ge(q_copied, g + 1)
                dve.tensor_reduce(qsum[:, :], qT[:, :].rearrange("p (j t) -> p j t", j=G), X, ALU.add)
                dve.drain()
                dve.reciprocal(inv1[:, :, :], sum1[:, :, :])
                dve.scalar_tensor_tensor(qk_sum[:, :], ksum[:, :], bk77[:, 0:1], qsum[:, :], ALU.add, ALU.mult)
                dve.drain()
                dve.tensor_tensor(sum2[:, :, :], sum2[:, :, :], inv1[:, :, :], ALU.mult)
                dve.tensor_tensor(qk_heads[:, :, :], qk_sum[:, :].unsqueeze(2).broadcast_to([P, G, XH]),
                                  c.w["head_of"][:, :].unsqueeze(1).broadcast_to([P, G, XH]), ALU.mult)
                dve.drain()
                dve.tensor_tensor(sum2[:, :, :], sum2[:, :, :], inv1[:, :, :], ALU.mult).then_inc(feats_ready, 1)

            def clip(g):
                dve.wait_ge(mlp_pe, g * 4 + 4)
                dve.tensor_scalar(log_t[:, :], misc[:, 192:256], w["b3"][:, 0:1], LOG_T_MIN, ALU.add, ALU.max)
                dve.drain()
                dve.tensor_scalar(log_t[:, :], log_t[:, :], LOG_T_MAX, None, ALU.min).then_inc(clipped, 1)

            def normalise(g, j):
                dve.wait_ge(probs_done, g * G + (j + 1))
                dve.tensor_reduce(row_sum[:, j, :], shifted[:, j, :, :], X, ALU.add)
                dve.drain()
                last = dve.reciprocal(row_inv[:, j, :], row_sum[:, j, :])
                if not tempered:
                    last.then_inc(sum_inverted, 1)
                    return
                dve.drain()
                dve.tensor_scalar(row_inv[:, j, :], row_inv[:, j, :], 0.0, None, ALU.max)
                dve.drain()
                dve.scalar_tensor_tensor(shifted[:, j, :, :], shifted[:, j, :, :], 0.0,
                                         row_inv[:, j, :].unsqueeze(2).broadcast_to([P, XH, SC]),
                                         ALU.max, ALU.mult).then_inc(normed, 1)

            ones_credit(dve, [(scores_done, 4), (shift_done, 1), (transposed, T), (pv_done, 4), (out_done, 2)])
            if tempered:
                ones_credit(dve, [(sums_done, 2)])
                dve.tensor_scalar(bk77[:, :], w["bk"][:, :], float(SC), None, ALU.mult)
            else:
                dve.wait_ge(mask_loaded, 16)
                dve.tensor_scalar(key_bias[:, :, :].rearrange("p b t -> p (b t)"), mask_int[:, :], 0, -1e20,
                                  ALU.is_equal, ALU.mult).then_inc(mask_ready, 1)
            dve.wait_ge(zeros_set, 1)
            with dve.Fori(0, NG) as g:
                spread(g)
                if tempered:
                    for j in range(G):
                        shift(g, j)
                        if j >= 1:
                            sums(g, j - 1)
                    sums(g, G - 1)
                    statistics(g)
                    clip(g)
                    for j in range(G):
                        normalise(g, j)
                else:
                    shift(g, 0)
                    for j in range(G):
                        if j + 1 < G:
                            shift(g, j + 1)
                        normalise(g, j)
                dve.wait_ge(out_done, g * G + (G + 2))
                tail_dve(c, dve, g + n0)
    memory.close()



class Router:

    def __init__(self, c, sb, sem, pre, weight):
        self.c, self.weight = c, weight
        self.shifted, self.probs = sb(pre + "r_shifted", [P, G, E]), sb(pre + "r_probs", [P, G, E])
        self.rank, self.chosen = sb(pre + "r_rank", [P, G, E]), sb(pre + "r_chosen", [P, G, E])
        self.w = sb(pre + "r_w", [P, G, E])
        self.best, self.total, self.inverse = (sb(pre + "r_" + x, [P, G]) for x in ("best", "total", "inverse"))
        self.above, self.equal = sb(pre + "r_above", [P, G, E, E]), sb(pre + "r_equal", [P, G, E, E])
        self.logits_done, self.shift_done = sem(pre + "logits_done"), sem(pre + "r_shift_done")
        self.exp_done, self.routed = sem(pre + "r_exp_done"), sem(pre + "routed")

    def pe(self, pe, g, bank):
        for j in range(G):
            last = pe.matmul(bank[:, j * E:(j + 1) * E], self.c.xTs[:, j * P:(j + 1) * P], self.weight[:, :],
                             start=True, stop=True)
        last.then_inc(self.logits_done, 1)

    def act(self, act, g):
        act.wait_ge(self.shift_done, g + 1)
        act.activation(self.probs[:, :, :], self.shifted[:, :, :], ACT.Exp).then_inc(self.exp_done, 1)

    def dve(self, dve, g, bank):
        dve.wait_ge(self.logits_done, g + 1)
        logits = bank[:, 0:G * E].rearrange("p (j e) -> p j e", j=G)
        wide = [P, G, E]
        dve.tensor_reduce(self.best[:, :], logits, X, ALU.max)
        dve.drain()
        dve.tensor_tensor(self.shifted[:, :, :], logits, self.best[:, :].unsqueeze(2).broadcast_to(wide),
                          ALU.subtract).then_inc(self.shift_done, 1)
        dve.wait_ge(self.exp_done, g + 1)
        dve.tensor_reduce(self.total[:, :], self.probs[:, :, :], X, ALU.add)
        dve.drain()
        dve.reciprocal(self.inverse[:, :], self.total[:, :])
        dve.drain()
        dve.tensor_tensor(self.probs[:, :, :], self.probs[:, :, :],
                          self.inverse[:, :].unsqueeze(2).broadcast_to(wide), ALU.mult)
        dve.drain()
        other = self.probs[:, :, :].unsqueeze(2).broadcast_to([P, G, E, E])
        own = self.probs[:, :, :].unsqueeze(3).broadcast_to([P, G, E, E])
        dve.tensor_tensor(self.above[:, :, :, :], other, own, ALU.is_gt)
        dve.tensor_tensor(self.equal[:, :, :, :], other, own, ALU.is_equal)
        dve.drain()
        dve.tensor_tensor(self.equal[:, :, :, :], self.equal[:, :, :, :],
                          self.c.w["earlier"][:, :, :].unsqueeze(1).broadcast_to([P, G, E, E]), ALU.mult)
        dve.drain()
        dve.tensor_tensor(self.above[:, :, :, :], self.above[:, :, :, :], self.equal[:, :, :, :], ALU.add)
        dve.drain()
        dve.tensor_reduce(self.rank[:, :, :], self.above[:, :, :, :], X, ALU.add)
        dve.drain()
        dve.tensor_scalar(self.chosen[:, :, :], self.rank[:, :, :], 1.5, None, ALU.is_lt)
        dve.drain()


def broadcast_weight(c, pe, out, router, e):
    for j in range(G):
        last = pe.matmul(out[:, j * P:(j + 1) * P], router.w[:, j, e:e + 1].broadcast_to([P, P]),
                         c.w["ident"][:, :], start=True, stop=True)
    return last



def linear_experts(c, nc, stage):
    n0 = c.n0
    sem, bank = c.sem, c.bank
    memory = ExitStack()
    sb = stage_memory(nc, memory)
    R = 4
    router = Router(c, sb, sem, "e_", c.w["e_router"])
    scaled = sb("e_scaled", [P, R, W])
    top_sum = sb("e_top_sum", [P, G])
    probs_w, bias = sb("e_probs_w", [P, G, E]), sb("e_bias", [P, G])
    w_done, scaled_done, used = sem("e_w_done"), sem("e_scaled_done"), sem("e_used")
    w_bank = [bank(1), bank(2)]

    with nc.Block() as block:
        @block.sync
        def _(sp):
            sp_stage(c, sp, stage)

        @block.gpsimd
        def _(pool):
            with pool.Fori(0, NG) as g:
                tail_pool(c, pool, g + n0)

        @block.tensor
        def _(pe):
            with pe.Fori(0, NG) as g:
                pe.wait_ge(c.xTs_loaded, (g + n0 + 1) * 16)
                router.pe(pe, g, bank(0))
                pe.wait_ge(c.resid_done, g + n0 + 1)
                pe.matmul(c.y_bank[:, :], c.ident16[:, :], c.zeros16[:, :], start=True, stop=False)
                pe.wait_ge(router.routed, g + 1)
                for s in range(E + 2):
                    if s < E:
                        pe.wait_ge(scaled_done, g * E + (s + 1))
                        broadcast_weight(c, pe, w_bank[s % 2], router, s).then_inc(w_done, 1)
                    if s >= 2:
                        e = s - 2
                        pe.wait_ge(scaled_done, g * E + (e + 3))
                        for j in range(G):
                            last = pe.matmul(c.y_bank[:, j * P:(j + 1) * P], scaled[:, e % R, j * P:(j + 1) * P],
                                             c.w["e_experts"][:, e, :], start=False,
                                             stop=(e == E - 1 and j == G - 1))
                            if e == E - 1 and j == 0:
                                last.then_inc(c.xTs_used, 1)
                        last.then_inc(used, 1)
                tail_pe(c, pe, g + n0, bank(3))

        @block.scalar
        def _(act):
            with act.Fori(0, NG) as g:
                router.act(act, g)
                tail_act(c, act, g + n0, bank(3))

        @block.vector
        def _(dve):
            ones_credit(dve, [(scaled_done, 2), (used, R)])
            with dve.Fori(0, NG) as g:
                wide = [P, G, E]
                router.dve(dve, g, bank(0))
                dve.tensor_tensor(router.w[:, :, :], router.probs[:, :, :], router.chosen[:, :, :], ALU.mult)
                dve.drain()
                dve.tensor_reduce(top_sum[:, :], router.w[:, :, :], X, ALU.add)
                dve.drain()
                dve.tensor_scalar(top_sum[:, :], top_sum[:, :], 1e-6, None, ALU.add)
                dve.drain()
                dve.reciprocal(router.inverse[:, :], top_sum[:, :])
                dve.drain()
                dve.tensor_tensor(router.w[:, :, :], router.w[:, :, :],
                                  router.inverse[:, :].unsqueeze(2).broadcast_to(wide), ALU.mult)\
                    .then_inc(router.routed, 1)
                dve.drain()
                dve.tensor_tensor(probs_w[:, :, :], router.probs[:, :, :], router.w[:, :, :], ALU.mult)
                for e in range(E):
                    dve.wait_ge(w_done, g * E + (e + 1))
                    dve.wait_ge(used, g * E + (e + 1))
                    if e == 0:
                        dve.wait_ge(c.xTs_loaded, (g + n0 + 1) * 16)
                    dve.tensor_tensor(scaled[:, e % R, :], w_bank[e % 2][:, :], c.xTs[:, :], ALU.mult)\
                        .then_inc(scaled_done, 1)
                dve.tensor_reduce(bias[:, :], probs_w[:, :, :], X, ALU.add)
                dve.drain()
                dve.wait_ge(c.xs_loaded, (g + n0 + 1) * 16)
                for j in range(G):
                    dve.tensor_scalar(c.xs[:, j, :], c.xs[:, j, :], bias[:, j:j + 1], None, ALU.add)
                dve.drain()
                dve.wait_ge(used, g * E + (E + R))
                tail_dve(c, dve, g + n0)
    memory.close()



def gated_experts(c, nc, stage):
    n0 = c.n0
    sem, bank = c.sem, c.bank
    memory = ExitStack()
    sb = stage_memory(nc, memory)
    NSH = 2
    NI = NSH + E
    router = Router(c, sb, sem, "f_", c.w["f_router"])
    scaled = sb("f_scaled", [P, 2, W])
    hidden = sb("f_hidden", [P, 2, W])
    gate = sb("f_gate", [P, 2, W])
    product = sb("f_product", [P, 2, W])
    w_done, scaled_done = sem("f_w_done"), sem("f_scaled_done")
    h_done, gate_done, hidden_done = sem("f_h_done"), sem("f_gate_done"), sem("f_hidden_done")
    gate_copied, masked, out_done = sem("f_gate_copied"), sem("f_masked"), sem("f_out_done")
    product_done, summed = sem("f_product_done"), sem("f_summed")
    router_bank, out_bank = bank(0), bank(5)
    w_bank, h_bank, gate_bank = [bank(1), bank(2)], [bank(3), bank(6)], [bank(4), bank(0)]

    with nc.Block() as block:
        @block.sync
        def _(sp):
            sp_stage(c, sp, stage)

        @block.gpsimd
        def _(pool):
            with pool.Fori(0, NG) as g:
                tail_pool(c, pool, g + n0)

        @block.tensor
        def _(pe):
            def weight(g, s):
                e = s - NSH
                if e == 0:
                    pe.wait_ge(router.routed, g + 1)
                pe.wait_ge(masked, g * E + (e + 1))
                broadcast_weight(c, pe, w_bank[e % 2], router, e).then_inc(w_done, 1)

            def inner(g, s):
                n = g * NI + s
                if s < NSH:
                    rhs, w_h, w_gate = c.xTs[:, :], c.w["f_sw1"][:, s, :], c.w["f_sw2"][:, s, :]
                else:
                    e = s - NSH
                    rhs, w_h, w_gate = scaled[:, e % 2, :], c.w["f_w1"][:, e, :], c.w["f_w3"][:, e, :]
                    pe.wait_ge(scaled_done, g * E + (e + 1))
                pe.wait_ge(hidden_done, n + 1)
                pe.matmul(h_bank[s % 2][:, :], w_h, rhs, start=True, stop=True).then_inc(h_done, 1)
                pe.wait_ge(product_done, n + 1)
                pe.matmul(gate_bank[s % 2][:, :], w_gate, rhs, start=True, stop=True).then_inc(gate_done, 1)

            def outer(g, s):
                n = g * NI + s
                pe.wait_ge(hidden_done, n + 3)
                pe.wait_ge(product_done, n + 2)
                pe.matmul(out_bank[:, :], c.w["f_w2"][:, s - NSH, :], hidden[:, s % 2, :],
                          start=True, stop=True).then_inc(out_done, 1)

            def accumulate(g, s):
                n = g * NI + s
                pe.wait_ge(product_done, n + 3)
                if s == 0:
                    pe.wait_ge(c.resid_done, g + n0 + 1)
                    pe.matmul(c.y_bank[:, :], c.ident16[:, :], c.zeros16[:, :], start=True, stop=False)
                rhs = c.w["f_sw3"][:, s, :] if s < NSH else c.w["ident"][:, :]
                for j in range(G):
                    last = pe.matmul(c.y_bank[:, j * P:(j + 1) * P], product[:, s % 2, j * P:(j + 1) * P], rhs,
                                     start=False, stop=(s == NI - 1 and j == G - 1))
                    if s == NI - 2 and j == 0:
                        last.then_inc(c.xTs_used, 1)
                last.then_inc(summed, 1)

            with pe.Fori(0, NG) as g:
                pe.wait_ge(c.xTs_loaded, (g + n0 + 1) * 16)
                pe.wait_ge(product_done, g * NI + 2)
                router.pe(pe, g, router_bank)
                for s in range(NI + 2):
                    if s < NI:
                        if s == 1:
                            pe.wait_ge(router.shift_done, g + 1)
                        inner(g, s)
                    if NSH <= s + 1 < NI:
                        weight(g, s + 1)
                    if NSH <= s - 1 < NI:
                        outer(g, s - 1)
                    if s >= 2:
                        accumulate(g, s - 2)
                if not c.last:
                    tail_pe(c, pe, g + n0, out_bank)

        @block.scalar
        def _(act):
            ones_credit(act, [(hidden_done, 2)])
            with act.Fori(0, NG) as g:
                router.act(act, g)
                for s in range(NI):
                    n = g * NI + s
                    act.wait_ge(h_done, n + 1)
                    act.wait_ge(product_done, n + 1)
                    bias = c.w["f_b1"][:, s - NSH:s - NSH + 1] if s >= NSH else 0.0
                    act.activation(hidden[:, s % 2, :], h_bank[s % 2][:, :], ACT.Silu, bias=bias)\
                        .then_inc(hidden_done, 1)
                    if s >= NSH:
                        act.wait_ge(gate_done, n + 3)
                        act.activation(gate[:, s % 2, :], gate_bank[s % 2][:, :], ACT.Identity,
                                       bias=c.w["f_b3"][:, s - NSH:s - NSH + 1]).then_inc(gate_copied, 1)
                tail_act(c, act, g + n0, out_bank)

        @block.vector
        def _(dve):
            def scale(g, s):
                e = s - NSH
                dve.wait_ge(w_done, g * E + (e + 1))
                dve.wait_ge(gate_done, g * NI + (s + 1))
                dve.scalar_tensor_tensor(scaled[:, e % 2, :], w_bank[e % 2][:, :], 0.0, c.xTs[:, :],
                                         ALU.max, ALU.mult).then_inc(scaled_done, 1)

            def mask(g, s):
                e = s - NSH
                dve.wait_ge(gate_copied, g * E + (e + 1))
                dve.scalar_tensor_tensor(gate[:, s % 2, :], w_bank[e % 2][:, :], 0.0, gate[:, s % 2, :],
                                         ALU.is_ge, ALU.mult).then_inc(masked, 1)

            def multiply(g, s):
                n = g * NI + s
                if s < NSH:
                    dve.wait_ge(hidden_done, n + 3)
                    dve.wait_ge(gate_done, n + 3)
                    dve.wait_ge(summed, n + 1)
                    dve.tensor_tensor(product[:, s % 2, :], gate_bank[s % 2][:, :], hidden[:, s % 2, :],
                                      ALU.mult).then_inc(product_done, 1)
                    return
                e = s - NSH
                dve.wait_ge(masked, g * E + (e + 3))
                dve.wait_ge(out_done, g * E + (e + 1))
                dve.wait_ge(summed, n + 1)
                dve.scalar_tensor_tensor(product[:, s % 2, :], out_bank[:, :], c.w["f_b2"][:, e:e + 1],
                                         gate[:, s % 2, :], ALU.add, ALU.mult).then_inc(product_done, 1)

            ones_credit(dve, [(gate_done, 2), (masked, 2), (product_done, 2), (summed, 2)])
            with dve.Fori(0, NG) as g:
                router.dve(dve, g, router_bank)
                dve.tensor_tensor(router.w[:, :, :], router.probs[:, :, :], router.chosen[:, :, :], ALU.mult)
                dve.drain()
                dve.scalar_tensor_tensor(router.w[:, :, :], router.chosen[:, :, :], -1.0, router.w[:, :, :],
                                         ALU.add, ALU.add).then_inc(router.routed, 1)
                for s in range(NI + 1):
                    if s > NSH:
                        mask(g, s - 1)
                    if NSH <= s + 1 < NI:
                        scale(g, s + 1)
                    if s >= 1:
                        multiply(g, s - 1)
                dve.wait_ge(summed, g * NI + (NI + 2))
                tail_dve(c, dve, g + n0)
    memory.close()



def mamba(c, nc, stage):
    n0 = c.n0
    sem, bank = c.sem, c.bank
    memory = ExitStack()
    sb = stage_memory(nc, memory)
    TD = DI // P
    U = NS * TD
    R = 4
    L = P + 1
    padded = sb("m_padded", [P, TD, G, P + KC - 1])
    conv = sb("m_conv", [P, TD, W])
    u = sb("m_u", [P, TD, W])
    gate = sb("m_gate", [P, TD, W])
    x_dbl = sb("m_x_dbl", [P, W])
    exp_v, one_plus, lost = sb("m_exp_v", [P, TD, W]), sb("m_one_plus", [P, TD, W]), sb("m_lost", [P, TD, W])
    delta, log_part, du = sb("m_delta", [P, TD, W]), sb("m_log", [P, TD, W]), sb("m_du", [P, TD, W])
    minus_a = sb("m_minus_a", [P, TD, NS])
    decay, drive = sb("m_decay", [P, R, G * L]), sb("m_drive", [P, R, G * L])
    state = sb("m_state", [P, R, G * L])
    c_wide = sb("m_c_wide", [P, 2, W])
    read = sb("m_read", [P, R, W])
    y = sb("m_y", [P, TD, W])

    zeros_set, a_exp, a_ready = sem("m_zeros_set"), sem("m_a_exp"), sem("m_a_ready")
    in_done, in_copied, conv_done = sem("m_in_done"), sem("m_in_copied"), sem("m_conv_done")
    u_done, dbl_done, dbl_copied, dt_done = sem("m_u_done"), sem("m_dbl_done"), sem("m_dbl_copied"), sem("m_dt_done")
    exp_v_done, one_plus_done, log_done = sem("m_exp_v_done"), sem("m_one_plus_done"), sem("m_log_done")
    delta_done, abs_done = sem("m_delta_done"), sem("m_abs_done")
    b_done, c_done, c_copied = sem("m_b_done"), sem("m_c_done"), sem("m_c_copied")
    decay_done, drive_done, scanned = sem("m_decay_done"), sem("m_drive_done"), sem("m_scanned")
    read_done, summed, y_ready = sem("m_read_done"), sem("m_summed"), sem("m_y_ready")
    out_done = sem("m_out_done")
    b_bank, c_bank = [bank(0), bank(1)], [bank(2), bank(3)]
    sum_bank, misc = [bank(4), bank(5)], bank(6)

    def unit(buffer, slot):
        return buffer[:, slot, :].rearrange("p (j t) -> p j t", j=G)[:, :, 1:L]

    def by_sequence(columns):
        return columns.rearrange("p (j t) -> p j t", j=G)

    with nc.Block() as block:
        @block.sync
        def _(sp):
            sp_stage(c, sp, stage)

        @block.gpsimd
        def _(pool):
            for buffer in (padded, decay, drive, x_dbl):
                last = pool.memset(buffer[:], 0.0)
            last.then_inc(zeros_set, 1)
            with pool.Fori(0, NG) as g:
                for m in range(U):
                    n = m // TD
                    pool.wait_ge(scanned, g * U + (m + 5))
                    pool.wait_ge(c_copied, g * NS + (n + 3))
                    pool.wait_ge(summed, g * U + (m + 1))
                    pool.tensor_tensor(by_sequence(read[:, m % R, :]), unit(state, m % R),
                                       by_sequence(c_wide[:, n % 2, :]), ALU.mult).then_inc(read_done, 1)
                tail_pool(c, pool, g + n0)

        @block.tensor
        def _(pe):
            def broadcast(g, n):
                gn = g * NS + n
                row = lambda i: c.w["ident"][:, i:i + 1].broadcast_to([P, P])
                pe.wait_ge(drive_done, (gn + 1) * 2)
                pe.matmul(b_bank[n % 2][:, :], row(DR + n), x_dbl[:, :], start=True, stop=True).then_inc(b_done, 1)
                pe.wait_ge(c_copied, gn + 1)
                pe.matmul(c_bank[n % 2][:, :], row(DR + NS + n), x_dbl[:, :], start=True, stop=True)\
                    .then_inc(c_done, 1)

            pe.wait_ge(zeros_set, 1)
            with pe.Fori(0, NG) as g:
                pe.wait_ge(c.xTs_loaded, (g + n0 + 1) * 16)
                pe.wait_ge(drive_done, g * U + 4)
                pe.wait_ge(c_copied, g * NS + 2)
                for t in range(2 * TD):
                    pe.matmul(bank(t)[:, :], c.w["m_in"][:, t * P:(t + 1) * P], c.xTs[:, :],
                              start=True, stop=True).then_inc(in_done, 1)
                if not c.last:
                    pe.wait_ge(c.yT_copied, g + n0 + 1)
                for t in range(TD):
                    pe.wait_ge(u_done, g * TD + (t + 1))
                    last = pe.matmul(misc[0:DR + 2 * NS, :], c.w["m_x_proj"][:, t, :], u[:, t, :],
                                     start=(t == 0), stop=(t == TD - 1))
                    if t == 0:
                        last.then_inc(c.xTs_used, 1)
                last.then_inc(dbl_done, 1)
                pe.wait_ge(dbl_copied, g + 1)
                pe.wait_ge(y_ready, g * TD + 2)
                for t in range(TD):
                    pe.matmul(sum_bank[t][:, :], c.w["m_dt"][:, t * P:(t + 1) * P], x_dbl[:, :],
                              start=True, stop=True).then_inc(dt_done, 1)
                broadcast(g, 0)
                broadcast(g, 1)
                for n in range(NS):
                    if n + 2 < NS:
                        broadcast(g, n + 2)
                    for t in range(TD):
                        m = n * TD + t
                        pe.wait_ge(read_done, g * U + (m + 1))
                        pe.matmul(sum_bank[t][:, :], c.w["ident"][:, :], read[:, m % R, :],
                                  start=(n == 0), stop=(n == NS - 1)).then_inc(summed, 1)
                pe.wait_ge(y_ready, g * TD + 4)
                pe.wait_ge(c.resid_done, g + n0 + 1)
                for j in range(G):
                    for t in range(TD):
                        last = pe.matmul(c.y_bank[:, j * P:(j + 1) * P], y[:, t, j * P:(j + 1) * P],
                                         c.w["m_out"][:, t, :], start=(t == 0), stop=(t == TD - 1))
                last.then_inc(out_done, 1)
                tail_pe(c, pe, g + n0, misc)

        @block.scalar
        def _(act):
            act.activation(minus_a[:, :, :], c.w["m_a_log"][:, :, :], ACT.Exp).then_inc(a_exp, 1)
            act.wait_ge(zeros_set, 1)
            act.wait_ge(a_ready, 1)
            ones_credit(act, [(c_copied, 2)])
            with act.Fori(0, NG) as g:
                for t in range(TD):
                    act.wait_ge(in_done, g * (2 * TD) + (t + 1))
                    act.wait_ge(conv_done, g * TD + (t + 1))
                    act.activation(padded[:, t, :, KC - 1:], by_sequence(bank(t)[:, :]), ACT.Copy)\
                        .then_inc(in_copied, 1)
                for t in range(TD):
                    act.wait_ge(in_done, g * (2 * TD) + (TD + t + 1))
                    act.wait_ge(out_done, g + 1)
                    act.activation(gate[:, t, :], bank(TD + t)[:, :], ACT.Silu)
                for t in range(TD):
                    act.wait_ge(conv_done, g * TD + (t + 3))
                    act.activation(u[:, t, :], conv[:, t, :], ACT.Silu).then_inc(u_done, 1)
                act.wait_ge(dbl_done, g + 1)
                act.activation(x_dbl[0:DR + 2 * NS, :], misc[0:DR + 2 * NS, :], ACT.Copy).then_inc(dbl_copied, 1)
                for t in range(TD):
                    act.wait_ge(dt_done, g * TD + (t + 1))
                    act.activation(exp_v[:, t, :], sum_bank[t][:, :], ACT.Abs, bias=c.w["m_dt_bias"][:, t:t + 1])\
                        .then_inc(abs_done, 1)
                act.wait_ge(abs_done, g * TD + TD)
                act.activation(exp_v[:, :, :], exp_v[:, :, :], ACT.Exp, scale=-1.0).then_inc(exp_v_done, 1)
                act.wait_ge(one_plus_done, g + 1)
                act.activation(log_part[:, :, :], one_plus[:, :, :], ACT.Ln).then_inc(log_done, 1)
                act.wait_ge(delta_done, g + 1)
                for n in range(NS):
                    for t in range(TD):
                        m = n * TD + t
                        act.wait_ge(scanned, g * U + (m + 1))
                        act.activation(unit(decay, m % R), by_sequence(delta[:, t, :]), ACT.Exp,
                                       scale=minus_a[:, t, n:n + 1]).then_inc(decay_done, 1)
                    act.wait_ge(c_done, g * NS + (n + 1))
                    act.wait_ge(summed, (g * NS + n) * 2 + 2)
                    act.activation(c_wide[:, n % 2, :], c_bank[n % 2][:, :], ACT.Copy).then_inc(c_copied, 1)
                tail_act(c, act, g + n0, misc)

        @block.vector
        def _(dve):
            def taps(g):
                for k in range(KC):
                    for t in range(TD):
                        if k == 0:
                            dve.wait_ge(in_copied, g * TD + (t + 1))
                        tap = KC - 1 - k
                        src = padded[:, t, :, tap:tap + P]
                        out = by_sequence(conv[:, t, :])
                        weight = c.w["m_conv"][:, t, tap:tap + 1]
                        if k == 0:
                            last = dve.tensor_scalar(out, src, weight, c.w["m_conv_bias"][:, t:t + 1],
                                                     ALU.mult, ALU.add)
                        else:
                            last = dve.scalar_tensor_tensor(out, src, weight, out, ALU.mult, ALU.add)
                        if k == KC - 1:
                            last.then_inc(conv_done, 1)
                    dve.drain()

            def softplus(g):
                dve.wait_ge(exp_v_done, g + 1)
                dve.tensor_scalar(one_plus[:, :, :], exp_v[:, :, :], 1.0, None, ALU.add).then_inc(one_plus_done, 1)
                for t in range(TD):
                    dve.tensor_scalar(delta[:, t, :], sum_bank[t][:, :], c.w["m_dt_bias"][:, t:t + 1], 0.0,
                                      ALU.add, ALU.max)
                dve.drain()
                dve.scalar_tensor_tensor(lost[:, :, :], one_plus[:, :, :], -1.0, exp_v[:, :, :],
                                         ALU.add, ALU.subtract)
                dve.drain()
                dve.tensor_tensor(delta[:, :, :], delta[:, :, :], lost[:, :, :], ALU.subtract)
                dve.drain()
                dve.wait_ge(log_done, g + 1)
                dve.tensor_tensor(delta[:, :, :], delta[:, :, :], log_part[:, :, :], ALU.add).then_inc(delta_done, 1)
                dve.drain()
                dve.tensor_tensor(du[:, :, :], delta[:, :, :], u[:, :, :], ALU.mult)
                dve.drain()

            def drive_unit(g, m):
                n, t = m // TD, m % TD
                dve.wait_ge(b_done, g * NS + (n + 1))
                dve.wait_ge(scanned, g * U + (m + 1))
                dve.tensor_tensor(unit(drive, m % R), by_sequence(b_bank[n % 2][:, :]), by_sequence(du[:, t, :]),
                                  ALU.mult).then_inc(drive_done, 1)

            def scan_unit(g, m):
                dve.wait_ge(decay_done, g * U + (m + 1))
                dve.wait_ge(drive_done, g * U + (m + 5))
                dve.wait_ge(summed, g * U + (m + 1))
                dve.tensor_tensor_scan(state[:, m % R, :], decay[:, m % R, :], drive[:, m % R, :], 0.0,
                                       ALU.mult, ALU.add).then_inc(scanned, 1)

            dve.wait_ge(a_exp, 1)
            dve.tensor_scalar(minus_a[:, :, :], minus_a[:, :, :], -1.0, None, ALU.mult).then_inc(a_ready, 1)
            dve.wait_ge(zeros_set, 1)
            ones_credit(dve, [(drive_done, 4), (scanned, 4), (summed, 4), (conv_done, 2), (y_ready, 2), (out_done, 1)])
            with dve.Fori(0, NG) as g:
                taps(g)
                softplus(g)
                drive_unit(g, 0)
                for m in range(U):
                    if m + 1 < U:
                        drive_unit(g, m + 1)
                    scan_unit(g, m)
                for t in range(TD):
                    dve.wait_ge(summed, g * U + (U - TD + t + 5))
                    if t == 0:
                        dve.wait_ge(out_done, g + 1)
                    dve.scalar_tensor_tensor(y[:, t, :], u[:, t, :], c.w["m_d"][:, t:t + 1], sum_bank[t][:, :],
                                             ALU.mult, ALU.add)
                dve.drain()
                for t in range(TD):
                    dve.tensor_tensor(y[:, t, :], y[:, t, :], gate[:, t, :], ALU.mult).then_inc(y_ready, 1)
                dve.wait_ge(out_done, g + 2)
                tail_dve(c, dve, g + n0)
    memory.close()



WEIGHTS = {
    "ident": ([P, P], F32), "causal": ([P, P], F32), "minus_half": ([P, G], F32),
    "a_wq": ([P, AH * AD], F32), "a_wk": ([P, AH * AD], F32), "a_wv": ([P, AH * AD], F32),
    "a_wo": ([P, 8, P], F32),
    "earlier": ([P, E, E], F32), "e_router": ([P, E], F32), "e_experts": ([P, E, P], F32),
    "m_in": ([P, 2 * DI], F32), "m_conv": ([P, 2, KC], F32), "m_conv_bias": ([P, 2], F32),
    "m_x_proj": ([P, 2, DR + 2 * NS], F32), "m_dt": ([P, DI], F32), "m_dt_bias": ([P, 2], F32),
    "m_a_log": ([P, 2, NS], F32), "m_d": ([P, 2], F32), "m_out": ([P, 2, P], F32),
    "f_router": ([P, E], F32), "f_w1": ([P, E, P], F32), "f_w2": ([P, E, P], F32), "f_w3": ([P, E, P], F32),
    "f_b1": ([P, E], F32), "f_b2": ([P, E], F32), "f_b3": ([P, E], F32),
    "f_sw1": ([P, 2, P], F32), "f_sw2": ([P, 2, P], F32), "f_sw3": ([P, 2, P], F32),
    "ones_row": ([1, P], F32), "head_of": ([P, XH], F32),
    "x0_wq": ([P, P], F32), "x0_wk": ([P, P], F32), "x0_wv": ([P, P], F32), "x0_wo": ([P, P], F32),
    "x0_bq": ([P, 1], F32), "x0_bk": ([P, 1], F32), "x0_bv": ([SC, P], F32), "x0_bo": ([1, P], F32),
    "x0_select": ([P, 3, 3], F32), "x0_feat_bias": ([3, 1], F32),
    "x0_w1": ([3, 64], F32), "x0_b1": ([64, 1], F32), "x0_w2": ([64, P], F32), "x0_b2": ([64, 1], F32),
    "x0_w3": ([64, P], F32), "x0_b3": ([P, 1], F32),
    "x1_wq": ([P, P], F32), "x1_wk": ([P, P], F32), "x1_wv": ([P, P], F32), "x1_wo": ([P, P], F32),
    "x1_bo": ([1, P], F32),
}


def decoder(nc, dram, out, stages=(0, 1, 2, 3, 4, 5)):
    c = Core()
    c.x_dram = dram["x"].rearrange("b p d -> p b d")
    c.xT_dram = dram["xT"]
    c.dram = dram
    c.out_dram = out.rearrange("b p d -> p b d")
    c.sem = nc.alloc_semaphore
    c.sb = lambda name, shape, dtype=F32: nc.alloc_sbuf_tensor(name, shape, dtype)
    psum = nc.alloc_psum_tensor("psum", [P, 8, 512], F32)
    c.psum = psum
    c.bank = lambda i: psum[:, i, :]
    c.y_bank = c.bank(7)
    c.w = {name: c.sb("w_" + name, shape, dtype) for name, (shape, dtype) in WEIGHTS.items()}
    c.ident16, c.zeros16, c.causal16 = (c.sb(name, [P, n], BF16) for name, n in
                                        (("ident16", P), ("zeros16", W), ("causal16", W)))
    c.x_all = c.sb("x_all", [P, B, P])
    c.xT_all = c.sb("xT_all", [P, B * P])
    c.xs = c.sb("xs", [P, G, P])
    c.xTs = c.sb("xTs", [P, W])
    c.ctxTs = c.sb("ctxTs", [P, G * SC])
    c.ys = c.sb("ys", [P, G, P])
    c.yTs = c.sb("yTs", [P, W])
    c.resid = c.sb("resid", [P, G, P])
    c.bn = c.sb("bn", [P, G, 6])
    c.meanvar = c.sb("meanvar", [P, G, 2])
    c.var_eps = c.sb("var_eps", [P, G])
    c.rstd = c.sb("rstd", [P, G])

    c.loaded = c.sem("weights_loaded")
    c.resid_done = c.sem("resid_done")
    c.var_done, c.rstd_done = c.sem("var_done"), c.sem("rstd_done")
    c.y_normed, c.y_transposed = c.sem("y_normed"), c.sem("y_transposed")
    c.y_stored, c.yT_copied, c.yT_stored = c.sem("y_stored"), c.sem("yT_copied"), c.sem("yT_stored")
    c.xs_loaded, c.xTs_loaded, c.xTs_used = c.sem("xs_loaded"), c.sem("xTs_loaded"), c.sem("xTs_used")
    c.ctx_loaded = c.sem("ctx_loaded")

    with nc.Block() as block:
        @block.sync
        def _(sp):
            ones_credit(sp, [(c.resid_done, 1), (c.y_stored, 16), (c.yT_stored, 16), (c.y_transposed, 1),
                             (c.yT_copied, 1), (c.xTs_used, 1)])
            for name in c.w:
                sp.dma_start(c.w[name][:], dram[name]).then_inc(c.loaded, 16)
            sp.wait_ge(c.loaded, 16 * len(c.w))

        @block.gpsimd
        def _(pool):
            pool.memset(c.zeros16[:, :], 0.0)

        @block.vector
        def _(dve):
            dve.wait_ge(c.loaded, 16 * len(c.w))
            dve.tensor_copy(c.ident16[:, :], c.w["ident"][:, :])
            dve.tensor_copy(c.causal16[:, :].rearrange("p (m t) -> p m t", m=G),
                            c.w["causal"][:, :].unsqueeze(1).broadcast_to([P, G, P]))

    for stage in stages:
        c.last = stage == stages[-1]
        c.n0 = stages.index(stage) * NG
        c.ctx0 = sum(x in (1, 4) for x in stages[:stages.index(stage)]) * NG
        STAGES[stage](c, nc, stage)


STAGES = {0: causal_attention, 1: cross_attention, 2: linear_experts, 3: mamba, 4: cross_attention,
          5: gated_experts}



def by_block(rows):
    return rows.reshape(2, P, *rows.shape[1:]).swapaxes(0, 1)


def block_diagonal(weight):
    import numpy as np
    out = np.zeros((P, P), weight.dtype)
    for h in range(XH):
        out[h * XD:(h + 1) * XD, h * XD:(h + 1) * XD] = weight
    return out


def statistics_weights():
    import numpy as np
    out = np.zeros((P, 3, 3), np.float32)
    out[:, 0, 0] = XD ** -0.5 / (P * SC)
    out[:, 1, 1] = XD ** -0.5 / P
    out[:, 2, 2] = 1.0 / (P * (SC - 1))
    return out


def layouts(a):
    import numpy as np
    f32 = np.float32
    token = np.arange(P)
    d = {
        "x": a["x"],
        "xT": a["x"].transpose(2, 0, 1).reshape(P, B * P),
        "ident": np.eye(P, dtype=f32),
        "causal": np.where(token[None, :] > token[:, None], f32(-1e30), f32(0.0)),
        "minus_half": np.full((P, G), -0.5, f32),
        "a_wq": a["L0_attn_w_q"].transpose(2, 0, 1).reshape(P, AH * AD),
        "a_wk": a["L0_attn_w_k"].transpose(2, 0, 1).reshape(P, AH * AD),
        "a_wv": a["L0_attn_w_v"].transpose(2, 0, 1).reshape(P, AH * AD),
        "a_wo": a["L0_attn_w_o"].T.reshape(8, P, P).transpose(1, 0, 2),
        "earlier": np.broadcast_to(np.arange(E)[None, :] < np.arange(E)[:, None], (P, E, E)).astype(f32),
        "e_router": a["L0_ffn_router_w"].T, "e_experts": a["L0_ffn_expert_weights"].transpose(1, 0, 2),
        "m_in": a["L1_attn_in_proj_w"].T, "m_conv": by_block(a["L1_attn_conv_w"][:, 0, :]),
        "m_conv_bias": by_block(a["L1_attn_conv_b"]), "m_x_proj": by_block(a["L1_attn_x_proj_w"].T),
        "m_dt": np.concatenate([a["L1_attn_dt_proj_w"].T, np.zeros((P - DR, DI), f32)]),
        "m_dt_bias": by_block(a["L1_attn_dt_proj_b"]), "m_a_log": by_block(a["L1_attn_A_log"]),
        "m_d": by_block(a["L1_attn_D"]), "m_out": by_block(a["L1_attn_out_proj_w"].T),
        "f_router": a["L1_ffn_gate_w"].T, "f_w1": a["L1_ffn_w1"].transpose(2, 0, 1),
        "f_w2": a["L1_ffn_w2"].transpose(2, 0, 1), "f_w3": a["L1_ffn_w3"].transpose(2, 0, 1),
        "f_b1": a["L1_ffn_b1"].T, "f_b2": a["L1_ffn_b2"].T, "f_b3": a["L1_ffn_b3"].T,
        "f_sw1": a["L1_ffn_sw1"].T.reshape(P, 2, P), "f_sw2": a["L1_ffn_sw2"].T.reshape(P, 2, P),
        "f_sw3": by_block(a["L1_ffn_sw3"].T),
        "ones_row": np.ones((1, P), f32),
        "head_of": (token[:, None] // XD == np.arange(XH)[None, :]).astype(f32),
        "ctxT": a["ctx_1024"].transpose(2, 0, 1).reshape(P, B * SC),
        "mask": np.broadcast_to(a["mask_Bx1x1xS2_if1"].reshape(1, B * SC), (P, B * SC)),
        "x0_wq": a["L0_xattn_Wq"].T, "x0_wk": a["L0_xattn_Wk"].T, "x0_wv": a["L0_xattn_Wv"].T,
        "x0_wo": a["L0_xattn_Wo"].T,
        "x0_bq": a["L0_xattn_bq"][:, None], "x0_bk": a["L0_xattn_bk"][:, None],
        "x0_bv": np.broadcast_to(a["L0_xattn_bv"][None, :], (SC, P)), "x0_bo": a["L0_xattn_bo"][None, :],
        "x0_select": statistics_weights(),
        "x0_feat_bias": np.array([[0.0], [0.0], [-1.0 / (SC * (SC - 1))]], f32),
        "x0_w1": a["L0_xattn_w1"].T, "x0_b1": a["L0_xattn_b1"][:, None],
        "x0_w2": np.concatenate([a["L0_xattn_w2"].T, np.zeros((64, 64), f32)], 1), "x0_b2": a["L0_xattn_b2"][:, None],
        "x0_w3": np.broadcast_to(a["L0_xattn_w3"].T, (64, P)),
        "x0_b3": np.broadcast_to(a["L0_xattn_b3"][None, :], (P, 1)),
        "x1_wq": block_diagonal(a["L1_xattn_Wq"]), "x1_wk": block_diagonal(a["L1_xattn_Wk"]),
        "x1_wv": block_diagonal(a["L1_xattn_Wv"].T), "x1_wo": a["L1_xattn_Wo"].T,
        "x1_bo": a["L1_xattn_bo"][None, :],
    }
    return {k: np.ascontiguousarray(v) for k, v in d.items()}


def kernel(**inputs):
    import numpy as np
    import concourse.bacc as bacc
    from concourse.bass_utils import run_bass_kernel_spmd

    arrays = layouts({name: np.asarray(value) for name, value in inputs.items()})
    nc = bacc.Bacc("TRN2", target_bir_lowering=False, num_devices=1)
    dram = {name: nc.dram_tensor("in_" + name, v.shape, mybir.dt.from_np(v.dtype), kind="ExternalInput").ap()
            for name, v in arrays.items()}
    out = nc.dram_tensor("out", (B, P, P), F32, kind="ExternalOutput").ap()
    decoder(nc, dram, out)
    result = run_bass_kernel_spmd(nc, [{"in_" + name: v for name, v in arrays.items()}], core_ids=[0])
    return result.results[0]["out"]
```

```python
from contextlib import ExitStack

import concourse.bass as bass
from concourse import mybir

F32 = mybir.dt.float32
BF16 = mybir.dt.bfloat16
I32 = mybir.dt.int32
ALU = mybir.AluOpType
ACT = mybir.ActivationFunctionType
X = mybir.AxisListType.X

P = 128
B = 32
G = 4
NG = B // G
W = G * P
SC = 77
EPS = 1e-5

AH, AD = 16, 64
XH, XD = 16, 8
E = 8
DI, NS, DR, KC = 256, 16, 64, 4
LOG_T_MIN, LOG_T_MAX = -2.302585092994046, 2.302585092994046


def stage_memory(nc, memory):
    return lambda name, shape, dtype=F32: memory.enter_context(nc.sbuf_tensor(name, shape, dtype))


class Core:
    pass


def ones_credit(engine, pairs):
    for semaphore, count in pairs:
        engine.sem_inc(semaphore, count)



def tail_dve_variance(c, dve, n):
    dve.wait_ge(c.xs_loaded, (n + 1) * 16)
    dve.tensor_tensor(c.resid[:, :, :], c.y_bank[:, :].rearrange("p (j d) -> p j d", j=G), c.xs[:, :, :],
                      ALU.add).then_inc(c.resid_done, 1)
    dve.drain()
    for j in range(G):
        dve.bn_stats(c.bn[:, j, :], c.resid[:, j, :])
    dve.drain()
    for j in range(G):
        dve.bn_aggr(c.meanvar[:, j, :], c.bn[:, j, :])
    dve.drain()
    dve.tensor_scalar(c.var_eps[:, :], c.meanvar[:, :, 1], EPS, None, ALU.add).then_inc(c.var_done, 1)


def tail_dve_norm(c, dve, n):
    dve.wait_ge(c.rstd_done, n + 1)
    dve.wait_ge(c.y_stored, (n + 1) * 16)
    if not c.last:
        dve.wait_ge(c.y_transposed, n + 1)
    for j in range(G):
        last = dve.tensor_scalar(c.ys[:, j, :], c.resid[:, j, :], c.meanvar[:, j, 0:1], c.rstd[:, j:j + 1],
                                 ALU.subtract, ALU.mult)
    last.then_inc(c.y_normed, 1)


def tail_dve(c, dve, n):
    tail_dve_variance(c, dve, n)
    tail_dve_norm(c, dve, n)


def tail_pool(c, pool, n):
    pool.wait_ge(c.var_done, n + 1)
    pool.tensor_tensor(c.rstd[:, :], c.var_eps[:, :], c.w["minus_half"][:, :], ALU.pow).then_inc(c.rstd_done, 1)


def tail_pe(c, pe, n, bank):
    if c.last:
        return
    pe.wait_ge(c.y_normed, n + 1)
    for j in range(G):
        last = pe.transpose(bank[:, j * P:(j + 1) * P], c.ys[:, j, :], c.w["ident"][:, :])
    last.then_inc(c.y_transposed, 1)


def tail_act(c, act, n, bank):
    if c.last:
        return
    act.wait_ge(c.y_transposed, n + 2)
    act.wait_ge(c.yT_stored, (n + 1) * 16)
    act.activation(c.yTs[:, :], bank[:, :], ACT.Copy).then_inc(c.yT_copied, 1)


def load_xT(c, sp, n, g, source_T, with_ctx=False):
    sp.wait_ge(c.xTs_used, n + 1)
    sp.dma_start(c.xTs[:, :], source_T[:, bass.ds(g * W, W)]).then_inc(c.xTs_loaded, 16)
    if with_ctx:
        sp.dma_start(c.ctxTs[:, :], c.dram["ctxT"][:, bass.ds(g * (G * SC), G * SC)]).then_inc(c.ctx_loaded, 16)


def load_xs(c, sp, n, g, source):
    sp.wait_ge(c.resid_done, n + 1)
    sp.dma_start(c.xs[:, :, :], source[:, bass.ds(g * G, G), :]).then_inc(c.xs_loaded, 16)


def store_x(c, sp, n, g, target, target_T):
    sp.wait_ge(c.y_normed, n + 1)
    sp.dma_start(target[:, bass.ds(g * G, G), :], c.ys[:, :, :]).then_inc(c.y_stored, 16)
    if target_T is not None:
        sp.wait_ge(c.yT_copied, n + 2)
        sp.dma_start(target_T[:, bass.ds(g * W, W)], c.yTs[:, :]).then_inc(c.yT_stored, 16)


def ends_of(c):
    source = (c.x_dram, c.xT_dram) if c.n0 == 0 else (c.x_all, c.xT_all)
    target = (c.out_dram, None) if c.last else (c.x_all, c.xT_all)
    return source + target


def all_stored(c, sp):
    sp.wait_ge(c.y_stored, (c.n0 + NG) * 16 + 16)
    if not c.last:
        sp.wait_ge(c.yT_stored, (c.n0 + NG) * 16 + 16)


def sp_stage(c, sp):
    n0 = c.n0
    source, source_T, target, target_T = ends_of(c)
    load_xT(c, sp, n0, 0, source_T)
    load_xs(c, sp, n0, 0, source)
    with sp.Fori(0, NG - 1) as g:
        load_xT(c, sp, g + n0 + 1, g + 1, source_T)
        load_xs(c, sp, g + n0 + 1, g + 1, source)
        store_x(c, sp, g + n0, g, target, target_T)
    store_x(c, sp, n0 + NG - 1, NG - 1, target, target_T)
    all_stored(c, sp)


def sp_stage_ahead(c, sp):
    n0 = c.n0
    source, source_T, target, target_T = ends_of(c)
    load_xT(c, sp, n0, 0, source_T, with_ctx=True)
    load_xT(c, sp, n0 + 1, 1, source_T, with_ctx=True)
    load_xs(c, sp, n0, 0, source)
    with sp.Fori(0, NG - 2) as g:
        load_xT(c, sp, g + n0 + 2, g + 2, source_T, with_ctx=True)
        load_xs(c, sp, g + n0 + 1, g + 1, source)
        store_x(c, sp, g + n0, g, target, target_T)
    load_xs(c, sp, n0 + NG - 1, NG - 1, source)
    store_x(c, sp, n0 + NG - 2, NG - 2, target, target_T)
    store_x(c, sp, n0 + NG - 1, NG - 1, target, target_T)
    all_stored(c, sp)



def causal_attention(c, nc, stage):
    n0 = c.n0
    NQ = AH // 4
    CH = 6
    sem, bank = c.sem, c.bank
    memory = ExitStack()
    sb = stage_memory(nc, memory)

    qT = sb("qT", [P, 2, 8, P])
    kT = sb("kT", [P, 2, 8, P])
    v = sb("v", [P, 2, AH, AD])
    probs = sb("probs", [P, 4, 4, P])
    probsT = sb("probsT", [P, 2, 4, P])
    row_max = sb("row_max", [P, 2, 4])
    row_sum, row_inv = sb("row_sum", [P, 2, 4]), sb("row_inv", [P, 2, 4])
    heads_outT = sb("heads_outT", [P, 2, 4, P])

    proj_bank = [bank(0), bank(1)]
    score_bank = [bank(2), bank(3)]
    probsT_bank, outT_bank = bank(4), [bank(5), bank(6)]

    proj_done, proj_copied = sem("a_proj_done"), sem("a_proj_copied")
    scores_done, scores_shifted = sem("a_scores_done"), sem("a_scores_shifted")
    probs_done, transposed = sem("a_probs_done"), sem("a_transposed")
    probsT_copied, pv_done = sem("a_probsT_copied"), sem("a_pv_done")
    normed, outT_copied = sem("a_normed"), sem("a_outT_copied")
    outT_used = sem("a_outT_used")

    def quad_heads(q):
        return [8 * (q // 2) + q % 2 + 2 * m for m in range(4)]

    with nc.Block() as block:
        @block.sync
        def _(sp):
            sp_stage(c, sp)

        @block.gpsimd
        def _(pool):
            with pool.Fori(0, NG) as g:
                tail_pool(c, pool, g + n0)

        @block.tensor
        def _(pe):
            def project(g, j, chunks):
                for ch in chunks:
                    t = g * (G * CH) + (j * CH + ch)
                    out = proj_bank[ch % 2]
                    if ch == 0 and j == 0:
                        pe.wait_ge(c.xTs_loaded, (g + n0 + 1) * 16)
                    pe.wait_ge(proj_copied, t + 1)
                    xj = c.xTs[:, j * P:(j + 1) * P]
                    if ch < 4:
                        w = (c.w["a_wq"], c.w["a_wk"])[ch // 2]
                        for m in range(4):
                            hp = 4 * (ch % 2) + m
                            last = pe.matmul(out[:, m * P:(m + 1) * P], w[:, hp * P:(hp + 1) * P], xj,
                                             start=True, stop=True)
                    else:
                        last = pe.matmul(out[:, :], xj, c.w["a_wv"][:, (ch - 4) * 512:(ch - 3) * 512],
                                         start=True, stop=True)
                    last.then_inc(proj_done, 1)

            def scores(g, q):
                j, r = q // NQ, (q // NQ) % 2
                if q % NQ == 0:
                    pe.wait_ge(proj_copied, g * (G * CH) + (j * CH + 4 + 2))
                pe.wait_ge(scores_shifted, g * (G * NQ) + (q + 1))
                out = score_bank[q % 2]
                mask = pe.matmul(out[:, :], c.ident16[:, :], c.causal16[:, :], start=True, stop=False)
                if q == (G - 2) * NQ + 3:
                    mask.then_inc(c.xTs_used, 1)
                for m, h in enumerate(quad_heads(q % NQ)):
                    rows = slice(64 * (h % 2), 64 * (h % 2) + 64)
                    last = pe.matmul(out[:, m * P:(m + 1) * P], qT[rows, r, h // 2, :], kT[rows, r, h // 2, :],
                                     start=False, stop=(m == 3))
                last.then_inc(scores_done, 1)

            def transpose_probs(g, q):
                pe.wait_ge(normed, g * (G * NQ) + (q + 1))
                pe.wait_ge(probsT_copied, g * (G * NQ) + (q + 1))
                for m in range(4):
                    last = pe.transpose(probsT_bank[:, m * P:(m + 1) * P], probs[:, q % 4, m, :],
                                        c.w["ident"][:, :])
                last.then_inc(transposed, 1)

            def times_v(g, q):
                j, half = q // NQ, q // 2
                pe.wait_ge(probsT_copied, g * (G * NQ) + (q + 2))
                if q % NQ == 0:
                    pe.wait_ge(proj_copied, g * (G * CH) + (j * CH + CH + 2))
                if q % 2 == 0:
                    pe.wait_ge(outT_copied, g * (G * 2) + (half + 1))
                if q == 0 and not c.last:
                    pe.wait_ge(c.yT_copied, g + n0 + 1)
                for m, h in enumerate(quad_heads(q % NQ)):
                    rows = slice(64 * (h % 2), 64 * (h % 2) + 64)
                    last = pe.matmul(outT_bank[half % 2][rows, m * P:(m + 1) * P], v[:, j % 2, h, :],
                                     probsT[:, q % 2, m, :], start=True, stop=True)
                last.then_inc(pv_done, 1)

            def project_out(g, half):
                j = half // 2
                pe.wait_ge(outT_copied, g * (G * 2) + (half + 3))
                if half == 0:
                    pe.wait_ge(c.resid_done, g + n0 + 1)
                for m in range(4):
                    hp = 4 * (half % 2) + m
                    last = pe.matmul(c.y_bank[:, j * P:(j + 1) * P], heads_outT[:, half % 2, m, :],
                                     c.w["a_wo"][:, hp, :], start=(hp == 0), stop=(hp == 7))
                last.then_inc(outT_used, 1)

            with pe.Fori(0, NG) as g:
                project(g, 0, range(CH))
                for s in range(G * NQ + 5):
                    if s < G * NQ:
                        scores(g, s)
                    if 2 <= s < G * NQ + 2:
                        transpose_probs(g, s - 2)
                    if s % NQ < 3 and s // NQ + 1 < G:
                        project(g, s // NQ + 1, range(2 * (s % NQ), 2 * (s % NQ) + 2))
                    if 3 <= s < G * NQ + 3:
                        times_v(g, s - 3)
                    if s >= 6 and s % 2 == 0:
                        project_out(g, (s - 6) // 2)
                tail_pe(c, pe, g + n0, outT_bank[0])

        @block.scalar
        def _(act):
            def copy_projection(g, j, chunks):
                for ch in chunks:
                    t = g * (G * CH) + (j * CH + ch)
                    r = j % 2
                    act.wait_ge(proj_done, t + 1)
                    if ch == 0:
                        act.wait_ge(scores_done, g * (G * NQ) + ((j - 2) * NQ + NQ + 8))
                    if ch == 4:
                        act.wait_ge(pv_done, g * (G * NQ) + ((j - 2) * NQ + NQ + 8))
                    src = proj_bank[ch % 2]
                    if ch < 4:
                        dst = (qT, kT)[ch // 2][:, r, 4 * (ch % 2):4 * (ch % 2) + 4, :]
                        act.activation(dst, src[:, :].rearrange("p (m t) -> p m t", m=4), ACT.Copy)\
                            .then_inc(proj_copied, 1)
                    else:
                        dst = v[:, r, 8 * (ch - 4):8 * (ch - 3), :]
                        act.activation(dst, src[:, :].rearrange("p (h d) -> p h d", h=8), ACT.Copy)\
                            .then_inc(proj_copied, 1)

            def exp(g, q):
                act.wait_ge(scores_shifted, g * (G * NQ) + (q + 1 + 2))
                act.activation(probs[:, q % 4, :, :], probs[:, q % 4, :, :], ACT.Exp, scale=float(AD) ** -0.5)\
                    .then_inc(probs_done, 1)

            def copy_probsT(g, q):
                act.wait_ge(transposed, g * (G * NQ) + (q + 1 + 4))
                act.wait_ge(pv_done, g * (G * NQ) + (q - 1 + 8))
                act.activation(probsT[:, q % 2, :, :], probsT_bank[:, :].rearrange("p (m t) -> p m t", m=4),
                               ACT.Copy).then_inc(probsT_copied, 1)

            def copy_outT(g, half):
                act.wait_ge(pv_done, g * (G * NQ) + (2 * half + 2 + 8))
                act.wait_ge(outT_used, g * (G * 2) + (half + 1))
                act.activation(heads_outT[:, half % 2, :, :], outT_bank[half % 2][:, :].rearrange("p (m t) -> p m t", m=4),
                               ACT.Copy).then_inc(outT_copied, 1)

            ones_credit(act, [(proj_copied, 2), (probsT_copied, 1), (outT_copied, 2)])
            with act.Fori(0, NG) as g:
                copy_projection(g, 0, range(CH))
                for s in range(G * NQ + 5):
                    if s < G * NQ:
                        exp(g, s)
                    if 2 <= s < G * NQ + 2:
                        copy_probsT(g, s - 2)
                    if s % NQ < 3 and s // NQ + 1 < G:
                        copy_projection(g, s // NQ + 1, range(2 * (s % NQ), 2 * (s % NQ) + 2))
                    if s >= 5 and s % 2 == 1:
                        copy_outT(g, (s - 5) // 2)
                tail_act(c, act, g + n0, outT_bank[0])

        @block.vector
        def _(dve):
            def shift(g, q):
                s = g * (G * NQ) + q
                dve.wait_ge(scores_done, s + (1 + 8))
                dve.wait_ge(transposed, s + 1)
                src = score_bank[q % 2][:, :].rearrange("p (m t) -> p m t", m=4)
                dve.tensor_reduce(row_max[:, q % 2, :], src, X, ALU.max)
                dve.drain()
                dve.tensor_tensor(probs[:, q % 4, :, :], src,
                                  row_max[:, q % 2, :].unsqueeze(2).broadcast_to([P, 4, P]),
                                  ALU.subtract).then_inc(scores_shifted, 1)

            def normalise(g, q):
                dve.wait_ge(probs_done, g * (G * NQ) + (q + 1))
                dve.tensor_reduce(row_sum[:, q % 2, :], probs[:, q % 4, :, :], X, ALU.add)
                dve.drain()
                dve.reciprocal(row_inv[:, q % 2, :], row_sum[:, q % 2, :])
                dve.drain()
                dve.tensor_tensor(probs[:, q % 4, :, :], probs[:, q % 4, :, :],
                                  row_inv[:, q % 2, :].unsqueeze(2).broadcast_to([P, 4, P]),
                                  ALU.mult).then_inc(normed, 1)

            ones_credit(dve, [(scores_shifted, 2), (transposed, 4), (scores_done, 8), (pv_done, 8), (outT_used, 2)])
            with dve.Fori(0, NG) as g:
                for s in range(G * NQ + 1):
                    if s < G * NQ:
                        shift(g, s)
                    if s >= 1:
                        normalise(g, s - 1)
                dve.wait_ge(outT_used, g * (2 * G) + (2 * G + 2))
                tail_dve(c, dve, g + n0)
    memory.close()



def cross_attention(c, nc, stage):
    n0 = c.n0
    tempered = stage == 1
    w = {k[3:]: v for k, v in c.w.items() if k.startswith("x0_" if tempered else "x1_")}
    NC = 4
    HC = XH // NC
    QF = HC * XD
    T = G * NC
    SCORES_AT = [None, 1, 5, 9]
    MLP_AT = 13
    A_ENTRIES = ["q", "k0", "k1", "v"] if tempered else ["k0", "v"]
    k_parts = 2 if tempered else 1
    NA, NM = len(A_ENTRIES), 4 if tempered else 0
    sem, bank = c.sem, c.bank
    memory = ExitStack()
    sb = stage_memory(nc, memory)
    pre = f"s{stage}_"

    q_quad = sb(pre + "q_quad", [P, NC, W])
    k_sb, v_sb = sb(pre + "k_sb", [P, G, SC]), sb(pre + "v_sb", [P, W])
    keys = sb(pre + "keys", [P, G, HC, SC])
    v_spread = sb(pre + "v_spread", [P, G, XH, QF])
    raw = sb(pre + "raw", [P, G, XH, SC])
    probs = sb(pre + "probs", [P, G, XH, SC])
    row_max = sb(pre + "row_max", [P, G, XH])
    row_sum, row_inv = sb(pre + "row_sum", [P, G, XH]), sb(pre + "row_inv", [P, G, XH])
    probsT = sb(pre + "probsT", [P, 2, HC, P])
    heads_outT = sb(pre + "heads_outT", [P, 2, P])
    own_head = c.w["own_head"][:, :].unsqueeze(2).broadcast_to([P, HC, SC])
    score_banks = c.psum[:, 0:4, 0:HC * SC].rearrange("p q (m t) -> p q m t", m=HC)
    ring_bank = [bank(4), bank(5)]
    pv_bank = bank(6)

    ring_done, ring_free = sem(pre + "ring_done"), sem(pre + "ring_free")
    q_copied, keys_done, v_spread_done = sem(pre + "q_copied"), sem(pre + "keys_done"), sem(pre + "v_spread_done")
    scores_done, shift_done = sem(pre + "scores_done"), sem(pre + "shift_done")
    probs_done, pv_done = sem(pre + "probs_done"), sem(pre + "pv_done")
    normed, sum_inverted = sem(pre + "normed"), sem(pre + "sum_inverted")
    outT_copied, out_done = sem(pre + "outT_copied"), sem(pre + "out_done")
    zeros_set, mask_ready = sem(pre + "zeros_set"), sem(pre + "mask_ready")
    if tempered:
        SCALE = XD ** -0.5
        qT = sb(pre + "qT", [P, W])
        exp1 = sb(pre + "exp1", [P, 2, 2, XH, SC])
        sum1, sum2 = sb(pre + "sum1", [P, G, XH]), sb(pre + "sum2", [P, G, XH])
        inv1 = sb(pre + "inv1", [P, G, XH])
        ksum, qsum, qk_sum = sb(pre + "ksum", [P, G]), sb(pre + "qsum", [P, G]), sb(pre + "qk_sum", [P, G])
        qk_heads = sb(pre + "qk_heads", [P, G, XH])
        feats = sb(pre + "feats", [3, G * XH])
        hidden1, hidden2 = sb(pre + "hidden1", [64, G * XH]), sb(pre + "hidden2", [64, G * XH])
        log_t, clip_t = sb(pre + "log_t", [P, G * XH]), sb(pre + "clip_t", [P, G * XH])
        inv_t = sb(pre + "inv_t", [P, G, XH])
        exp1_done, sums_done = sem(pre + "exp1_done"), sem(pre + "sums_done")
        feats_ready, clipped = sem(pre + "feats_ready"), sem(pre + "clipped")
        inv_t_ready, scaled = sem(pre + "inv_t_ready"), sem(pre + "scaled")
        v_bias = w["bv"]
    else:
        SCALE = float(P) ** -0.5
        mask_int = sb(pre + "mask_int", [P, B * SC], I32)
        key_bias = sb(pre + "key_bias", [P, B, SC], BF16)
        w_qk = sb(pre + "w_qk", [P, P])
        v_bias = sb(pre + "v_bias", [P, P])
        mask_loaded, w_qk_done, w_qk_copied = sem(pre + "mask_loaded"), sem(pre + "w_qk_done"), sem(pre + "w_qk_copied")

    def middle_entries(front, back):
        entries = []
        for t in range(T + 3):
            if tempered and front and 0 <= t - MLP_AT < 4:
                entries.append(f"mlp{t - MLP_AT}")
            if back and t < T:
                entries.append(f"chunk{t}")
        return entries

    def run(fori, ahead, middle):
        ahead(0, None, None, 0)
        middle(0, None, NA)
        ahead(1, 0, None, NA + NM)
        start, step = 2 * NA + NM, T + NM + NA
        with fori(0, NG - 2) as r:
            middle(r + 1, r, start + r * step)
            ahead(r + 2, r + 1, r, start + r * step + (T + NM))
        start = start + (NG - 2) * step
        middle(NG - 1, NG - 2, start)
        ahead(None, NG - 1, NG - 2, None)
        middle(None, NG - 1, start + T + NM)
        ahead(None, None, NG - 1, None)

    with nc.Block() as block:
        @block.sync
        def _(sp):
            if not tempered:
                sp.dma_start(mask_int[:, :], c.dram["mask"]).then_inc(mask_loaded, 16)
            sp_stage_ahead(c, sp)

        @block.gpsimd
        def _(pool):
            def spread_keys(g, j):
                if j == 0:
                    pool.wait_ge(ring_free, k_free[0])
                pool.wait_ge(scores_done, g * G + (j + 1))
                pool.tensor_tensor(keys[:, j, :, :], k_sb[:, j, :].unsqueeze(1).broadcast_to([P, HC, SC]),
                                   own_head, ALU.mult).then_inc(keys_done, 1)

            def spread_values(g, j):
                block = v_spread[0:SC, j, :, :]
                own = bass.AP(block.tensor, block.offset, [block.ap[0], [HC * QF, NC], [QF + XD, HC], [1, XD]])
                src = v_sb[0:SC, j * P:(j + 1) * P].rearrange("p (q m d) -> p q m d", q=NC, m=HC)
                pool.wait_ge(pv_done, (g * G + (j + 1)) * NC)
                pool.tensor_tensor(own, src, v_bias[0:SC, :].rearrange("p (q m d) -> p q m d", q=NC, m=HC),
                                   ALU.add).then_inc(v_spread_done, 1)

            def scale(b, j):
                if j == 0:
                    pool.wait_ge(inv_t_ready, b + 1)
                pool.wait_ge(pv_done, (b * G + (j + 1)) * NC)
                pool.tensor_tensor(probs[:, j, :, :], raw[:, j, :, :],
                                   inv_t[:, j, :].unsqueeze(2).broadcast_to([P, XH, SC]),
                                   ALU.mult).then_inc(scaled, 1)

            def normalise(b, j):
                pool.wait_ge(sum_inverted, b * G + (j + 1))
                inverse = row_inv[:, j, :].unsqueeze(2).broadcast_to([P, XH, SC])
                pool.tensor_tensor(probs[:, j, :, :], probs[:, j, :, :], inverse, ALU.mult).then_inc(normed, 1)

            k_free = [None]

            def ahead(g, b, tail, base):
                if g is not None:
                    k_free[0] = base + (A_ENTRIES.index("v") + 2)
                    for j in range(G):
                        spread_keys(g, j)
                if tail is not None:
                    tail_pool(c, pool, tail + n0)
                if b is not None:
                    if tempered:
                        scale(b, 0)
                        scale(b, 1)
                    normalise(b, 0)

            def middle(g, b, base):
                if b is not None:
                    for j in range(1, G):
                        if tempered and j + 1 < G:
                            scale(b, j + 1)
                        normalise(b, j)
                if g is not None:
                    pool.wait_ge(ring_free, base + 2)
                    for j in range(G):
                        spread_values(g, j)

            ones_credit(pool, [(keys_done, 1), (v_spread_done, 1)])
            pool.memset(v_spread[:], 0.0)
            if not tempered:
                pool.memset(v_bias[:], 0.0)
            pool.memset(q_quad[:], 0.0)
            pool.memset(probsT[:], 0.0).then_inc(zeros_set, 1)
            pool.drain()
            run(pool.Fori, ahead, middle)

        @block.tensor
        def _(pe):
            def entry(number):
                pe.wait_ge(ring_free, number + 1)

            def scores(g, j, base_q):
                if j == 0:
                    if tempered:
                        pe.wait_ge(ring_free, base_q + 3)
                    else:
                        pe.wait_ge(q_copied, g + 1)
                pe.wait_ge(keys_done, g * G + (j + 2))
                pe.wait_ge(shift_done, g * G + (j + 1))
                for q in range(NC):
                    out = score_banks[:, q, :, :]
                    if not tempered:
                        bias = key_bias[:, bass.ds(g * G + j, 1), :].broadcast_to([P, HC, SC])
                        pe.matmul(out, c.ident16[:, :], bias, start=True, stop=False)
                    last = pe.matmul(out, q_quad[:, q, j * P:(j + 1) * P], keys[:, j, :, :],
                                     start=tempered, stop=True)
                    if j == 0 and q == 0:
                        last.then_inc(c.xTs_used, 1)
                last.then_inc(scores_done, 1)

            def project(g, base):
                pe.wait_ge(c.xTs_loaded, (g + n0 + 1) * 16)
                pe.wait_ge(c.ctx_loaded, (g + c.ctx0 + 1) * 16)
                for i, name in enumerate(A_ENTRIES):
                    entry(base + i)
                    out = ring_bank[i % 2]
                    if name == "q":
                        last = pe.matmul(out[:, :], w["wq"][:, :], c.xTs[:, :], start=True, stop=True)
                    elif name == "v":
                        for j in range(G):
                            last = pe.matmul(out[0:SC, j * P:(j + 1) * P], c.ctxTs[:, j * SC:(j + 1) * SC],
                                             w["wv"][:, :], start=True, stop=True)
                    else:
                        n = G * SC // k_parts
                        part = int(name[1]) * n
                        last = pe.matmul(out[:, 0:n], w["wk"][:, :] if tempered else w_qk[:, :],
                                         c.ctxTs[:, part:part + n], start=True, stop=True)
                    last.then_inc(ring_done, 1)

            def ahead(g, b, tail, base):
                if g is not None:
                    project(g, base)
                    scores(g, 0, base)
                if tail is not None:
                    tail_pe(c, pe, tail + n0, c.y_bank)

            def temperature_layer(g, k, base, order):
                entry(base + order.index(f"mlp{k}"))
                out = ring_bank[order.index(f"mlp{k}") % 2]
                if k == 0:
                    pe.wait_ge(feats_ready, g + 1)
                    for f, stat in enumerate((qk_heads, row_max, sum2)):
                        last = pe.matmul(out[0:3, 0:G * XH], w["select"][:, f, :],
                                         stat[:, :, :].rearrange("p j h -> p (j h)"), start=(f == 0), stop=(f == 2))
                else:
                    pe.wait_ge(ring_free, base + order.index(f"mlp{k - 1}") + 3)
                    rows, weight, source = ((64, w["w1"], feats), (P, w["w2"], hidden1), (P, w["w3"], hidden2))[k - 1]
                    last = pe.matmul(out[0:rows, 0:G * XH], weight[:, :], source[:, :], start=True, stop=True)
                last.then_inc(ring_done, 1)

            def transpose_chunk(b, u, base, order):
                j, k = u // NC, u % NC
                number = order.index(f"chunk{u}")
                if k == 0:
                    pe.wait_ge(normed, b * G + (j + 1))
                entry(base + number)
                for m in range(HC):
                    last = pe.transpose(ring_bank[number % 2][0:SC, m * P:(m + 1) * P], probs[:, j, k * HC + m, :],
                                        c.w["ident"][:, :])
                last.then_inc(ring_done, 1)

            def times_v(b, u, base, order):
                j, k = u // NC, u % NC
                if k == 0:
                    pe.wait_ge(v_spread_done, b * G + (j + 2))
                    pe.wait_ge(outT_copied, b * G + (j + 1))
                pe.wait_ge(ring_free, base + (order.index(f"chunk{u}") + 3))
                for m in range(HC):
                    last = pe.matmul(pv_bank[k * QF:(k + 1) * QF, 0:P], v_spread[:, j, k * HC + m, :],
                                     probsT[:, u % 2, m, :], start=(m == 0), stop=(m == HC - 1))
                last.then_inc(pv_done, 1)

            def project_out(b, j):
                pe.wait_ge(outT_copied, b * G + (j + 2))
                if j == 0:
                    pe.wait_ge(c.resid_done, b + n0 + 1)
                    if not c.last:
                        pe.wait_ge(c.yT_copied, b + n0 + 1)
                y = c.y_bank[:, j * P:(j + 1) * P]
                pe.matmul(y, heads_outT[:, j % 2, :], w["wo"][:, :], start=True, stop=False)
                pe.matmul(y, c.w["ones_row"][:, :], w["bo"][:, :], start=False, stop=True).then_inc(out_done, 1)

            def middle(g, b, base):
                order = middle_entries(g is not None, b is not None)
                for t in range(T + 3):
                    if g is not None and t in SCORES_AT:
                        scores(g, SCORES_AT.index(t), None)
                    if f"mlp{t - MLP_AT}" in order:
                        temperature_layer(g, t - MLP_AT, base, order)
                    if b is not None:
                        if t < T:
                            transpose_chunk(b, t, base, order)
                        if 1 <= t <= T:
                            times_v(b, t - 1, base, order)
                        if t >= 6 and (t - 6) % NC == 0:
                            project_out(b, (t - 6) // NC)

            pe.wait_ge(zeros_set, 1)
            if not tempered:
                pe.matmul(pv_bank[:, 0:P], w["wk"][:, :], w["wq"][:, :], start=True, stop=True).then_inc(w_qk_done, 1)
                pe.wait_ge(w_qk_copied, 1)
                pe.wait_ge(mask_ready, 1)
            run(pe.Fori, ahead, middle)

        @block.scalar
        def _(act):
            def first_exp(g, j):
                act.wait_ge(shift_done, g * G + (j + 2))
                act.wait_ge(sums_done, g * G + (j + 1))
                for power in (1, 2):
                    act.activation(exp1[:, j % 2, power - 1, :, :], raw[:, j, :, :], ACT.Exp,
                                   scale=power * SCALE).then_inc(exp1_done, 1)

            def exp(b, j):
                if tempered:
                    act.wait_ge(scaled, b * G + (j + 5))
                    act.activation(probs[:, j, :, :], probs[:, j, :, :], ACT.Exp, scale=0.5).then_inc(probs_done, 1)
                else:
                    act.wait_ge(shift_done, b * G + (j + 2))
                    act.wait_ge(pv_done, (b * G + (j + 1)) * NC)
                    act.activation(probs[:, j, :, :], raw[:, j, :, :], ACT.Exp, scale=SCALE).then_inc(probs_done, 1)

            def copy_queries(g, source, base):
                act.wait_ge(scores_done, g * G + 4)
                bias = w["bq"] if tempered else None
                for q in range(NC):
                    rows = slice(q * QF, (q + 1) * QF)
                    last = act.activation(q_quad[rows, q, :], source[rows, :], ACT.Identity,
                                          bias=bias[rows, 0:1] if tempered else 0.0)
                return last

            def ahead(g, b, tail, base):
                if g is not None:
                    if not tempered:
                        act.wait_ge(c.xTs_loaded, (g + n0 + 1) * 16)
                        copy_queries(g, c.xTs, base).then_inc(q_copied, 1)
                    for i, name in enumerate(A_ENTRIES):
                        src = ring_bank[i % 2]
                        act.wait_ge(ring_done, base + (i + 1))
                        if name == "q":
                            act.activation(qT[:, :], src[:, :], ACT.Identity, bias=w["bq"][:, 0:1])
                            last = copy_queries(g, src, base)
                        elif name == "v":
                            act.wait_ge(v_spread_done, g * G + 1)
                            last = act.activation(v_sb[0:SC, :], src[0:SC, :], ACT.Copy)
                        else:
                            act.wait_ge(keys_done, g * G + 1)
                            js = G // k_parts
                            part = int(name[1]) * js
                            last = act.activation(
                                k_sb[:, part:part + js, :], src[:, 0:js * SC].rearrange("p (j t) -> p j t", j=js),
                                ACT.Identity, bias=w["bk"][:, 0:1] if tempered else 0.0)
                        last.then_inc(ring_free, 1)
                if b is not None:
                    exp(b, 0)
                    exp(b, 1)
                if g is not None and tempered:
                    first_exp(g, 0)
                if tail is not None:
                    tail_act(c, act, tail + n0, c.y_bank)

            def temperature_layer(g, k, base, order):
                number = order.index(f"mlp{k}")
                src = ring_bank[number % 2]
                act.wait_ge(ring_done, base + (number + 1))
                out, rows, func, bias = ((feats, 3, ACT.Identity, w["feat_bias"]), (hidden1, 64, ACT.Gelu, w["b1"]),
                                         (hidden2, 64, ACT.Gelu, w["b2"]), (log_t, P, ACT.Identity, w["b3"]))[k]
                act.activation(out[:, :], src[0:rows, 0:G * XH], func, bias=bias[:, 0:1]).then_inc(ring_free, 1)
                if k == 3:
                    act.wait_ge(clipped, g + 1)
                    act.wait_ge(scaled, g * G + 4)
                    act.activation(inv_t[:, :, :].rearrange("p j h -> p (j h)"), clip_t[:, :], ACT.Exp, scale=-1.0)\
                        .then_inc(inv_t_ready, 1)

            def copy_chunk(b, u, base, order):
                number = order.index(f"chunk{u}")
                act.wait_ge(ring_done, base + (number + 1))
                act.wait_ge(pv_done, b * T + (u - 1 + T))
                act.activation(probsT[0:SC, u % 2, :, :],
                               ring_bank[number % 2][0:SC, :].rearrange("p (m t) -> p m t", m=HC), ACT.Copy)\
                    .then_inc(ring_free, 1)

            def copy_outT(b, j):
                act.wait_ge(pv_done, (b * G + j) * NC + (NC + T))
                act.wait_ge(out_done, b * G + (j + 1))
                act.activation(heads_outT[:, j % 2, :], pv_bank[:, 0:P], ACT.Copy).then_inc(outT_copied, 1)

            def middle(g, b, base):
                order = middle_entries(g is not None, b is not None)
                for t in range(T + 3):
                    if f"mlp{t - MLP_AT}" in order:
                        temperature_layer(g, t - MLP_AT, base, order)
                    if b is not None:
                        if t < T:
                            copy_chunk(b, t, base, order)
                        if t % NC == 1 and t // NC + 2 < G:
                            exp(b, t // NC + 2)
                        if t >= 5 and (t - 5) % NC == 0:
                            copy_outT(b, (t - 5) // NC)
                    if g is not None and tempered and t - 2 in SCORES_AT:
                        first_exp(g, SCORES_AT.index(t - 2))

            ones_credit(act, [(ring_free, 2), (outT_copied, 1), (probs_done, 4)])
            act.wait_ge(zeros_set, 1)
            if not tempered:
                act.wait_ge(w_qk_done, 1)
                act.activation(w_qk[:, :], pv_bank[:, 0:P], ACT.Copy).then_inc(w_qk_copied, 1)
            run(act.Fori, ahead, middle)

        @block.vector
        def _(dve):
            def shift(g, j):
                dve.wait_ge(scores_done, g * G + (j + 5))
                dve.wait_ge(scaled if tempered else probs_done, g * G + (j + 1))
                dve.tensor_reduce(row_max[:, j, :].rearrange("p (q m) -> p q m", q=NC), score_banks, X, ALU.max)
                dve.drain()
                dve.tensor_tensor(raw[:, j, :, :].rearrange("p (q m) t -> p q m t", q=NC), score_banks,
                                  row_max[:, j, :].rearrange("p (q m) -> p q m", q=NC).unsqueeze(3)
                                  .broadcast_to([P, NC, HC, SC]), ALU.subtract).then_inc(shift_done, 1)

            def sums(g, j):
                dve.wait_ge(exp1_done, (g * G + j) * 2 + 2)
                dve.tensor_reduce(sum1[:, j, :], exp1[:, j % 2, 0, :, :], X, ALU.add)
                dve.tensor_reduce(sum2[:, j, :], exp1[:, j % 2, 1, :, :], X, ALU.add).then_inc(sums_done, 1)

            def statistics(g):
                dve.tensor_reduce(qsum[:, :], qT[:, :].rearrange("p (j t) -> p j t", j=G), X, ALU.add)
                dve.tensor_reduce(ksum[:, :], k_sb[:, :, :], X, ALU.add)
                dve.drain()
                dve.reciprocal(inv1[:, :, :], sum1[:, :, :])
                dve.tensor_tensor(qk_sum[:, :], ksum[:, :], qsum[:, :], ALU.mult)
                dve.drain()
                dve.tensor_tensor(sum2[:, :, :], sum2[:, :, :], inv1[:, :, :], ALU.mult)
                dve.tensor_tensor(qk_heads[:, :, :], qk_sum[:, :].unsqueeze(2).broadcast_to([P, G, XH]),
                                  c.w["head_of"][:, :].unsqueeze(1).broadcast_to([P, G, XH]), ALU.mult)
                dve.drain()
                dve.tensor_tensor(sum2[:, :, :], sum2[:, :, :], inv1[:, :, :], ALU.mult).then_inc(feats_ready, 1)

            def clip(g, log_t_free):
                dve.wait_ge(ring_free, log_t_free)
                dve.tensor_scalar(clip_t[:, :], log_t[:, :], LOG_T_MIN, LOG_T_MAX, ALU.max, ALU.min)\
                    .then_inc(clipped, 1)

            def invert_sum(b, j):
                dve.wait_ge(probs_done, b * G + (j + 5))
                dve.tensor_reduce(row_sum[:, j, :], probs[:, j, :, :], X, ALU.add)
                dve.drain()
                dve.reciprocal(row_inv[:, j, :], row_sum[:, j, :]).then_inc(sum_inverted, 1)

            def ahead(g, b, tail, base):
                if tail is not None:
                    dve.wait_ge(out_done, tail * G + (G + 2))
                    tail_dve_variance(c, dve, tail + n0)
                if g is not None:
                    shift(g, 0)
                if tail is not None:
                    tail_dve_norm(c, dve, tail + n0)
                if b is not None:
                    invert_sum(b, 0)
                    invert_sum(b, 1)

            def middle(g, b, base):
                order = middle_entries(g is not None, b is not None)
                for j in range(G):
                    if g is not None and j + 1 < G:
                        shift(g, j + 1)
                    if b is not None and j + 2 < G:
                        invert_sum(b, j + 2)
                    if g is not None and tempered:
                        sums(g, j)
                if g is not None and tempered:
                    statistics(g)
                    clip(g, base + (order.index("mlp3") + 3))

            ones_credit(dve, [(scores_done, 4), (shift_done, 1), (pv_done, T), (out_done, 2)])
            if tempered:
                ones_credit(dve, [(sums_done, 2), (scaled, 4)])
            else:
                dve.wait_ge(mask_loaded, 16)
                dve.tensor_scalar(key_bias[:, :, :].rearrange("p b t -> p (b t)"), mask_int[:, :], 0, -1e20,
                                  ALU.is_equal, ALU.mult).then_inc(mask_ready, 1)
            run(dve.Fori, ahead, middle)
    memory.close()



class Router:

    def __init__(self, c, sb, sem, pre, weight):
        self.c, self.weight = c, weight
        self.shifted, self.probs = sb(pre + "r_shifted", [P, G, E]), sb(pre + "r_probs", [P, G, E])
        self.rank, self.chosen = sb(pre + "r_rank", [P, G, E]), sb(pre + "r_chosen", [P, G, E])
        self.w = sb(pre + "r_w", [P, G, E])
        self.best, self.total, self.inverse = (sb(pre + "r_" + x, [P, G]) for x in ("best", "total", "inverse"))
        self.above, self.equal = sb(pre + "r_above", [P, G, E, E]), sb(pre + "r_equal", [P, G, E, E])
        self.logits_done, self.shift_done = sem(pre + "logits_done"), sem(pre + "r_shift_done")
        self.exp_done, self.routed = sem(pre + "r_exp_done"), sem(pre + "routed")

    def pe(self, pe, g, bank):
        for j in range(G):
            last = pe.matmul(bank[:, j * E:(j + 1) * E], self.c.xTs[:, j * P:(j + 1) * P], self.weight[:, :],
                             start=True, stop=True)
        last.then_inc(self.logits_done, 1)

    def act(self, act, g):
        act.wait_ge(self.shift_done, g + 1)
        act.activation(self.probs[:, :, :], self.shifted[:, :, :], ACT.Exp).then_inc(self.exp_done, 1)

    def dve(self, dve, g, bank):
        dve.wait_ge(self.logits_done, g + 1)
        logits = bank[:, 0:G * E].rearrange("p (j e) -> p j e", j=G)
        wide = [P, G, E]
        dve.tensor_reduce(self.best[:, :], logits, X, ALU.max)
        dve.drain()
        dve.tensor_tensor(self.shifted[:, :, :], logits, self.best[:, :].unsqueeze(2).broadcast_to(wide),
                          ALU.subtract).then_inc(self.shift_done, 1)
        dve.wait_ge(self.exp_done, g + 1)
        dve.tensor_reduce(self.total[:, :], self.probs[:, :, :], X, ALU.add)
        dve.drain()
        dve.reciprocal(self.inverse[:, :], self.total[:, :])
        dve.drain()
        dve.tensor_tensor(self.probs[:, :, :], self.probs[:, :, :],
                          self.inverse[:, :].unsqueeze(2).broadcast_to(wide), ALU.mult)
        dve.drain()
        other = self.probs[:, :, :].unsqueeze(2).broadcast_to([P, G, E, E])
        own = self.probs[:, :, :].unsqueeze(3).broadcast_to([P, G, E, E])
        dve.tensor_tensor(self.above[:, :, :, :], other, own, ALU.is_gt)
        dve.tensor_tensor(self.equal[:, :, :, :], other, own, ALU.is_equal)
        dve.drain()
        dve.tensor_tensor(self.equal[:, :, :, :], self.equal[:, :, :, :],
                          self.c.w["earlier"][:, :, :].unsqueeze(1).broadcast_to([P, G, E, E]), ALU.mult)
        dve.drain()
        dve.tensor_tensor(self.above[:, :, :, :], self.above[:, :, :, :], self.equal[:, :, :, :], ALU.add)
        dve.drain()
        dve.tensor_reduce(self.rank[:, :, :], self.above[:, :, :, :], X, ALU.add)
        dve.drain()
        dve.tensor_scalar(self.chosen[:, :, :], self.rank[:, :, :], 1.5, None, ALU.is_lt)
        dve.drain()


def broadcast_weight(c, pe, out, router, e):
    for j in range(G):
        last = pe.matmul(out[:, j * P:(j + 1) * P], router.w[:, j, e:e + 1].broadcast_to([P, P]),
                         c.w["ident"][:, :], start=True, stop=True)
    return last



def linear_experts(c, nc, stage):
    n0 = c.n0
    sem, bank = c.sem, c.bank
    memory = ExitStack()
    sb = stage_memory(nc, memory)
    R = 4
    router = Router(c, sb, sem, "e_", c.w["e_router"])
    scaled = sb("e_scaled", [P, R, W])
    top_sum = sb("e_top_sum", [P, G])
    probs_w, bias = sb("e_probs_w", [P, G, E]), sb("e_bias", [P, G])
    w_done, scaled_done, used = sem("e_w_done"), sem("e_scaled_done"), sem("e_used")
    w_bank = [bank(1), bank(2)]

    with nc.Block() as block:
        @block.sync
        def _(sp):
            sp_stage(c, sp)

        @block.gpsimd
        def _(pool):
            with pool.Fori(0, NG) as g:
                tail_pool(c, pool, g + n0)

        @block.tensor
        def _(pe):
            with pe.Fori(0, NG) as g:
                pe.wait_ge(c.xTs_loaded, (g + n0 + 1) * 16)
                router.pe(pe, g, bank(0))
                pe.wait_ge(c.resid_done, g + n0 + 1)
                pe.matmul(c.y_bank[:, :], c.ident16[:, :], c.zeros16[:, :], start=True, stop=False)
                pe.wait_ge(router.routed, g + 1)
                for s in range(E + 2):
                    if s < E:
                        pe.wait_ge(scaled_done, g * E + (s + 1))
                        broadcast_weight(c, pe, w_bank[s % 2], router, s).then_inc(w_done, 1)
                    if s >= 2:
                        e = s - 2
                        pe.wait_ge(scaled_done, g * E + (e + 3))
                        for j in range(G):
                            last = pe.matmul(c.y_bank[:, j * P:(j + 1) * P], scaled[:, e % R, j * P:(j + 1) * P],
                                             c.w["e_experts"][:, e, :], start=False,
                                             stop=(e == E - 1 and j == G - 1))
                            if e == E - 1 and j == 0:
                                last.then_inc(c.xTs_used, 1)
                        last.then_inc(used, 1)
                tail_pe(c, pe, g + n0, bank(3))

        @block.scalar
        def _(act):
            with act.Fori(0, NG) as g:
                router.act(act, g)
                tail_act(c, act, g + n0, bank(3))

        @block.vector
        def _(dve):
            ones_credit(dve, [(scaled_done, 2), (used, R)])
            with dve.Fori(0, NG) as g:
                wide = [P, G, E]
                router.dve(dve, g, bank(0))
                dve.tensor_tensor(router.w[:, :, :], router.probs[:, :, :], router.chosen[:, :, :], ALU.mult)
                dve.drain()
                dve.tensor_reduce(top_sum[:, :], router.w[:, :, :], X, ALU.add)
                dve.drain()
                dve.tensor_scalar(top_sum[:, :], top_sum[:, :], 1e-6, None, ALU.add)
                dve.drain()
                dve.reciprocal(router.inverse[:, :], top_sum[:, :])
                dve.drain()
                dve.tensor_tensor(router.w[:, :, :], router.w[:, :, :],
                                  router.inverse[:, :].unsqueeze(2).broadcast_to(wide), ALU.mult)\
                    .then_inc(router.routed, 1)
                dve.drain()
                dve.tensor_tensor(probs_w[:, :, :], router.probs[:, :, :], router.w[:, :, :], ALU.mult)
                for e in range(E):
                    dve.wait_ge(w_done, g * E + (e + 1))
                    dve.wait_ge(used, g * E + (e + 1))
                    if e == 0:
                        dve.wait_ge(c.xTs_loaded, (g + n0 + 1) * 16)
                    dve.tensor_tensor(scaled[:, e % R, :], w_bank[e % 2][:, :], c.xTs[:, :], ALU.mult)\
                        .then_inc(scaled_done, 1)
                dve.tensor_reduce(bias[:, :], probs_w[:, :, :], X, ALU.add)
                dve.drain()
                dve.wait_ge(c.xs_loaded, (g + n0 + 1) * 16)
                for j in range(G):
                    dve.tensor_scalar(c.xs[:, j, :], c.xs[:, j, :], bias[:, j:j + 1], None, ALU.add)
                dve.drain()
                dve.wait_ge(used, g * E + (E + R))
                tail_dve(c, dve, g + n0)
    memory.close()



def gated_experts(c, nc, stage):
    n0 = c.n0
    sem, bank = c.sem, c.bank
    memory = ExitStack()
    sb = stage_memory(nc, memory)
    NSH = 2
    NI = NSH + E
    router = Router(c, sb, sem, "f_", c.w["f_router"])
    scaled = sb("f_scaled", [P, 2, W])
    hidden = sb("f_hidden", [P, 2, W])
    gate = sb("f_gate", [P, 2, W])
    product = sb("f_product", [P, 2, W])
    w_done, scaled_done = sem("f_w_done"), sem("f_scaled_done")
    h_done, gate_done, hidden_done = sem("f_h_done"), sem("f_gate_done"), sem("f_hidden_done")
    gate_copied, masked, out_done = sem("f_gate_copied"), sem("f_masked"), sem("f_out_done")
    product_done, summed = sem("f_product_done"), sem("f_summed")
    router_bank, out_bank = bank(0), bank(5)
    w_bank, h_bank, gate_bank = [bank(1), bank(2)], [bank(3), bank(6)], [bank(4), bank(0)]

    with nc.Block() as block:
        @block.sync
        def _(sp):
            sp_stage(c, sp)

        @block.gpsimd
        def _(pool):
            with pool.Fori(0, NG) as g:
                tail_pool(c, pool, g + n0)

        @block.tensor
        def _(pe):
            def weight(g, s):
                e = s - NSH
                if e == 0:
                    pe.wait_ge(router.routed, g + 1)
                pe.wait_ge(masked, g * E + (e + 1))
                broadcast_weight(c, pe, w_bank[e % 2], router, e).then_inc(w_done, 1)

            def inner(g, s):
                n = g * NI + s
                if s < NSH:
                    rhs, w_h, w_gate = c.xTs[:, :], c.w["f_sw1"][:, s, :], c.w["f_sw2"][:, s, :]
                else:
                    e = s - NSH
                    rhs, w_h, w_gate = scaled[:, e % 2, :], c.w["f_w1"][:, e, :], c.w["f_w3"][:, e, :]
                    pe.wait_ge(scaled_done, g * E + (e + 1))
                pe.wait_ge(hidden_done, n + 1)
                pe.matmul(h_bank[s % 2][:, :], w_h, rhs, start=True, stop=True).then_inc(h_done, 1)
                pe.wait_ge(product_done, n + 1)
                pe.matmul(gate_bank[s % 2][:, :], w_gate, rhs, start=True, stop=True).then_inc(gate_done, 1)

            def outer(g, s):
                n = g * NI + s
                pe.wait_ge(hidden_done, n + 3)
                pe.wait_ge(product_done, n + 2)
                pe.matmul(out_bank[:, :], c.w["f_w2"][:, s - NSH, :], hidden[:, s % 2, :],
                          start=True, stop=True).then_inc(out_done, 1)

            def accumulate(g, s):
                n = g * NI + s
                pe.wait_ge(product_done, n + 3)
                if s == 0:
                    pe.wait_ge(c.resid_done, g + n0 + 1)
                    pe.matmul(c.y_bank[:, :], c.ident16[:, :], c.zeros16[:, :], start=True, stop=False)
                rhs = c.w["f_sw3"][:, s, :] if s < NSH else c.w["ident"][:, :]
                for j in range(G):
                    last = pe.matmul(c.y_bank[:, j * P:(j + 1) * P], product[:, s % 2, j * P:(j + 1) * P], rhs,
                                     start=False, stop=(s == NI - 1 and j == G - 1))
                    if s == NI - 2 and j == 0:
                        last.then_inc(c.xTs_used, 1)
                last.then_inc(summed, 1)

            with pe.Fori(0, NG) as g:
                pe.wait_ge(c.xTs_loaded, (g + n0 + 1) * 16)
                pe.wait_ge(product_done, g * NI + 2)
                router.pe(pe, g, router_bank)
                for s in range(NI + 2):
                    if s < NI:
                        if s == 1:
                            pe.wait_ge(router.shift_done, g + 1)
                        inner(g, s)
                    if NSH <= s + 1 < NI:
                        weight(g, s + 1)
                    if NSH <= s - 1 < NI:
                        outer(g, s - 1)
                    if s >= 2:
                        accumulate(g, s - 2)
                if not c.last:
                    tail_pe(c, pe, g + n0, out_bank)

        @block.scalar
        def _(act):
            ones_credit(act, [(hidden_done, 2)])
            with act.Fori(0, NG) as g:
                router.act(act, g)
                for s in range(NI):
                    n = g * NI + s
                    act.wait_ge(h_done, n + 1)
                    act.wait_ge(product_done, n + 1)
                    bias = c.w["f_b1"][:, s - NSH:s - NSH + 1] if s >= NSH else 0.0
                    act.activation(hidden[:, s % 2, :], h_bank[s % 2][:, :], ACT.Silu, bias=bias)\
                        .then_inc(hidden_done, 1)
                    if s >= NSH:
                        act.wait_ge(gate_done, n + 3)
                        act.activation(gate[:, s % 2, :], gate_bank[s % 2][:, :], ACT.Identity,
                                       bias=c.w["f_b3"][:, s - NSH:s - NSH + 1]).then_inc(gate_copied, 1)
                tail_act(c, act, g + n0, out_bank)

        @block.vector
        def _(dve):
            def scale(g, s):
                e = s - NSH
                dve.wait_ge(w_done, g * E + (e + 1))
                dve.wait_ge(gate_done, g * NI + (s + 1))
                dve.scalar_tensor_tensor(scaled[:, e % 2, :], w_bank[e % 2][:, :], 0.0, c.xTs[:, :],
                                         ALU.max, ALU.mult).then_inc(scaled_done, 1)

            def mask(g, s):
                e = s - NSH
                dve.wait_ge(gate_copied, g * E + (e + 1))
                dve.scalar_tensor_tensor(gate[:, s % 2, :], w_bank[e % 2][:, :], 0.0, gate[:, s % 2, :],
                                         ALU.is_ge, ALU.mult).then_inc(masked, 1)

            def multiply(g, s):
                n = g * NI + s
                if s < NSH:
                    dve.wait_ge(hidden_done, n + 3)
                    dve.wait_ge(gate_done, n + 3)
                    dve.wait_ge(summed, n + 1)
                    dve.tensor_tensor(product[:, s % 2, :], gate_bank[s % 2][:, :], hidden[:, s % 2, :],
                                      ALU.mult).then_inc(product_done, 1)
                    return
                e = s - NSH
                dve.wait_ge(masked, g * E + (e + 3))
                dve.wait_ge(out_done, g * E + (e + 1))
                dve.wait_ge(summed, n + 1)
                dve.scalar_tensor_tensor(product[:, s % 2, :], out_bank[:, :], c.w["f_b2"][:, e:e + 1],
                                         gate[:, s % 2, :], ALU.add, ALU.mult).then_inc(product_done, 1)

            ones_credit(dve, [(gate_done, 2), (masked, 2), (product_done, 2), (summed, 2)])
            with dve.Fori(0, NG) as g:
                router.dve(dve, g, router_bank)
                dve.tensor_tensor(router.w[:, :, :], router.probs[:, :, :], router.chosen[:, :, :], ALU.mult)
                dve.drain()
                dve.scalar_tensor_tensor(router.w[:, :, :], router.chosen[:, :, :], -1.0, router.w[:, :, :],
                                         ALU.add, ALU.add).then_inc(router.routed, 1)
                for s in range(NI + 1):
                    if s > NSH:
                        mask(g, s - 1)
                    if NSH <= s + 1 < NI:
                        scale(g, s + 1)
                    if s >= 1:
                        multiply(g, s - 1)
                dve.wait_ge(summed, g * NI + (NI + 2))
                tail_dve(c, dve, g + n0)
    memory.close()



def mamba(c, nc, stage):
    n0 = c.n0
    sem, bank = c.sem, c.bank
    memory = ExitStack()
    sb = stage_memory(nc, memory)
    TD = DI // P
    U = NS * TD
    R = 4
    L = P + 1
    padded = sb("m_padded", [P, TD, G, P + KC - 1])
    conv = sb("m_conv", [P, TD, W])
    u = sb("m_u", [P, TD, W])
    gate = sb("m_gate", [P, TD, W])
    x_dbl = sb("m_x_dbl", [P, W])
    exp_v, one_plus, lost = sb("m_exp_v", [P, TD, W]), sb("m_one_plus", [P, TD, W]), sb("m_lost", [P, TD, W])
    delta, log_part, du = sb("m_delta", [P, TD, W]), sb("m_log", [P, TD, W]), sb("m_du", [P, TD, W])
    minus_a = sb("m_minus_a", [P, TD, NS])
    decay, drive = sb("m_decay", [P, R, G * L]), sb("m_drive", [P, R, G * L])
    state = sb("m_state", [P, R, G * L])
    c_wide = sb("m_c_wide", [P, 2, W])
    read = sb("m_read", [P, R, W])
    y = sb("m_y", [P, TD, W])

    zeros_set, a_exp, a_ready = sem("m_zeros_set"), sem("m_a_exp"), sem("m_a_ready")
    in_done, in_copied, conv_done = sem("m_in_done"), sem("m_in_copied"), sem("m_conv_done")
    u_done, dbl_done, dbl_copied, dt_done = sem("m_u_done"), sem("m_dbl_done"), sem("m_dbl_copied"), sem("m_dt_done")
    exp_v_done, one_plus_done, log_done = sem("m_exp_v_done"), sem("m_one_plus_done"), sem("m_log_done")
    delta_done, abs_done = sem("m_delta_done"), sem("m_abs_done")
    b_done, c_done, c_copied = sem("m_b_done"), sem("m_c_done"), sem("m_c_copied")
    decay_done, drive_done, scanned = sem("m_decay_done"), sem("m_drive_done"), sem("m_scanned")
    read_done, summed, y_ready = sem("m_read_done"), sem("m_summed"), sem("m_y_ready")
    out_done = sem("m_out_done")
    b_bank, c_bank = [bank(0), bank(1)], [bank(2), bank(3)]
    sum_bank, misc = [bank(4), bank(5)], bank(6)

    def unit(buffer, slot):
        return buffer[:, slot, :].rearrange("p (j t) -> p j t", j=G)[:, :, 1:L]

    def by_sequence(columns):
        return columns.rearrange("p (j t) -> p j t", j=G)

    with nc.Block() as block:
        @block.sync
        def _(sp):
            sp_stage(c, sp)

        @block.gpsimd
        def _(pool):
            for buffer in (padded, decay, drive, x_dbl):
                last = pool.memset(buffer[:], 0.0)
            last.then_inc(zeros_set, 1)
            with pool.Fori(0, NG) as g:
                for m in range(U):
                    n = m // TD
                    pool.wait_ge(scanned, g * U + (m + 5))
                    pool.wait_ge(c_copied, g * NS + (n + 3))
                    pool.wait_ge(summed, g * U + (m + 1))
                    pool.tensor_tensor(by_sequence(read[:, m % R, :]), unit(state, m % R),
                                       by_sequence(c_wide[:, n % 2, :]), ALU.mult).then_inc(read_done, 1)
                tail_pool(c, pool, g + n0)

        @block.tensor
        def _(pe):
            def broadcast(g, n):
                gn = g * NS + n
                row = lambda i: c.w["ident"][:, i:i + 1].broadcast_to([P, P])
                pe.wait_ge(drive_done, (gn + 1) * 2)
                pe.matmul(b_bank[n % 2][:, :], row(DR + n), x_dbl[:, :], start=True, stop=True).then_inc(b_done, 1)
                pe.wait_ge(c_copied, gn + 1)
                pe.matmul(c_bank[n % 2][:, :], row(DR + NS + n), x_dbl[:, :], start=True, stop=True)\
                    .then_inc(c_done, 1)

            pe.wait_ge(zeros_set, 1)
            with pe.Fori(0, NG) as g:
                pe.wait_ge(c.xTs_loaded, (g + n0 + 1) * 16)
                pe.wait_ge(drive_done, g * U + 4)
                pe.wait_ge(c_copied, g * NS + 2)
                for t in range(2 * TD):
                    pe.matmul(bank(t)[:, :], c.w["m_in"][:, t * P:(t + 1) * P], c.xTs[:, :],
                              start=True, stop=True).then_inc(in_done, 1)
                if not c.last:
                    pe.wait_ge(c.yT_copied, g + n0 + 1)
                for t in range(TD):
                    pe.wait_ge(u_done, g * TD + (t + 1))
                    last = pe.matmul(misc[0:DR + 2 * NS, :], c.w["m_x_proj"][:, t, :], u[:, t, :],
                                     start=(t == 0), stop=(t == TD - 1))
                    if t == 0:
                        last.then_inc(c.xTs_used, 1)
                last.then_inc(dbl_done, 1)
                pe.wait_ge(dbl_copied, g + 1)
                pe.wait_ge(y_ready, g * TD + 2)
                for t in range(TD):
                    pe.matmul(sum_bank[t][:, :], c.w["m_dt"][:, t * P:(t + 1) * P], x_dbl[:, :],
                              start=True, stop=True).then_inc(dt_done, 1)
                broadcast(g, 0)
                broadcast(g, 1)
                for n in range(NS):
                    if n + 2 < NS:
                        broadcast(g, n + 2)
                    for t in range(TD):
                        m = n * TD + t
                        pe.wait_ge(read_done, g * U + (m + 1))
                        pe.matmul(sum_bank[t][:, :], c.w["ident"][:, :], read[:, m % R, :],
                                  start=(n == 0), stop=(n == NS - 1)).then_inc(summed, 1)
                pe.wait_ge(y_ready, g * TD + 4)
                pe.wait_ge(c.resid_done, g + n0 + 1)
                for j in range(G):
                    for t in range(TD):
                        last = pe.matmul(c.y_bank[:, j * P:(j + 1) * P], y[:, t, j * P:(j + 1) * P],
                                         c.w["m_out"][:, t, :], start=(t == 0), stop=(t == TD - 1))
                last.then_inc(out_done, 1)
                tail_pe(c, pe, g + n0, misc)

        @block.scalar
        def _(act):
            act.activation(minus_a[:, :, :], c.w["m_a_log"][:, :, :], ACT.Exp).then_inc(a_exp, 1)
            act.wait_ge(zeros_set, 1)
            act.wait_ge(a_ready, 1)
            ones_credit(act, [(c_copied, 2)])
            with act.Fori(0, NG) as g:
                for t in range(TD):
                    act.wait_ge(in_done, g * (2 * TD) + (t + 1))
                    act.wait_ge(conv_done, g * TD + (t + 1))
                    act.activation(padded[:, t, :, KC - 1:], by_sequence(bank(t)[:, :]), ACT.Copy)\
                        .then_inc(in_copied, 1)
                for t in range(TD):
                    act.wait_ge(in_done, g * (2 * TD) + (TD + t + 1))
                    act.wait_ge(out_done, g + 1)
                    act.activation(gate[:, t, :], bank(TD + t)[:, :], ACT.Silu)
                for t in range(TD):
                    act.wait_ge(conv_done, g * TD + (t + 3))
                    act.activation(u[:, t, :], conv[:, t, :], ACT.Silu).then_inc(u_done, 1)
                act.wait_ge(dbl_done, g + 1)
                act.activation(x_dbl[0:DR + 2 * NS, :], misc[0:DR + 2 * NS, :], ACT.Copy).then_inc(dbl_copied, 1)
                for t in range(TD):
                    act.wait_ge(dt_done, g * TD + (t + 1))
                    act.activation(exp_v[:, t, :], sum_bank[t][:, :], ACT.Abs, bias=c.w["m_dt_bias"][:, t:t + 1])\
                        .then_inc(abs_done, 1)
                act.wait_ge(abs_done, g * TD + TD)
                act.activation(exp_v[:, :, :], exp_v[:, :, :], ACT.Exp, scale=-1.0).then_inc(exp_v_done, 1)
                act.wait_ge(one_plus_done, g + 1)
                act.activation(log_part[:, :, :], one_plus[:, :, :], ACT.Ln).then_inc(log_done, 1)
                act.wait_ge(delta_done, g + 1)
                for n in range(NS):
                    for t in range(TD):
                        m = n * TD + t
                        act.wait_ge(scanned, g * U + (m + 1))
                        act.activation(unit(decay, m % R), by_sequence(delta[:, t, :]), ACT.Exp,
                                       scale=minus_a[:, t, n:n + 1]).then_inc(decay_done, 1)
                    act.wait_ge(c_done, g * NS + (n + 1))
                    act.wait_ge(summed, (g * NS + n) * 2 + 2)
                    act.activation(c_wide[:, n % 2, :], c_bank[n % 2][:, :], ACT.Copy).then_inc(c_copied, 1)
                tail_act(c, act, g + n0, misc)

        @block.vector
        def _(dve):
            def taps(g):
                for k in range(KC):
                    for t in range(TD):
                        if k == 0:
                            dve.wait_ge(in_copied, g * TD + (t + 1))
                        tap = KC - 1 - k
                        src = padded[:, t, :, tap:tap + P]
                        out = by_sequence(conv[:, t, :])
                        weight = c.w["m_conv"][:, t, tap:tap + 1]
                        if k == 0:
                            last = dve.tensor_scalar(out, src, weight, c.w["m_conv_bias"][:, t:t + 1],
                                                     ALU.mult, ALU.add)
                        else:
                            last = dve.scalar_tensor_tensor(out, src, weight, out, ALU.mult, ALU.add)
                        if k == KC - 1:
                            last.then_inc(conv_done, 1)
                    dve.drain()

            def softplus(g):
                dve.wait_ge(exp_v_done, g + 1)
                dve.tensor_scalar(one_plus[:, :, :], exp_v[:, :, :], 1.0, None, ALU.add).then_inc(one_plus_done, 1)
                for t in range(TD):
                    dve.tensor_scalar(delta[:, t, :], sum_bank[t][:, :], c.w["m_dt_bias"][:, t:t + 1], 0.0,
                                      ALU.add, ALU.max)
                dve.drain()
                dve.scalar_tensor_tensor(lost[:, :, :], one_plus[:, :, :], -1.0, exp_v[:, :, :],
                                         ALU.add, ALU.subtract)
                dve.drain()
                dve.tensor_tensor(delta[:, :, :], delta[:, :, :], lost[:, :, :], ALU.subtract)
                dve.drain()
                dve.wait_ge(log_done, g + 1)
                dve.tensor_tensor(delta[:, :, :], delta[:, :, :], log_part[:, :, :], ALU.add).then_inc(delta_done, 1)
                dve.drain()
                dve.tensor_tensor(du[:, :, :], delta[:, :, :], u[:, :, :], ALU.mult)
                dve.drain()

            def drive_unit(g, m):
                n, t = m // TD, m % TD
                dve.wait_ge(b_done, g * NS + (n + 1))
                dve.wait_ge(scanned, g * U + (m + 1))
                dve.tensor_tensor(unit(drive, m % R), by_sequence(b_bank[n % 2][:, :]), by_sequence(du[:, t, :]),
                                  ALU.mult).then_inc(drive_done, 1)

            def scan_unit(g, m):
                dve.wait_ge(decay_done, g * U + (m + 1))
                dve.wait_ge(drive_done, g * U + (m + 5))
                dve.wait_ge(summed, g * U + (m + 1))
                dve.tensor_tensor_scan(state[:, m % R, :], decay[:, m % R, :], drive[:, m % R, :], 0.0,
                                       ALU.mult, ALU.add).then_inc(scanned, 1)

            dve.wait_ge(a_exp, 1)
            dve.tensor_scalar(minus_a[:, :, :], minus_a[:, :, :], -1.0, None, ALU.mult).then_inc(a_ready, 1)
            dve.wait_ge(zeros_set, 1)
            ones_credit(dve, [(drive_done, 4), (scanned, 4), (summed, 4), (conv_done, 2), (y_ready, 2), (out_done, 1)])
            with dve.Fori(0, NG) as g:
                taps(g)
                softplus(g)
                drive_unit(g, 0)
                for m in range(U):
                    if m + 1 < U:
                        drive_unit(g, m + 1)
                    scan_unit(g, m)
                for t in range(TD):
                    dve.wait_ge(summed, g * U + (U - TD + t + 5))
                    if t == 0:
                        dve.wait_ge(out_done, g + 1)
                    dve.scalar_tensor_tensor(y[:, t, :], u[:, t, :], c.w["m_d"][:, t:t + 1], sum_bank[t][:, :],
                                             ALU.mult, ALU.add)
                dve.drain()
                for t in range(TD):
                    dve.tensor_tensor(y[:, t, :], y[:, t, :], gate[:, t, :], ALU.mult).then_inc(y_ready, 1)
                dve.wait_ge(out_done, g + 2)
                tail_dve(c, dve, g + n0)
    memory.close()



WEIGHTS = {
    "ident": ([P, P], F32), "causal": ([P, P], F32), "minus_half": ([P, G], F32),
    "a_wq": ([P, AH * AD], F32), "a_wk": ([P, AH * AD], F32), "a_wv": ([P, AH * AD], F32),
    "a_wo": ([P, 8, P], F32),
    "earlier": ([P, E, E], F32), "e_router": ([P, E], F32), "e_experts": ([P, E, P], F32),
    "m_in": ([P, 2 * DI], F32), "m_conv": ([P, 2, KC], F32), "m_conv_bias": ([P, 2], F32),
    "m_x_proj": ([P, 2, DR + 2 * NS], F32), "m_dt": ([P, DI], F32), "m_dt_bias": ([P, 2], F32),
    "m_a_log": ([P, 2, NS], F32), "m_d": ([P, 2], F32), "m_out": ([P, 2, P], F32),
    "f_router": ([P, E], F32), "f_w1": ([P, E, P], F32), "f_w2": ([P, E, P], F32), "f_w3": ([P, E, P], F32),
    "f_b1": ([P, E], F32), "f_b2": ([P, E], F32), "f_b3": ([P, E], F32),
    "f_sw1": ([P, 2, P], F32), "f_sw2": ([P, 2, P], F32), "f_sw3": ([P, 2, P], F32),
    "ones_row": ([1, P], F32), "head_of": ([P, XH], F32),
    "own_head": ([P, 4], F32),
    "x0_wq": ([P, P], F32), "x0_wk": ([P, P], F32), "x0_wv": ([P, P], F32), "x0_wo": ([P, P], F32),
    "x0_bq": ([P, 1], F32), "x0_bk": ([P, 1], F32), "x0_bv": ([SC, P], F32), "x0_bo": ([1, P], F32),
    "x0_select": ([P, 3, 3], F32), "x0_feat_bias": ([3, 1], F32),
    "x0_w1": ([3, 64], F32), "x0_b1": ([64, 1], F32), "x0_w2": ([64, P], F32), "x0_b2": ([64, 1], F32),
    "x0_w3": ([64, P], F32), "x0_b3": ([P, 1], F32),
    "x1_wq": ([P, P], F32), "x1_wk": ([P, P], F32), "x1_wv": ([P, P], F32), "x1_wo": ([P, P], F32),
    "x1_bo": ([1, P], F32),
}


def decoder(nc, dram, out, stages=(0, 1, 2, 3, 4, 5)):
    c = Core()
    c.x_dram = dram["x"].rearrange("b p d -> p b d")
    c.xT_dram = dram["xT"]
    c.dram = dram
    c.out_dram = out.rearrange("b p d -> p b d")
    c.sem = nc.alloc_semaphore
    c.sb = lambda name, shape, dtype=F32: nc.alloc_sbuf_tensor(name, shape, dtype)
    psum = nc.alloc_psum_tensor("psum", [P, 8, 512], F32)
    c.psum = psum
    c.bank = lambda i: psum[:, i, :]
    c.y_bank = c.bank(7)
    c.w = {name: c.sb("w_" + name, shape, dtype) for name, (shape, dtype) in WEIGHTS.items()}
    c.ident16, c.zeros16, c.causal16 = (c.sb(name, [P, n], BF16) for name, n in
                                        (("ident16", P), ("zeros16", W), ("causal16", W)))
    c.x_all = c.sb("x_all", [P, B, P])
    c.xT_all = c.sb("xT_all", [P, B * P])
    c.xs = c.sb("xs", [P, G, P])
    c.xTs = c.sb("xTs", [P, W])
    c.ctxTs = c.sb("ctxTs", [P, G * SC])
    c.ys = c.sb("ys", [P, G, P])
    c.yTs = c.sb("yTs", [P, W])
    c.resid = c.sb("resid", [P, G, P])
    c.bn = c.sb("bn", [P, G, 6])
    c.meanvar = c.sb("meanvar", [P, G, 2])
    c.var_eps = c.sb("var_eps", [P, G])
    c.rstd = c.sb("rstd", [P, G])

    c.loaded = c.sem("weights_loaded")
    c.resid_done = c.sem("resid_done")
    c.var_done, c.rstd_done = c.sem("var_done"), c.sem("rstd_done")
    c.y_normed, c.y_transposed = c.sem("y_normed"), c.sem("y_transposed")
    c.y_stored, c.yT_copied, c.yT_stored = c.sem("y_stored"), c.sem("yT_copied"), c.sem("yT_stored")
    c.xs_loaded, c.xTs_loaded, c.xTs_used = c.sem("xs_loaded"), c.sem("xTs_loaded"), c.sem("xTs_used")
    c.ctx_loaded = c.sem("ctx_loaded")

    with nc.Block() as block:
        @block.sync
        def _(sp):
            ones_credit(sp, [(c.resid_done, 1), (c.y_stored, 16), (c.yT_stored, 16), (c.y_transposed, 1),
                             (c.yT_copied, 1), (c.xTs_used, 1)])
            for name in c.w:
                sp.dma_start(c.w[name][:], dram[name]).then_inc(c.loaded, 16)
            sp.wait_ge(c.loaded, 16 * len(c.w))

        @block.gpsimd
        def _(pool):
            pool.memset(c.zeros16[:, :], 0.0)

        @block.vector
        def _(dve):
            dve.wait_ge(c.loaded, 16 * len(c.w))
            dve.tensor_copy(c.ident16[:, :], c.w["ident"][:, :])
            dve.tensor_copy(c.causal16[:, :].rearrange("p (m t) -> p m t", m=G),
                            c.w["causal"][:, :].unsqueeze(1).broadcast_to([P, G, P]))

    for stage in stages:
        c.last = stage == stages[-1]
        c.n0 = stages.index(stage) * NG
        c.ctx0 = sum(x in (1, 4) for x in stages[:stages.index(stage)]) * NG
        STAGES[stage](c, nc, stage)


STAGES = {0: causal_attention, 1: cross_attention, 2: linear_experts, 3: mamba, 4: cross_attention,
          5: gated_experts}



def by_block(rows):
    return rows.reshape(2, P, *rows.shape[1:]).swapaxes(0, 1)


def block_diagonal(weight):
    import numpy as np
    out = np.zeros((P, P), weight.dtype)
    for h in range(XH):
        out[h * XD:(h + 1) * XD, h * XD:(h + 1) * XD] = weight
    return out


def statistics_weights():
    import numpy as np
    out = np.zeros((P, 3, 3), np.float32)
    out[:, 0, 0] = XD ** -0.5 / (P * SC)
    out[:, 1, 1] = XD ** -0.5 / P
    out[:, 2, 2] = 1.0 / (P * (SC - 1))
    return out


def layouts(a):
    import numpy as np
    f32 = np.float32
    token = np.arange(P)
    d = {
        "x": a["x"],
        "xT": a["x"].transpose(2, 0, 1).reshape(P, B * P),
        "ident": np.eye(P, dtype=f32),
        "causal": np.where(token[None, :] > token[:, None], f32(-1e30), f32(0.0)),
        "minus_half": np.full((P, G), -0.5, f32),
        "a_wq": a["L0_attn_w_q"].transpose(2, 0, 1).reshape(P, AH * AD),
        "a_wk": a["L0_attn_w_k"].transpose(2, 0, 1).reshape(P, AH * AD),
        "a_wv": a["L0_attn_w_v"].transpose(2, 0, 1).reshape(P, AH * AD),
        "a_wo": a["L0_attn_w_o"].T.reshape(8, P, P).transpose(1, 0, 2),
        "earlier": np.broadcast_to(np.arange(E)[None, :] < np.arange(E)[:, None], (P, E, E)).astype(f32),
        "e_router": a["L0_ffn_router_w"].T, "e_experts": a["L0_ffn_expert_weights"].transpose(1, 0, 2),
        "m_in": a["L1_attn_in_proj_w"].T, "m_conv": by_block(a["L1_attn_conv_w"][:, 0, :]),
        "m_conv_bias": by_block(a["L1_attn_conv_b"]), "m_x_proj": by_block(a["L1_attn_x_proj_w"].T),
        "m_dt": np.concatenate([a["L1_attn_dt_proj_w"].T, np.zeros((P - DR, DI), f32)]),
        "m_dt_bias": by_block(a["L1_attn_dt_proj_b"]), "m_a_log": by_block(a["L1_attn_A_log"]),
        "m_d": by_block(a["L1_attn_D"]), "m_out": by_block(a["L1_attn_out_proj_w"].T),
        "f_router": a["L1_ffn_gate_w"].T, "f_w1": a["L1_ffn_w1"].transpose(2, 0, 1),
        "f_w2": a["L1_ffn_w2"].transpose(2, 0, 1), "f_w3": a["L1_ffn_w3"].transpose(2, 0, 1),
        "f_b1": a["L1_ffn_b1"].T, "f_b2": a["L1_ffn_b2"].T, "f_b3": a["L1_ffn_b3"].T,
        "f_sw1": a["L1_ffn_sw1"].T.reshape(P, 2, P), "f_sw2": a["L1_ffn_sw2"].T.reshape(P, 2, P),
        "f_sw3": by_block(a["L1_ffn_sw3"].T),
        "ones_row": np.ones((1, P), f32),
        "head_of": (token[:, None] // XD == np.arange(XH)[None, :]).astype(f32),
        "own_head": (token[:, None] // XD % 4 == np.arange(4)[None, :]).astype(f32),
        "ctxT": a["ctx_1024"].transpose(2, 0, 1).reshape(P, B * SC),
        "mask": np.broadcast_to(a["mask_Bx1x1xS2_if1"].reshape(1, B * SC), (P, B * SC)),
        "x0_wq": a["L0_xattn_Wq"].T, "x0_wk": a["L0_xattn_Wk"].T, "x0_wv": a["L0_xattn_Wv"].T,
        "x0_wo": a["L0_xattn_Wo"].T,
        "x0_bq": a["L0_xattn_bq"][:, None], "x0_bk": a["L0_xattn_bk"][:, None],
        "x0_bv": np.broadcast_to(a["L0_xattn_bv"][None, :], (SC, P)), "x0_bo": a["L0_xattn_bo"][None, :],
        "x0_select": statistics_weights(),
        "x0_feat_bias": np.array([[0.0], [0.0], [-1.0 / (SC * (SC - 1))]], f32),
        "x0_w1": a["L0_xattn_w1"].T, "x0_b1": a["L0_xattn_b1"][:, None],
        "x0_w2": np.concatenate([a["L0_xattn_w2"].T, np.zeros((64, 64), f32)], 1), "x0_b2": a["L0_xattn_b2"][:, None],
        "x0_w3": np.broadcast_to(a["L0_xattn_w3"].T, (64, P)),
        "x0_b3": np.broadcast_to(a["L0_xattn_b3"][None, :], (P, 1)),
        "x1_wq": block_diagonal(a["L1_xattn_Wq"]), "x1_wk": block_diagonal(a["L1_xattn_Wk"]),
        "x1_wv": block_diagonal(a["L1_xattn_Wv"].T), "x1_wo": a["L1_xattn_Wo"].T,
        "x1_bo": a["L1_xattn_bo"][None, :],
    }
    return {k: np.ascontiguousarray(v) for k, v in d.items()}


def kernel(**inputs):
    import numpy as np
    import concourse.bacc as bacc
    from concourse.bass_utils import run_bass_kernel_spmd

    arrays = layouts({name: np.asarray(value) for name, value in inputs.items()})
    nc = bacc.Bacc("TRN2", target_bir_lowering=False, num_devices=1)
    dram = {name: nc.dram_tensor("in_" + name, v.shape, mybir.dt.from_np(v.dtype), kind="ExternalInput").ap()
            for name, v in arrays.items()}
    out = nc.dram_tensor("out", (B, P, P), F32, kind="ExternalOutput").ap()
    decoder(nc, dram, out)
    result = run_bass_kernel_spmd(nc, [{"in_" + name: v for name, v in arrays.items()}], core_ids=[0])
    return result.results[0]["out"]
```

```python
from contextlib import ExitStack

import concourse.bass as bass
from concourse import mybir

F32 = mybir.dt.float32
BF16 = mybir.dt.bfloat16
I32 = mybir.dt.int32
ALU = mybir.AluOpType
ACT = mybir.ActivationFunctionType
X = mybir.AxisListType.X

P = 128
B = 32
G = 4
NG = B // G
W = G * P
SC = 77
EPS = 1e-5

AH, AD = 16, 64
XH, XD = 16, 8
E = 8
DI, NS, DR, KC = 256, 16, 64, 4
LOG_T_MIN, LOG_T_MAX = -2.302585092994046, 2.302585092994046


def stage_memory(nc, memory):
    return lambda name, shape, dtype=F32: memory.enter_context(nc.sbuf_tensor(name, shape, dtype))


class Core:
    pass


def ones_credit(engine, pairs):
    for semaphore, count in pairs:
        engine.sem_inc(semaphore, count)



def tail_dve_variance(c, dve, n):
    dve.wait_ge(c.xs_loaded, (n + 1) * 16)
    dve.tensor_tensor(c.resid[:, :, :], c.y_bank[:, :].rearrange("p (j d) -> p j d", j=G), c.xs[:, :, :],
                      ALU.add).then_inc(c.resid_done, 1)
    dve.drain()
    for j in range(G):
        dve.bn_stats(c.bn[:, j, :], c.resid[:, j, :])
    dve.drain()
    for j in range(G):
        dve.bn_aggr(c.meanvar[:, j, :], c.bn[:, j, :])
    dve.drain()
    dve.tensor_scalar(c.var_eps[:, :], c.meanvar[:, :, 1], EPS, None, ALU.add).then_inc(c.var_done, 1)


def tail_dve_norm(c, dve, n):
    dve.wait_ge(c.rstd_done, n + 1)
    dve.wait_ge(c.y_stored, (n + 1) * 16)
    if not c.last:
        dve.wait_ge(c.y_transposed, n + 1)
    for j in range(G):
        last = dve.tensor_scalar(c.ys[:, j, :], c.resid[:, j, :], c.meanvar[:, j, 0:1], c.rstd[:, j:j + 1],
                                 ALU.subtract, ALU.mult)
    last.then_inc(c.y_normed, 1)


def tail_dve(c, dve, n):
    tail_dve_variance(c, dve, n)
    tail_dve_norm(c, dve, n)


def tail_pool(c, pool, n):
    pool.wait_ge(c.var_done, n + 1)
    pool.tensor_tensor(c.rstd[:, :], c.var_eps[:, :], c.w["minus_half"][:, :], ALU.pow).then_inc(c.rstd_done, 1)


def tail_pe(c, pe, n, bank):
    if c.last:
        return
    pe.wait_ge(c.y_normed, n + 1)
    for j in range(G):
        last = pe.transpose(bank[:, j * P:(j + 1) * P], c.ys[:, j, :], c.w["ident"][:, :])
    last.then_inc(c.y_transposed, 1)


def tail_act(c, act, n, bank):
    if c.last:
        return
    act.wait_ge(c.y_transposed, n + 2)
    act.wait_ge(c.yT_stored, (n + 1) * 16)
    act.activation(c.yTs[:, :], bank[:, :], ACT.Copy).then_inc(c.yT_copied, 1)


def load_xT(c, sp, n, g, source_T, with_ctx=False):
    sp.wait_ge(c.xTs_used, n + 1)
    sp.dma_start(c.xTs[:, :], source_T[:, bass.ds(g * W, W)]).then_inc(c.xTs_loaded, 16)
    if with_ctx:
        sp.dma_start(c.ctxTs[:, :], c.dram["ctxT"][:, bass.ds(g * (G * SC), G * SC)]).then_inc(c.ctx_loaded, 16)


def load_xs(c, sp, n, g, source):
    sp.wait_ge(c.resid_done, n + 1)
    sp.dma_start(c.xs[:, :, :], source[:, bass.ds(g * G, G), :]).then_inc(c.xs_loaded, 16)


def store_x(c, sp, n, g, target, target_T):
    sp.wait_ge(c.y_normed, n + 1)
    sp.dma_start(target[:, bass.ds(g * G, G), :], c.ys[:, :, :]).then_inc(c.y_stored, 16)
    if target_T is not None:
        sp.wait_ge(c.yT_copied, n + 2)
        sp.dma_start(target_T[:, bass.ds(g * W, W)], c.yTs[:, :]).then_inc(c.yT_stored, 16)


def ends_of(c):
    source = (c.x_dram, c.xT_dram) if c.n0 == 0 else (c.x_all, c.xT_all)
    target = (c.out_dram, None) if c.last else (c.x_all, c.xT_all)
    return source + target


def all_stored(c, sp):
    sp.wait_ge(c.y_stored, (c.n0 + NG) * 16 + 16)
    if not c.last:
        sp.wait_ge(c.yT_stored, (c.n0 + NG) * 16 + 16)


def load_late(c, sp):
    for name in c.late:
        sp.dma_start(c.w[name][:], c.dram[name]).then_inc(c.late_loaded, 16)


def sp_stage(c, sp, first=False):
    n0 = c.n0
    source, source_T, target, target_T = ends_of(c)
    load_xT(c, sp, n0, 0, source_T)
    load_xs(c, sp, n0, 0, source)
    if first:
        load_late(c, sp)
    with sp.Fori(0, NG - 1) as g:
        load_xT(c, sp, g + n0 + 1, g + 1, source_T)
        load_xs(c, sp, g + n0 + 1, g + 1, source)
        store_x(c, sp, g + n0, g, target, target_T)
    store_x(c, sp, n0 + NG - 1, NG - 1, target, target_T)
    all_stored(c, sp)
    if first:
        sp.wait_ge(c.late_loaded, 16 * len(c.late))


def sp_stage_ahead(c, sp, with_ctx):
    n0 = c.n0
    source, source_T, target, target_T = ends_of(c)
    load_xT(c, sp, n0, 0, source_T, with_ctx)
    load_xT(c, sp, n0 + 1, 1, source_T, with_ctx)
    load_xs(c, sp, n0, 0, source)
    with sp.Fori(0, NG - 2) as g:
        load_xT(c, sp, g + n0 + 2, g + 2, source_T, with_ctx)
        load_xs(c, sp, g + n0 + 1, g + 1, source)
        store_x(c, sp, g + n0, g, target, target_T)
    load_xs(c, sp, n0 + NG - 1, NG - 1, source)
    store_x(c, sp, n0 + NG - 2, NG - 2, target, target_T)
    store_x(c, sp, n0 + NG - 1, NG - 1, target, target_T)
    all_stored(c, sp)



def causal_attention(c, nc, stage):
    n0 = c.n0
    NQ = AH // 4
    CH = 6
    S = G * NQ
    TURN, TIMES, OUT = 3, 4, 7
    VARIANCE, NORM, TAIL = 6, 8, 10
    sem, bank = c.sem, c.bank
    memory = ExitStack()
    sb = stage_memory(nc, memory)

    qT = sb("qT", [P, 2, 8, P])
    kT = sb("kT", [P, 2, 8, P])
    v = sb("v", [P, 2, AH, AD])
    probs = sb("probs", [P, 4, 4, P])
    probsT = sb("probsT", [P, 2, 4, P])
    row_max = sb("row_max", [P, 2, 4])
    row_sum, row_inv = sb("row_sum", [P, 2, 4]), sb("row_inv", [P, 4, 4])
    heads_outT = sb("heads_outT", [P, 2, 4, P])

    proj_bank = [bank(0), bank(1)]
    score_bank = [bank(2), bank(3)]
    probsT_bank, outT_bank = bank(4), [bank(5), bank(6)]

    proj_done, proj_copied = sem("a_proj_done"), sem("a_proj_copied")
    scores_done, scores_shifted = sem("a_scores_done"), sem("a_scores_shifted")
    probs_done, transposed = sem("a_probs_done"), sem("a_transposed")
    probsT_copied, pv_done = sem("a_probsT_copied"), sem("a_pv_done")
    normed, outT_copied = sem("a_normed"), sem("a_outT_copied")
    outT_used, sum_inverted = sem("a_outT_used"), sem("a_sum_inverted")

    def run(fori, before, steps):
        before()
        steps(0, range(S), False, True)
        with fori(0, NG - 2) as r:
            steps(r + 1, range(S), True, True)
        steps(NG - 1, range(S), True, False)
        steps(NG, range(TAIL + 2), True, None)

    def chunks_of(s, more):
        if s % NQ == 0 or s // NQ + 1 == G and not more:
            return None
        return s // NQ + 1, range(2 * (s % NQ) - 2, 2 * (s % NQ))

    def quad_heads(q):
        return [8 * (q // 2) + q % 2 + 2 * m for m in range(4)]

    with nc.Block() as block:
        @block.sync
        def _(sp):
            sp_stage(c, sp, first=True)

        @block.gpsimd
        def _(pool):
            def normalise(g, q):
                pool.wait_ge(sum_inverted, g * S + (q + 1))
                pool.tensor_tensor(probs[:, q % 4, :, :], probs[:, q % 4, :, :],
                                   row_inv[:, q % 4, :].unsqueeze(2).broadcast_to([P, 4, P]),
                                   ALU.mult).then_inc(normed, 1)

            def steps(g, which, former, more):
                for s in which:
                    if (s >= 1 or former) and (s < 1 or more is not None):
                        normalise(g, s - 1)
                    if s == VARIANCE and former:
                        tail_pool(c, pool, g - 1 + n0)

            run(pool.Fori, lambda: None, steps)

        @block.tensor
        def _(pe):
            def project(g, j, chunks):
                for ch in chunks:
                    t = g * (G * CH) + (j * CH + ch)
                    out = proj_bank[ch % 2]
                    if ch == 0 and j % G == 0:
                        pe.wait_ge(c.xTs_loaded, (g + n0 + j // G + 1) * 16)
                    pe.wait_ge(proj_copied, t + 1)
                    xj = c.xTs[:, j % G * P:(j % G + 1) * P]
                    if ch < 4:
                        w = (c.w["a_wq"], c.w["a_wk"])[ch // 2]
                        for m in range(4):
                            hp = 4 * (ch % 2) + m
                            last = pe.matmul(out[:, m * P:(m + 1) * P], w[:, hp * P:(hp + 1) * P], xj,
                                             start=True, stop=True)
                    else:
                        last = pe.matmul(out[:, :], xj, c.w["a_wv"][:, (ch - 4) * 512:(ch - 3) * 512],
                                         start=True, stop=True)
                    last.then_inc(proj_done, 1)

            def scores(g, q):
                j, r = q // NQ, (q // NQ) % 2
                if q % NQ == 0:
                    pe.wait_ge(proj_copied, g * (G * CH) + (j * CH + 4 + 2))
                pe.wait_ge(scores_shifted, g * S + (q + 1))
                out = score_bank[q % 2]
                mask = pe.matmul(out[:, :], c.ident16[:, :], c.causal16[:, :], start=True, stop=False)
                if q == (G - 1) * NQ:
                    mask.then_inc(c.xTs_used, 1)
                for m, h in enumerate(quad_heads(q % NQ)):
                    rows = slice(64 * (h % 2), 64 * (h % 2) + 64)
                    last = pe.matmul(out[:, m * P:(m + 1) * P], qT[rows, r, h // 2, :], kT[rows, r, h // 2, :],
                                     start=False, stop=(m == 3))
                last.then_inc(scores_done, 1)

            def transpose_probs(g, q, former):
                pe.wait_ge(normed, g * S + (q + 1))
                pe.wait_ge(probsT_copied, g * S + (q + 1))
                if q == TAIL - TURN and former and not c.last:
                    pe.wait_ge(c.yT_copied, g + n0 + 1)
                for m in range(4):
                    last = pe.transpose(probsT_bank[:, m * P:(m + 1) * P], probs[:, q % 4, m, :],
                                        c.w["ident"][:, :])
                last.then_inc(transposed, 1)

            def times_v(g, q):
                j, half = q // NQ, q // 2
                pe.wait_ge(probsT_copied, g * S + (q + 2))
                if q % NQ == 0:
                    pe.wait_ge(proj_copied, g * (G * CH) + (j * CH + CH + 2))
                if q % 2 == 0:
                    pe.wait_ge(outT_copied, g * (G * 2) + (half + 1))
                for m, h in enumerate(quad_heads(q % NQ)):
                    rows = slice(64 * (h % 2), 64 * (h % 2) + 64)
                    last = pe.matmul(outT_bank[half % 2][rows, m * P:(m + 1) * P], v[:, j % 2, h, :],
                                     probsT[:, q % 2, m, :], start=True, stop=True)
                last.then_inc(pv_done, 1)

            def project_out(g, half):
                j = half // 2
                pe.wait_ge(outT_copied, g * (G * 2) + (half + 3))
                if half % 8 == 0:
                    pe.wait_ge(c.resid_done, g + n0 + 1)
                for m in range(4):
                    hp = 4 * (half % 2) + m
                    last = pe.matmul(c.y_bank[:, j % G * P:(j % G + 1) * P], heads_outT[:, half % 2, m, :],
                                     c.w["a_wo"][:, hp, :], start=(hp == 0), stop=(hp == 7))
                last.then_inc(outT_used, 1)

            def steps(g, which, former, more):
                def exists(index):
                    return (index >= 0 or former) and (index < 0 or more is not None)

                for s in which:
                    if exists(s):
                        scores(g, s)
                    if exists(s) and chunks_of(s, more):
                        project(g, *chunks_of(s, more))
                    if s == TAIL and former:
                        pe.wait_ge(probsT_copied, g * S + (s - TURN + 1) if exists(s) else g * S + 1)
                        tail_pe(c, pe, g - 1 + n0, probsT_bank)
                    if exists(s - TURN):
                        transpose_probs(g, s - TURN, former)
                    if exists(s - TIMES):
                        times_v(g, s - TIMES)
                    if s % 2 == 1 and exists((s - OUT) // 2):
                        project_out(g, (s - OUT) // 2)

            run(pe.Fori, lambda: project(0, 0, range(CH)), steps)

        @block.scalar
        def _(act):
            def copy_projection(g, j, chunks):
                for ch in chunks:
                    t = g * (G * CH) + (j * CH + ch)
                    r = j % 2
                    act.wait_ge(proj_done, t + 1)
                    if ch == 0:
                        act.wait_ge(scores_done, g * S + ((j - 2) * NQ + NQ + 8))
                    if ch == 4:
                        act.wait_ge(pv_done, g * S + ((j - 2) * NQ + NQ + 8))
                    src = proj_bank[ch % 2]
                    if ch < 4:
                        dst = (qT, kT)[ch // 2][:, r, 4 * (ch % 2):4 * (ch % 2) + 4, :]
                        act.activation(dst, src[:, :].rearrange("p (m t) -> p m t", m=4), ACT.Copy)\
                            .then_inc(proj_copied, 1)
                    else:
                        dst = v[:, r, 8 * (ch - 4):8 * (ch - 3), :]
                        act.activation(dst, src[:, :].rearrange("p (h d) -> p h d", h=8), ACT.Copy)\
                            .then_inc(proj_copied, 1)

            def exp(g, q):
                act.wait_ge(scores_shifted, g * S + (q + 1 + 2))
                act.activation(probs[:, q % 4, :, :], probs[:, q % 4, :, :], ACT.Exp, scale=float(AD) ** -0.5)\
                    .then_inc(probs_done, 1)

            def copy_probsT(g, q):
                act.wait_ge(transposed, g * S + (q + 1 + 4))
                act.wait_ge(pv_done, g * S + (q - 1 + 8))
                act.activation(probsT[:, q % 2, :, :], probsT_bank[:, :].rearrange("p (m t) -> p m t", m=4),
                               ACT.Copy).then_inc(probsT_copied, 1)

            def copy_outT(g, half):
                act.wait_ge(pv_done, g * S + (2 * half + 2 + 8))
                act.wait_ge(outT_used, g * (G * 2) + (half + 1))
                act.activation(heads_outT[:, half % 2, :, :], outT_bank[half % 2][:, :].rearrange("p (m t) -> p m t", m=4),
                               ACT.Copy).then_inc(outT_copied, 1)

            def steps(g, which, former, more):
                def exists(index):
                    return (index >= 0 or former) and (index < 0 or more is not None)

                for s in which:
                    if exists(s):
                        exp(g, s)
                    if s == TAIL and former:
                        tail_act(c, act, g - 1 + n0, probsT_bank)
                    if exists(s - TURN):
                        copy_probsT(g, s - TURN)
                    if exists(s) and chunks_of(s, more):
                        copy_projection(g, *chunks_of(s, more))
                    if s % 2 == 0 and exists((s - OUT + 1) // 2):
                        copy_outT(g, (s - OUT + 1) // 2)

            ones_credit(act, [(proj_copied, 2), (probsT_copied, 1), (outT_copied, 2)])
            run(act.Fori, lambda: copy_projection(0, 0, range(CH)), steps)

        @block.vector
        def _(dve):
            def shift(g, q):
                s = g * S + q
                dve.wait_ge(scores_done, s + (1 + 8))
                dve.wait_ge(transposed, s + 1)
                src = score_bank[q % 2][:, :].rearrange("p (m t) -> p m t", m=4)
                dve.tensor_reduce(row_max[:, q % 2, :], src, X, ALU.max)
                dve.drain()
                dve.tensor_tensor(probs[:, q % 4, :, :], src,
                                  row_max[:, q % 2, :].unsqueeze(2).broadcast_to([P, 4, P]),
                                  ALU.subtract).then_inc(scores_shifted, 1)

            def invert_sum(g, q):
                dve.wait_ge(probs_done, g * S + (q + 1))
                dve.tensor_reduce(row_sum[:, q % 2, :], probs[:, q % 4, :, :], X, ALU.add)
                dve.drain()
                dve.reciprocal(row_inv[:, q % 4, :], row_sum[:, q % 2, :]).then_inc(sum_inverted, 1)

            def steps(g, which, former, more):
                for s in which:
                    if more is not None:
                        shift(g, s)
                    if (s >= 1 or former) and (s < 1 or more is not None):
                        invert_sum(g, s - 1)
                    if s == VARIANCE and former:
                        dve.wait_ge(outT_used, g * (2 * G) + 2)
                        tail_dve_variance(c, dve, g - 1 + n0)
                    if s == NORM and former:
                        tail_dve_norm(c, dve, g - 1 + n0)

            ones_credit(dve, [(scores_shifted, 2), (transposed, 4), (scores_done, 8), (pv_done, 8), (outT_used, 2)])
            run(dve.Fori, lambda: None, steps)
    memory.close()



def cross_attention(c, nc, stage):
    n0 = c.n0
    tempered = stage == 1
    w = {k[3:]: v for k, v in c.w.items() if k.startswith("x0_" if tempered else "x1_")}
    NC = 4
    HC = XH // NC
    QF = HC * XD
    T = G * NC
    Q_ENTRIES = ["q", "k0", "k1"] if tempered else ["k0"]
    k_parts = 2 if tempered else 1
    PROJECT_AT, FIRST_AT = (3, 8) if tempered else (6, 8)
    KEYS_AT, EXP_AT = (1, None) if tempered else (2, 11)
    MLP_AT = 13
    sem, bank = c.sem, c.bank
    memory = ExitStack()
    sb = stage_memory(nc, memory)
    pre = f"s{stage}_"

    q_quad = sb(pre + "q_quad", [P, NC, W])
    k_sb, v_sb = sb(pre + "k_sb", [P, G, SC]), sb(pre + "v_sb", [P, W])
    keys = sb(pre + "keys", [P, G, HC, SC])
    v_spread = sb(pre + "v_spread", [P, G, XH, QF])
    raw = sb(pre + "raw", [P, 2 * G, XH, SC])
    probs = sb(pre + "probs", [P, G, XH, SC])
    row_max = sb(pre + "row_max", [P, 2 * G, XH])
    row_sum, row_inv = sb(pre + "row_sum", [P, G, XH]), sb(pre + "row_inv", [P, G, XH])
    probsT = sb(pre + "probsT", [P, 2, HC, P])
    heads_outT = sb(pre + "heads_outT", [P, 2, P])
    own_head = c.w["own_head"][:, :].unsqueeze(2).broadcast_to([P, HC, SC])
    score_banks = c.psum[:, 0:4, 0:HC * SC].rearrange("p q (m t) -> p q m t", m=HC)
    ring_bank = [bank(4), bank(5)]
    pv_bank = bank(6)

    ring_done, ring_free = sem(pre + "ring_done"), sem(pre + "ring_free")
    q_copied, keys_done, v_spread_done = sem(pre + "q_copied"), sem(pre + "keys_done"), sem(pre + "v_spread_done")
    scores_done, shift_done = sem(pre + "scores_done"), sem(pre + "shift_done")
    probs_done, pv_done = sem(pre + "probs_done"), sem(pre + "pv_done")
    normed, sum_inverted = sem(pre + "normed"), sem(pre + "sum_inverted")
    outT_copied, out_done = sem(pre + "outT_copied"), sem(pre + "out_done")
    zeros_set, mask_ready = sem(pre + "zeros_set"), sem(pre + "mask_ready")
    if tempered:
        SCALE = XD ** -0.5
        qT = sb(pre + "qT", [P, W])
        exp1 = sb(pre + "exp1", [P, 2, 2, XH, SC])
        sum1, sum2 = sb(pre + "sum1", [P, G, XH]), sb(pre + "sum2", [P, 2 * G, XH])
        inv1 = sb(pre + "inv1", [P, G, XH])
        ksum, qsum, qk_sum = sb(pre + "ksum", [P, G]), sb(pre + "qsum", [P, G]), sb(pre + "qk_sum", [P, G])
        qk_heads = sb(pre + "qk_heads", [P, G, XH])
        feats = sb(pre + "feats", [3, G * XH])
        hidden1, hidden2 = sb(pre + "hidden1", [64, G * XH]), sb(pre + "hidden2", [64, G * XH])
        log_t, clip_t = sb(pre + "log_t", [P, G * XH]), sb(pre + "clip_t", [P, G * XH])
        inv_t = sb(pre + "inv_t", [P, G, XH])
        averaged = sem(pre + "averaged")
        exp1_done, sums_done = sem(pre + "exp1_done"), sem(pre + "sums_done")
        feats_ready, clipped = sem(pre + "feats_ready"), sem(pre + "clipped")
        inv_t_ready, scaled = sem(pre + "inv_t_ready"), sem(pre + "scaled")
        v_bias = w["bv"]
    else:
        SCALE = float(P) ** -0.5
        mask_int = sb(pre + "mask_int", [P, B * SC], I32)
        key_bias = sb(pre + "key_bias", [P, B, SC], BF16)
        w_qk = sb(pre + "w_qk", [P, P])
        v_bias = sb(pre + "v_bias", [P, P])
        mask_loaded, w_qk_done, w_qk_copied = sem(pre + "mask_loaded"), sem(pre + "w_qk_done"), sem(pre + "w_qk_copied")

    def entries_of(front, back, following):
        entries = []
        for t in range(T + 1):
            if following and 0 <= t - PROJECT_AT < len(Q_ENTRIES):
                entries.append(Q_ENTRIES[t - PROJECT_AT])
            if front and tempered and t >= MLP_AT:
                entries.append(f"mlp{t - MLP_AT}")
            if back and t < T:
                entries.append(f"chunk{t}")
        if following:
            entries.append("v")
        return entries

    def run(fori, first, iteration):
        first()
        base = len(Q_ENTRIES) + 1
        iteration(0, None, 1, base, 0)
        base += len(entries_of(True, False, True))
        step = len(entries_of(True, True, True))
        with fori(0, (NG - 2) // 2) as r:
            for i in range(2):
                iteration(r * 2 + (i + 1), r * 2 + i, r * 2 + (i + 2), base + r * (2 * step) + i * step, (i + 1) % 2)
        base += (NG - 2) * step
        iteration(NG - 1, NG - 2, None, base, (NG - 1) % 2)
        iteration(None, NG - 1, None, base + len(entries_of(True, True, False)), NG % 2)

    with nc.Block() as block:
        @block.sync
        def _(sp):
            if not tempered:
                sp.dma_start(mask_int[:, :], c.dram["mask"]).then_inc(mask_loaded, 16)
            sp_stage_ahead(c, sp, with_ctx=True)

        @block.gpsimd
        def _(pool):
            def spread_keys(g, j):
                pool.wait_ge(scores_done, g * G + (j + 1))
                pool.tensor_tensor(keys[:, j, :, :], k_sb[:, j, :].unsqueeze(1).broadcast_to([P, HC, SC]),
                                   own_head, ALU.mult).then_inc(keys_done, 1)

            def spread_values(g, j):
                block = v_spread[0:SC, j, :, :]
                own = bass.AP(block.tensor, block.offset, [block.ap[0], [HC * QF, NC], [QF + XD, HC], [1, XD]])
                src = v_sb[0:SC, j * P:(j + 1) * P].rearrange("p (q m d) -> p q m d", q=NC, m=HC)
                pool.wait_ge(pv_done, (g * G + (j + 1)) * NC)
                pool.tensor_tensor(own, src, v_bias[0:SC, :].rearrange("p (q m d) -> p q m d", q=NC, m=HC),
                                   ALU.add).then_inc(v_spread_done, 1)

            def scale(b, j, p):
                if j == 0:
                    pool.wait_ge(inv_t_ready, b + 1)
                pool.wait_ge(pv_done, (b * G + (j + 1)) * NC)
                pool.tensor_tensor(probs[:, j, :, :], raw[:, p * G + j, :, :],
                                   inv_t[:, j, :].unsqueeze(2).broadcast_to([P, XH, SC]),
                                   ALU.mult).then_inc(scaled, 1)

            def normalise(b, j):
                pool.wait_ge(sum_inverted, b * G + (j + 1))
                inverse = row_inv[:, j, :].unsqueeze(2).broadcast_to([P, XH, SC])
                pool.tensor_tensor(probs[:, j, :, :], probs[:, j, :, :], inverse, ALU.mult).then_inc(normed, 1)

            def first():
                pool.wait_ge(ring_free, len(Q_ENTRIES) + 2)
                for j in range(G):
                    spread_keys(0, j)

            def iteration(g, b, f, base, p):
                order = entries_of(g is not None, b is not None, f is not None)
                if b is not None:
                    if tempered:
                        scale(b, 0, 1 - p)
                        scale(b, 1, 1 - p)
                for j in range(G):
                    if b is not None:
                        if tempered and j + 2 < G:
                            scale(b, j + 2, 1 - p)
                        if tempered or j > 0:
                            normalise(b, j)
                    if f is not None and j == KEYS_AT:
                        pool.wait_ge(ring_free, base + (order.index(Q_ENTRIES[-1]) + 3))
                        for i in range(G):
                            spread_keys(f, i)
                if g is not None:
                    if not tempered:
                        normalise(g, 0)
                    pool.wait_ge(ring_free, base + 2)
                    for j in range(G):
                        spread_values(g, j)
                if b is not None:
                    tail_pool(c, pool, b + n0)

            ones_credit(pool, [(keys_done, 1), (v_spread_done, 1)])
            pool.memset(v_spread[:], 0.0)
            if not tempered:
                pool.memset(v_bias[:], 0.0)
            pool.memset(q_quad[:], 0.0)
            pool.memset(probsT[:], 0.0).then_inc(zeros_set, 1)
            pool.drain()
            run(pool.Fori, first, iteration)

        @block.tensor
        def _(pe):
            def entry(number):
                pe.wait_ge(ring_free, number + 1)

            def scores(g, j, q_free=None):
                if j == 0:
                    pe.wait_ge(*((ring_free, q_free) if tempered else (q_copied, g + 1)))
                pe.wait_ge(keys_done, g * G + (j + 2))
                pe.wait_ge(shift_done, g * G + (j + 1))
                for q in range(NC):
                    out = score_banks[:, q, :, :]
                    if not tempered:
                        bias = key_bias[:, bass.ds(g * G + j, 1), :].broadcast_to([P, HC, SC])
                        pe.matmul(out, c.ident16[:, :], bias, start=True, stop=False)
                    last = pe.matmul(out, q_quad[:, q, j * P:(j + 1) * P], keys[:, j, :, :],
                                     start=tempered, stop=True)
                    if j == 2 and q == 0:
                        last.then_inc(c.xTs_used, 1)
                last.then_inc(scores_done, 1)

            def project(g, name, number, slot):
                if name == Q_ENTRIES[0]:
                    pe.wait_ge(c.xTs_loaded, (g + n0 + 1) * 16)
                    pe.wait_ge(c.ctx_loaded, (g + c.ctx0 + 1) * 16)
                entry(number)
                out = ring_bank[slot]
                if name == "q":
                    last = pe.matmul(out[:, :], w["wq"][:, :], c.xTs[:, :], start=True, stop=True)
                elif name == "v":
                    for j in range(G):
                        last = pe.matmul(out[0:SC, j * P:(j + 1) * P], c.ctxTs[:, j * SC:(j + 1) * SC],
                                         w["wv"][:, :], start=True, stop=True)
                else:
                    n = G * SC // k_parts
                    part = int(name[1]) * n
                    last = pe.matmul(out[:, 0:n], w["wk"][:, :] if tempered else w_qk[:, :],
                                     c.ctxTs[:, part:part + n], start=True, stop=True)
                last.then_inc(ring_done, 1)

            def temperature_layer(g, k, base, order, p):
                entry(base + order.index(f"mlp{k}"))
                out = ring_bank[order.index(f"mlp{k}") % 2]
                if k == 0:
                    pe.wait_ge(feats_ready, g + 1)
                    slots = slice(p * G, (p + 1) * G)
                    for f, stat in enumerate((qk_heads[:, :, :], row_max[:, slots, :], sum2[:, slots, :])):
                        last = pe.matmul(out[0:3, 0:G * XH], w["select"][:, f, :],
                                         stat.rearrange("p j h -> p (j h)"), start=(f == 0), stop=(f == 2))
                else:
                    pe.wait_ge(ring_free, base + order.index(f"mlp{k - 1}") + 3)
                    rows, weight, source = ((64, w["w1"], feats), (P, w["w2"], hidden1), (P, w["w3"], hidden2))[k - 1]
                    last = pe.matmul(out[0:rows, 0:G * XH], weight[:, :], source[:, :], start=True, stop=True)
                last.then_inc(ring_done, 1)

            def transpose_chunk(b, u, base, order):
                j, k = u // NC, u % NC
                number = order.index(f"chunk{u}")
                if k == 0:
                    pe.wait_ge(normed, b * G + (j + 1))
                entry(base + number)
                for m in range(HC):
                    last = pe.transpose(ring_bank[number % 2][0:SC, m * P:(m + 1) * P], probs[:, j, k * HC + m, :],
                                        c.w["ident"][:, :])
                last.then_inc(ring_done, 1)

            def times_v(b, u, base, order):
                j, k = u // NC, u % NC
                if k == 0:
                    pe.wait_ge(v_spread_done, b * G + (j + 2))
                    pe.wait_ge(outT_copied, b * G + (j + 1))
                pe.wait_ge(ring_free, base + (order.index(f"chunk{u}") + 3))
                for m in range(HC):
                    last = pe.matmul(pv_bank[k * QF:(k + 1) * QF, 0:P], v_spread[:, j, k * HC + m, :],
                                     probsT[:, u % 2, m, :], start=(m == 0), stop=(m == HC - 1))
                last.then_inc(pv_done, 1)

            def project_out(b, j):
                pe.wait_ge(outT_copied, b * G + (j + 2))
                if j == 0:
                    pe.wait_ge(c.resid_done, b + n0 + 1)
                    if not c.last:
                        pe.wait_ge(c.yT_copied, b + n0 + 1)
                y = c.y_bank[:, j * P:(j + 1) * P]
                pe.matmul(y, heads_outT[:, j % 2, :], w["wo"][:, :], start=True, stop=False)
                pe.matmul(y, c.w["ones_row"][:, :], w["bo"][:, :], start=False, stop=True).then_inc(out_done, 1)

            def first():
                for i, name in enumerate(Q_ENTRIES + ["v"]):
                    project(0, name, i, i % 2)
                scores(0, 0, 3)
                scores(0, 1)

            def iteration(g, b, f, base, p):
                order = entries_of(g is not None, b is not None, f is not None)

                def project_next(name):
                    project(f, name, base + order.index(name), order.index(name) % 2)

                if g is not None:
                    scores(g, 2)
                    if tempered:
                        scores(g, 3)
                for t in range(T + 3):
                    if f is not None and 0 <= t - PROJECT_AT < len(Q_ENTRIES):
                        project_next(Q_ENTRIES[t - PROJECT_AT])
                    if g is not None and not tempered and t == FIRST_AT - 4:
                        scores(g, 3)
                    if f is not None and t == FIRST_AT:
                        scores(f, 0, base + (order.index("q") + 3) if tempered else None)
                    if f is not None and t == FIRST_AT + 4:
                        scores(f, 1)
                    if g is not None and tempered and MLP_AT <= t <= T:
                        temperature_layer(g, t - MLP_AT, base, order, p)
                    if b is not None:
                        if t < T:
                            transpose_chunk(b, t, base, order)
                        if 1 <= t <= T:
                            times_v(b, t - 1, base, order)
                        if t >= 6 and (t - 6) % NC == 0:
                            project_out(b, (t - 6) // NC)
                if f is not None:
                    project_next("v")
                if b is not None:
                    tail_pe(c, pe, b + n0, c.y_bank)

            pe.wait_ge(zeros_set, 1)
            if not tempered:
                pe.matmul(pv_bank[:, 0:P], w["wk"][:, :], w["wq"][:, :], start=True, stop=True).then_inc(w_qk_done, 1)
                pe.wait_ge(w_qk_copied, 1)
                pe.wait_ge(mask_ready, 1)
            run(pe.Fori, first, iteration)

        @block.scalar
        def _(act):
            def first_exp(g, j, p):
                act.wait_ge(shift_done, g * G + (j + 2))
                act.wait_ge(sums_done, g * G + (j + 1))
                for power in (1, 2):
                    act.activation(exp1[:, j % 2, power - 1, :, :], raw[:, p * G + j, :, :], ACT.Exp,
                                   scale=power * SCALE).then_inc(exp1_done, 1)

            def exp(b, j, p):
                if tempered:
                    act.wait_ge(scaled, b * G + (j + 9))
                    act.activation(probs[:, j, :, :], probs[:, j, :, :], ACT.Exp, scale=0.5).then_inc(probs_done, 1)
                else:
                    act.wait_ge(shift_done, b * G + (j + 2))
                    act.wait_ge(pv_done, (b * G + (j + 1)) * NC)
                    act.activation(probs[:, j, :, :], raw[:, p * G + j, :, :], ACT.Exp, scale=SCALE).then_inc(probs_done, 1)

            def copy_queries(g, source):
                act.wait_ge(scores_done, g * G + 4)
                bias = w["bq"] if tempered else None
                for q in range(NC):
                    rows = slice(q * QF, (q + 1) * QF)
                    last = act.activation(q_quad[rows, q, :], source[rows, :], ACT.Identity,
                                          bias=bias[rows, 0:1] if tempered else 0.0)
                return last

            def take(g, name, number, slot):
                src = ring_bank[slot]
                if name == Q_ENTRIES[0] and not tempered:
                    act.wait_ge(c.xTs_loaded, (g + n0 + 1) * 16)
                    copy_queries(g, c.xTs).then_inc(q_copied, 1)
                act.wait_ge(ring_done, number + 1)
                if name == "q":
                    act.wait_ge(averaged, g + 1)
                    act.activation(qT[:, :], src[:, :], ACT.Identity, bias=w["bq"][:, 0:1])
                    last = copy_queries(g, src)
                elif name == "v":
                    act.wait_ge(v_spread_done, g * G + 1)
                    last = act.activation(v_sb[0:SC, :], src[0:SC, :], ACT.Copy)
                else:
                    act.wait_ge(keys_done, g * G + 1)
                    js = G // k_parts
                    part = int(name[1]) * js
                    last = act.activation(
                        k_sb[:, part:part + js, :], src[:, 0:js * SC].rearrange("p (j t) -> p j t", j=js),
                        ACT.Identity, bias=w["bk"][:, 0:1] if tempered else 0.0)
                last.then_inc(ring_free, 1)

            def temperature_layer(g, k, base, order):
                number = order.index(f"mlp{k}")
                src = ring_bank[number % 2]
                act.wait_ge(ring_done, base + (number + 1))
                out, rows, func, bias = ((feats, 3, ACT.Identity, w["feat_bias"]), (hidden1, 64, ACT.Gelu, w["b1"]),
                                         (hidden2, 64, ACT.Gelu, w["b2"]), (log_t, P, ACT.Identity, w["b3"]))[k]
                act.activation(out[:, :], src[0:rows, 0:G * XH], func, bias=bias[:, 0:1]).then_inc(ring_free, 1)

            def inverse_temperature(g):
                act.wait_ge(clipped, g + 1)
                act.wait_ge(scaled, g * G + 8)
                act.activation(inv_t[:, :, :].rearrange("p j h -> p (j h)"), clip_t[:, :], ACT.Exp, scale=-1.0)\
                    .then_inc(inv_t_ready, 1)

            def copy_chunk(b, u, base, order):
                number = order.index(f"chunk{u}")
                act.wait_ge(ring_done, base + (number + 1))
                act.wait_ge(pv_done, b * T + (u - 1 + T))
                act.activation(probsT[0:SC, u % 2, :, :],
                               ring_bank[number % 2][0:SC, :].rearrange("p (m t) -> p m t", m=HC), ACT.Copy)\
                    .then_inc(ring_free, 1)

            def copy_outT(b, j):
                act.wait_ge(pv_done, (b * G + j) * NC + (NC + T))
                act.wait_ge(out_done, b * G + (j + 1))
                act.activation(heads_outT[:, j % 2, :], pv_bank[:, 0:P], ACT.Copy).then_inc(outT_copied, 1)

            def first():
                for i, name in enumerate(Q_ENTRIES + ["v"]):
                    take(0, name, i, i % 2)
                if tempered:
                    first_exp(0, 0, 0)

            def iteration(g, b, f, base, p):
                order = entries_of(g is not None, b is not None, f is not None)

                def take_next(name):
                    take(f, name, base + order.index(name), order.index(name) % 2)

                if b is not None and tempered:
                    exp(b, 0, 1 - p)
                if g is not None and tempered:
                    first_exp(g, 1, p)
                if b is not None and tempered:
                    exp(b, 1, 1 - p)
                if g is not None and tempered:
                    first_exp(g, 2, p)
                for t in range(T + 3):
                    if f is not None and 0 <= t - PROJECT_AT < len(Q_ENTRIES):
                        take_next(Q_ENTRIES[t - PROJECT_AT])
                    if g is not None and tempered and MLP_AT <= t <= T:
                        temperature_layer(g, t - MLP_AT, base, order)
                    if b is not None:
                        if t < T:
                            copy_chunk(b, t, base, order)
                        if t % NC == 1 and t // NC + 2 < G:
                            exp(b, t // NC + 2, 1 - p)
                        if t >= 5 and (t - 5) % NC == 0:
                            copy_outT(b, (t - 5) // NC)
                    if g is not None and not tempered and t in (EXP_AT, EXP_AT + 4):
                        exp(g, (t - EXP_AT) // NC, p)
                    if g is not None and tempered and t == 4:
                        first_exp(g, 3, p)
                    if f is not None and tempered and t == FIRST_AT + 2:
                        first_exp(f, 0, 1 - p)
                if f is not None:
                    take_next("v")
                if g is not None and tempered:
                    inverse_temperature(g)
                if b is not None:
                    tail_act(c, act, b + n0, c.y_bank)

            ones_credit(act, [(ring_free, 2), (outT_copied, 1), (probs_done, 8)])
            act.wait_ge(zeros_set, 1)
            if not tempered:
                act.wait_ge(w_qk_done, 1)
                act.activation(w_qk[:, :], pv_bank[:, 0:P], ACT.Copy).then_inc(w_qk_copied, 1)
            run(act.Fori, first, iteration)

        @block.vector
        def _(dve):
            def shift(g, j, p):
                slot = p * G + j
                dve.wait_ge(scores_done, g * G + (j + 5))
                dve.wait_ge(scaled if tempered else probs_done, g * G + (j + 1))
                largest = row_max[:, slot, :].rearrange("p (q m) -> p q m", q=NC)
                dve.tensor_reduce(largest, score_banks, X, ALU.max)
                dve.drain()
                dve.tensor_tensor(raw[:, slot, :, :].rearrange("p (q m) t -> p q m t", q=NC), score_banks,
                                  largest.unsqueeze(3).broadcast_to([P, NC, HC, SC]), ALU.subtract)\
                    .then_inc(shift_done, 1)

            def sums(g, j, p):
                if not tempered:
                    return
                dve.wait_ge(exp1_done, (g * G + j) * 2 + 2)
                dve.tensor_reduce(sum1[:, j, :], exp1[:, j % 2, 0, :, :], X, ALU.add)
                dve.tensor_reduce(sum2[:, p * G + j, :], exp1[:, j % 2, 1, :, :], X, ALU.add).then_inc(sums_done, 1)

            def averages(g):
                dve.tensor_reduce(qsum[:, :], qT[:, :].rearrange("p (j t) -> p j t", j=G), X, ALU.add)
                dve.tensor_reduce(ksum[:, :], k_sb[:, :, :], X, ALU.add).then_inc(averaged, 1)
                dve.drain()
                dve.tensor_tensor(qk_sum[:, :], ksum[:, :], qsum[:, :], ALU.mult)

            def statistics(g, p):
                square = sum2[:, p * G:(p + 1) * G, :]
                dve.drain()
                dve.reciprocal(inv1[:, :, :], sum1[:, :, :])
                dve.drain()
                dve.tensor_tensor(square, square, inv1[:, :, :], ALU.mult)
                dve.tensor_tensor(qk_heads[:, :, :], qk_sum[:, :].unsqueeze(2).broadcast_to([P, G, XH]),
                                  c.w["head_of"][:, :].unsqueeze(1).broadcast_to([P, G, XH]), ALU.mult)
                dve.drain()
                dve.tensor_tensor(square, square, inv1[:, :, :], ALU.mult).then_inc(feats_ready, 1)

            def clip(g, log_t_free):
                dve.wait_ge(ring_free, log_t_free)
                dve.tensor_scalar(clip_t[:, :], log_t[:, :], LOG_T_MIN, LOG_T_MAX, ALU.max, ALU.min)\
                    .then_inc(clipped, 1)

            def invert_sum(b, j):
                dve.wait_ge(probs_done, b * G + (j + 9))
                dve.tensor_reduce(row_sum[:, j, :], probs[:, j, :, :], X, ALU.add)
                dve.drain()
                dve.reciprocal(row_inv[:, j, :], row_sum[:, j, :]).then_inc(sum_inverted, 1)

            def first():
                shift(0, 0, 0)
                sums(0, 0, 0)
                shift(0, 1, 0)

            def iteration(g, b, f, base, p):
                order = entries_of(g is not None, b is not None, f is not None)
                if g is not None:
                    shift(g, 2, p)
                    if tempered:
                        averages(g)
                if b is not None:
                    invert_sum(b, 0 if tempered else 1)
                if g is not None:
                    sums(g, 1, p)
                    shift(g, 3, p)
                if b is not None:
                    invert_sum(b, 1 if tempered else 2)
                if g is not None:
                    sums(g, 2, p)
                if b is not None and tempered:
                    invert_sum(b, 2)
                if g is not None:
                    sums(g, 3, p)
                if g is not None and tempered:
                    statistics(g, p)
                if f is not None and not tempered:
                    shift(f, 0, 1 - p)
                if b is not None:
                    invert_sum(b, 3)
                if g is not None and not tempered:
                    invert_sum(g, 0)
                if f is not None:
                    if tempered:
                        shift(f, 0, 1 - p)
                        sums(f, 0, 1 - p)
                    shift(f, 1, 1 - p)
                if b is not None:
                    dve.wait_ge(out_done, b * G + (G + 2))
                    tail_dve_variance(c, dve, b + n0)
                if g is not None and tempered:
                    clip(g, base + (order.index("mlp3") + 3))
                if b is not None:
                    tail_dve_norm(c, dve, b + n0)

            ones_credit(dve, [(scores_done, 4), (shift_done, 1), (pv_done, T), (out_done, 2)])
            if tempered:
                ones_credit(dve, [(sums_done, 2), (scaled, 8), (averaged, 1)])
            else:
                dve.wait_ge(mask_loaded, 16)
                dve.tensor_scalar(key_bias[:, :, :].rearrange("p b t -> p (b t)"), mask_int[:, :], 0, -1e20,
                                  ALU.is_equal, ALU.mult).then_inc(mask_ready, 1)
            run(dve.Fori, first, iteration)
    memory.close()



def route(c, nc, pre, weight, wT, finish):
    memory = ExitStack()
    sb = stage_memory(nc, memory)
    sem = lambda name: c.sem(pre + name)
    wide, square = [P, B, E], [P, B, E, E]
    shifted, probs, chosen = sb(pre + "shifted", wide), sb(pre + "probs", wide), sb(pre + "chosen", wide)
    best, total, inverse = (sb(pre + name, [P, B]) for name in ("best", "total", "inverse"))
    above, equal, rank = sb(pre + "above", square), sb(pre + "equal", square), sb(pre + "rank", wide)
    w, rest = sb(pre + "w", wide), sb(pre + "rest", wide)
    parts = sb(pre + "parts", [P, B, P], BF16)
    logits_done, shift_done, exp_done = sem("logits_done"), sem("shift_done"), sem("exp_done")
    zeros_set, split, turned, copied = sem("zeros_set"), sem("split"), sem("turned"), sem("copied")
    logits = c.bank(0)[:, 0:B * E].rearrange("p (b e) -> p b e", b=B)

    with nc.Block() as block:
        @block.gpsimd
        def _(pool):
            pool.memset(parts[:], 0.0).then_inc(zeros_set, 1)

        @block.tensor
        def _(pe):
            for b in range(B):
                last = pe.matmul(c.bank(0)[:, b * E:(b + 1) * E], c.xT_all[:, b * P:(b + 1) * P], weight[:, :],
                                 start=True, stop=True)
            last.then_inc(logits_done, 1)
            pe.wait_ge(split, 1)
            for g in range(NG):
                if g >= 2:
                    pe.wait_ge(copied, g - 1)
                for j in range(G):
                    last = pe.matmul(c.bank(1 + g % 2)[:, j * P:(j + 1) * P], parts[:, g * G + j, :],
                                     c.ident16[:, :], start=True, stop=True)
                last.then_inc(turned, 1)

        @block.scalar
        def _(act):
            act.wait_ge(shift_done, 1)
            act.activation(probs[:, :, :], shifted[:, :, :], ACT.Exp).then_inc(exp_done, 1)
            for g in range(NG):
                act.wait_ge(turned, g + 1)
                act.activation(wT[:, g * W:(g + 1) * W], c.bank(1 + g % 2)[:, :], ACT.Copy).then_inc(copied, 1)

        @block.vector
        def _(dve):
            dve.wait_ge(logits_done, 1)
            dve.tensor_reduce(best[:, :], logits, X, ALU.max)
            dve.drain()
            dve.tensor_tensor(shifted[:, :, :], logits, best[:, :].unsqueeze(2).broadcast_to(wide),
                              ALU.subtract).then_inc(shift_done, 1)
            dve.wait_ge(exp_done, 1)
            dve.tensor_reduce(total[:, :], probs[:, :, :], X, ALU.add)
            dve.drain()
            dve.reciprocal(inverse[:, :], total[:, :])
            dve.drain()
            dve.tensor_tensor(probs[:, :, :], probs[:, :, :], inverse[:, :].unsqueeze(2).broadcast_to(wide), ALU.mult)
            dve.drain()
            other = probs[:, :, :].unsqueeze(2).broadcast_to(square)
            own = probs[:, :, :].unsqueeze(3).broadcast_to(square)
            dve.tensor_tensor(above[:], other, own, ALU.is_gt)
            dve.tensor_tensor(equal[:], other, own, ALU.is_equal)
            dve.drain()
            dve.tensor_tensor(equal[:], equal[:], c.w["earlier"][:, :, :].unsqueeze(1).broadcast_to(square), ALU.mult)
            dve.drain()
            dve.tensor_tensor(above[:], above[:], equal[:], ALU.add)
            dve.drain()
            dve.tensor_reduce(rank[:, :, :], above[:], X, ALU.add)
            dve.drain()
            dve.tensor_scalar(chosen[:, :, :], rank[:, :, :], 1.5, None, ALU.is_lt)
            dve.drain()
            dve.tensor_tensor(w[:, :, :], probs[:, :, :], chosen[:, :, :], ALU.mult)
            dve.drain()
            finish(dve, probs, chosen, w, total, inverse, shifted)
            high, mid, low = (parts[:, :, i * 32:i * 32 + E] for i in range(3))
            dve.wait_ge(zeros_set, 1)
            dve.tensor_copy(high, w[:, :, :])
            dve.drain()
            dve.tensor_tensor(rest[:, :, :], w[:, :, :], high, ALU.subtract)
            dve.drain()
            dve.tensor_copy(mid, rest[:, :, :])
            dve.drain()
            dve.tensor_tensor(low, rest[:, :, :], mid, ALU.subtract).then_inc(split, 1)
    memory.close()


def broadcast_weight(c, pe, out, wT, g, e):
    return pe.matmul(out[:, :], c.part_rows[:, e:e + 1].broadcast_to([P, P]), wT[:, bass.ds(g * W, W)],
                     start=True, stop=True)



def linear_experts(c, nc, stage):
    n0 = c.n0
    sem, bank = c.sem, c.bank
    memory = ExitStack()
    sb = stage_memory(nc, memory)
    R = 4
    wT = sb("e_wT", [P, B * P], BF16)
    bias = sb("e_bias", [P, B])
    scaled = sb("e_scaled", [P, R, W])
    w_done, scaled_done, used = sem("e_w_done"), sem("e_scaled_done"), sem("e_used")
    bias_added = sem("e_bias_added")
    w_bank = [bank(1), bank(2)]

    def finish(dve, probs, chosen, w, top_sum, inverse, scratch):
        dve.tensor_reduce(top_sum[:, :], w[:, :, :], X, ALU.add)
        dve.drain()
        dve.tensor_scalar(top_sum[:, :], top_sum[:, :], 1e-6, None, ALU.add)
        dve.drain()
        dve.reciprocal(inverse[:, :], top_sum[:, :])
        dve.drain()
        dve.tensor_tensor(w[:, :, :], w[:, :, :], inverse[:, :].unsqueeze(2).broadcast_to([P, B, E]), ALU.mult)
        dve.drain()
        dve.tensor_tensor(scratch[:, :, :], probs[:, :, :], w[:, :, :], ALU.mult)
        dve.drain()
        dve.tensor_reduce(bias[:, :], scratch[:, :, :], X, ALU.add)

    route(c, nc, "e_r_", c.w["e_router"], wT, finish)

    def run(fori, group, after):
        group(0, None)
        with fori(0, NG - 1) as r:
            group(r + 1, r)
        after(NG - 1)

    with nc.Block() as block:
        @block.sync
        def _(sp):
            sp_stage(c, sp)

        @block.gpsimd
        def _(pool):
            def group(g, tail):
                if tail is not None:
                    tail_pool(c, pool, tail + n0)

            run(pool.Fori, group, lambda g: tail_pool(c, pool, g + n0))

        @block.tensor
        def _(pe):
            def group(g, tail):
                for s in range(E + 2):
                    if s < E:
                        pe.wait_ge(scaled_done, g * E + (s + 1))
                        broadcast_weight(c, pe, w_bank[s % 2], wT, g, s).then_inc(w_done, 1)
                    if s == 2:
                        pe.wait_ge(c.resid_done, g + n0 + 1)
                        pe.matmul(c.y_bank[:, :], c.ident16[:, :], c.zeros16[:, :], start=True, stop=False)
                    if s >= 2:
                        e = s - 2
                        pe.wait_ge(scaled_done, g * E + (e + 3))
                        for j in range(G):
                            last = pe.matmul(c.y_bank[:, j * P:(j + 1) * P], scaled[:, e % R, j * P:(j + 1) * P],
                                             c.w["e_experts"][:, e, :], start=False,
                                             stop=(e == E - 1 and j == G - 1))
                            if e == E - 1 and j == 0:
                                last.then_inc(c.xTs_used, 1)
                        last.then_inc(used, 1)
                    if s == 7 and tail is not None:
                        turn(tail)

            def turn(g):
                if not c.last:
                    pe.wait_ge(c.yT_copied, g + n0 + 1)
                tail_pe(c, pe, g + n0, bank(3))

            run(pe.Fori, group, turn)

        @block.scalar
        def _(act):
            def group(g, tail):
                if tail is not None:
                    tail_act(c, act, tail + n0, bank(3))

            run(act.Fori, group, lambda g: tail_act(c, act, g + n0, bank(3)))

        @block.vector
        def _(dve):
            def scale(g, e):
                dve.wait_ge(w_done, g * E + (e + 1))
                dve.wait_ge(used, g * E + (e + 1))
                if e == 0:
                    dve.wait_ge(c.xTs_loaded, (g + n0 + 1) * 16)
                dve.tensor_tensor(scaled[:, e % R, :], w_bank[e % 2][:, :], c.xTs[:, :], ALU.mult)\
                    .then_inc(scaled_done, 1)

            def add_bias(g):
                dve.wait_ge(c.xs_loaded, (g + n0 + 1) * 16)
                dve.tensor_tensor(c.xs[:, :, :], c.xs[:, :, :],
                                  bias[:, bass.ds(g * G, G)].unsqueeze(2).broadcast_to([P, G, P]), ALU.add)\
                    .then_inc(bias_added, 1)

            def variance(g):
                dve.wait_ge(used, g * E + (E + R))
                dve.wait_ge(bias_added, g + 1)
                tail_dve_variance(c, dve, g + n0)

            def group(g, tail):
                scale(g, 0)
                if tail is not None:
                    add_bias(tail)
                scale(g, 1)
                if tail is not None:
                    variance(tail)
                for e in range(2, E):
                    scale(g, e)
                    if e == 4 and tail is not None:
                        tail_dve_norm(c, dve, tail + n0)

            def after(g):
                add_bias(g)
                variance(g)
                tail_dve_norm(c, dve, g + n0)

            ones_credit(dve, [(scaled_done, 2), (used, R)])
            run(dve.Fori, group, after)
    memory.close()



def gated_experts(c, nc, stage):
    n0 = c.n0
    sem, bank = c.sem, c.bank
    memory = ExitStack()
    sb = stage_memory(nc, memory)
    NSH = 2
    NI = NSH + E
    wT = sb("f_wT", [P, B * P], BF16)
    scaled = sb("f_scaled", [P, 2, W])
    hidden = sb("f_hidden", [P, 2, W])
    gate = sb("f_gate", [P, 2, W])
    product = sb("f_product", [P, 2, W])
    expert_sum = sb("f_expert_sum", [P, 2, W])
    no_sum = sb("f_no_sum", [P, W])
    w_done, scaled_done = sem("f_w_done"), sem("f_scaled_done")
    h_done, gate_done, hidden_done = sem("f_h_done"), sem("f_gate_done"), sem("f_hidden_done")
    gate_copied, masked, out_done = sem("f_gate_copied"), sem("f_masked"), sem("f_out_done")
    product_done, shared_summed, added, y_done = sem("f_product_done"), sem("f_shared_summed"), sem("f_added"), sem("f_y_done")
    out_bank = bank(5)
    w_bank, h_bank, gate_bank = [bank(1), bank(2)], [bank(3), bank(6)], [bank(4), bank(0)]

    def finish(dve, probs, chosen, w, total, inverse, scratch):
        dve.scalar_tensor_tensor(w[:, :, :], chosen[:, :, :], -1.0, w[:, :, :], ALU.add, ALU.add)
        dve.drain()

    route(c, nc, "f_r_", c.w["f_router"], wT, finish)

    def run(fori, group, after):
        group(0, None)
        with fori(0, NG - 1) as r:
            group(r + 1, r)
        after(NG - 1)

    with nc.Block() as block:
        @block.sync
        def _(sp):
            sp_stage_ahead(c, sp, with_ctx=False)

        @block.gpsimd
        def _(pool):
            def add(g, e):
                pool.wait_ge(product_done, g * NI + (NSH + e + 3))
                if e == 0:
                    pool.wait_ge(y_done, g + 1)
                    former = no_sum[:, :]
                else:
                    pool.wait_ge(added, g * E + (e + 2))
                    former = expert_sum[:, (e - 1) % 2, :]
                pool.tensor_tensor(expert_sum[:, e % 2, :], former, product[:, (NSH + e) % 2, :], ALU.add)\
                    .then_inc(added, 1)

            def group(g, tail):
                for e in range(E):
                    add(g, e)
                    if e == 0 and tail is not None:
                        tail_pool(c, pool, tail + n0)

            pool.memset(no_sum[:, :], 0.0)
            pool.drain()
            run(pool.Fori, group, lambda g: tail_pool(c, pool, g + n0))

        @block.tensor
        def _(pe):
            def weight(g, s):
                e = s - NSH
                pe.wait_ge(masked, g * E + (e + 1))
                broadcast_weight(c, pe, w_bank[e % 2], wT, g, e).then_inc(w_done, 1)

            def inner(g, s):
                n = g * NI + s
                if s < NSH:
                    rhs, w_h, w_gate = c.xTs[:, :], c.w["f_sw1"][:, s, :], c.w["f_sw2"][:, s, :]
                else:
                    e = s - NSH
                    rhs, w_h, w_gate = scaled[:, e % 2, :], c.w["f_w1"][:, e, :], c.w["f_w3"][:, e, :]
                    pe.wait_ge(scaled_done, g * E + (e + 1))
                pe.wait_ge(hidden_done, n + 1)
                pe.matmul(h_bank[s % 2][:, :], w_h, rhs, start=True, stop=True).then_inc(h_done, 1)
                pe.wait_ge(product_done, n + 1)
                pe.matmul(gate_bank[s % 2][:, :], w_gate, rhs, start=True, stop=True).then_inc(gate_done, 1)

            def outer(g, s):
                n = g * NI + s
                pe.wait_ge(hidden_done, n + 3)
                pe.wait_ge(product_done, n + 2)
                pe.matmul(out_bank[:, :], c.w["f_w2"][:, s - NSH, :], hidden[:, s % 2, :],
                                 start=True, stop=True).then_inc(out_done, 1)

            def accumulate_shared(g, s):
                pe.wait_ge(product_done, g * NI + (s + 3))
                if s == 0:
                    pe.wait_ge(c.resid_done, g + n0 + 1)
                    pe.matmul(c.y_bank[:, :], c.ident16[:, :], c.zeros16[:, :], start=True, stop=False)
                for j in range(G):
                    last = pe.matmul(c.y_bank[:, j * P:(j + 1) * P], product[:, s % 2, j * P:(j + 1) * P],
                                     c.w["f_sw3"][:, s, :], start=False, stop=False)
                last.then_inc(shared_summed, 1)

            def accumulate_experts(g):
                pe.wait_ge(added, g * E + (E + 2))
                for j in range(G):
                    last = pe.matmul(c.y_bank[:, j * P:(j + 1) * P],
                                     expert_sum[:, (E - 1) % 2, j * P:(j + 1) * P], c.w["ident"][:, :],
                                     start=False, stop=(j == G - 1))
                last.then_inc(y_done, 1)

            def group(g, tail):
                pe.wait_ge(c.xTs_loaded, (g + n0 + 1) * 16)
                for s in range(NI + 1):
                    if s < NI:
                        inner(g, s)
                    if s == 0 and tail is not None:
                        accumulate_experts(tail)
                    if NSH <= s + 1 < NI:
                        weight(g, s + 1)
                    if NSH <= s - 1 < NI:
                        outer(g, s - 1)
                    if 2 <= s < NSH + 2:
                        accumulate_shared(g, s - 2)
                    if s == NI - 1:
                        pe.sem_inc(c.xTs_used, 1)

            run(pe.Fori, group, accumulate_experts)

        @block.scalar
        def _(act):
            def group(g, tail):
                for s in range(NI):
                    n = g * NI + s
                    act.wait_ge(h_done, n + 1)
                    act.wait_ge(product_done, n + 1)
                    bias = c.w["f_b1"][:, s - NSH:s - NSH + 1] if s >= NSH else 0.0
                    act.activation(hidden[:, s % 2, :], h_bank[s % 2][:, :], ACT.Silu, bias=bias)\
                        .then_inc(hidden_done, 1)
                    if s >= NSH:
                        act.wait_ge(gate_done, n + 3)
                        act.activation(gate[:, s % 2, :], gate_bank[s % 2][:, :], ACT.Identity,
                                       bias=c.w["f_b3"][:, s - NSH:s - NSH + 1]).then_inc(gate_copied, 1)

            ones_credit(act, [(hidden_done, 2)])
            act.preload_act_table(ACT.Silu)
            run(act.Fori, group, lambda g: None)

        @block.vector
        def _(dve):
            def scale(g, s):
                e = s - NSH
                dve.wait_ge(w_done, g * E + (e + 1))
                dve.wait_ge(gate_done, g * NI + (s + 1))
                dve.scalar_tensor_tensor(scaled[:, e % 2, :], w_bank[e % 2][:, :], 0.0, c.xTs[:, :],
                                         ALU.max, ALU.mult).then_inc(scaled_done, 1)

            def mask(g, s):
                e = s - NSH
                dve.wait_ge(gate_copied, g * E + (e + 1))
                dve.scalar_tensor_tensor(gate[:, s % 2, :], w_bank[e % 2][:, :], 0.0, gate[:, s % 2, :],
                                         ALU.is_ge, ALU.mult).then_inc(masked, 1)

            def multiply(g, s):
                n = g * NI + s
                if s < NSH:
                    dve.wait_ge(hidden_done, n + 3)
                    dve.wait_ge(gate_done, n + 3)
                    dve.wait_ge(added, g * E + (s + 1))
                    dve.tensor_tensor(product[:, s % 2, :], gate_bank[s % 2][:, :], hidden[:, s % 2, :],
                                      ALU.mult).then_inc(product_done, 1)
                    return
                e = s - NSH
                dve.wait_ge(masked, g * E + (e + 3))
                dve.wait_ge(out_done, g * E + (e + 1))
                if e < 2:
                    dve.wait_ge(shared_summed, g * NSH + (e + 1))
                else:
                    dve.wait_ge(added, g * E + (e + 1))
                dve.scalar_tensor_tensor(product[:, s % 2, :], out_bank[:, :], c.w["f_b2"][:, e:e + 1],
                                         gate[:, s % 2, :], ALU.add, ALU.mult).then_inc(product_done, 1)

            def variance(g):
                dve.wait_ge(y_done, g + 2)
                tail_dve_variance(c, dve, g + n0)

            def group(g, tail):
                for s in range(NI + 1):
                    if s > NSH:
                        mask(g, s - 1)
                    if NSH <= s + 1 < NI:
                        scale(g, s + 1)
                    if s == 1 and tail is not None:
                        variance(tail)
                    if s >= 1:
                        multiply(g, s - 1)
                    if s == 4 and tail is not None:
                        tail_dve_norm(c, dve, tail + n0)

            def after(g):
                variance(g)
                tail_dve_norm(c, dve, g + n0)

            ones_credit(dve, [(gate_done, 2), (masked, 2), (product_done, 2), (added, 2), (y_done, 1)])
            run(dve.Fori, group, after)
    memory.close()



def mamba(c, nc, stage):
    n0 = c.n0
    sem, bank = c.sem, c.bank
    memory = ExitStack()
    sb = stage_memory(nc, memory)
    TD = DI // P
    U = NS * TD
    R, RD, RR, RC = 4, 8, 8, 4
    L = P + 1
    BC = 2 * NS
    LOG_EXP = "natural_log_exp_and_others"
    ENTRIES = ["in0", "in1", "z0", "z1", "dt", "bc", "delta0", "delta1"]
    NE = len(ENTRIES)
    padded = sb("m_padded", [P, TD, G, P + KC - 1])
    conv, u = sb("m_conv", [P, TD, W]), sb("m_u", [P, TD, W])
    z, gate = sb("m_z", [P, TD, W]), sb("m_gate", [P, TD, W])
    dt_in = sb("m_dt_in", [P, W])
    bc, rest, rest2 = sb("m_bc", [3 * BC, W]), sb("m_rest", [3 * BC, W]), sb("m_rest2", [3 * BC, W])
    high, mid = sb("m_high", [3 * BC, W], BF16), sb("m_mid", [3 * BC, W], BF16)
    parts = sb("m_parts", [P, W], BF16)
    exp_v, one_plus = sb("m_exp_v", [P, TD, W]), sb("m_one_plus", [P, TD, W])
    lost, log_part = exp_v, one_plus
    positive = sb("m_positive", [P, TD, W])
    delta, du = sb("m_delta", [P, TD, W]), sb("m_du", [P, TD, W])
    minus_a, diagonal = sb("m_minus_a", [P, TD, NS]), sb("m_diagonal", [P, TD, P])
    decay, drive = sb("m_decay", [P, RD, G * L]), sb("m_drive", [P, R, G * L])
    state = sb("m_state", [P, R, G * L])
    c_wide = sb("m_c_wide", [P, RC, W])
    read = sb("m_read", [P, RR, W])
    y = sb("m_y", [P, TD, W])

    zeros_set, a_exp, setup_done = sem("m_zeros_set"), sem("m_a_exp"), sem("m_setup_done")
    ring_done, ring_free = sem("m_ring_done"), sem("m_ring_free")
    conv_done, gate_done, u_done = sem("m_conv_done"), sem("m_gate_done"), sem("m_u_done")
    rest_done, mid_done, rest2_done, parts_ready = sem("m_rest_done"), sem("m_mid_done"), sem("m_rest2_done"), sem("m_parts_ready")
    abs_done, exp_v_done, one_plus_done = sem("m_abs_done"), sem("m_exp_v_done"), sem("m_one_plus_done")
    log_done, lost_done, linear_done = sem("m_log_done"), sem("m_lost_done"), sem("m_linear_done")
    delta_done = sem("m_delta_done")
    b_done, c_done, c_copied = sem("m_b_done"), sem("m_c_done"), sem("m_c_copied")
    decay_done, drive_done, scanned = sem("m_decay_done"), sem("m_drive_done"), sem("m_scanned")
    read_done, summed, y_ready = sem("m_read_done"), sem("m_summed"), sem("m_y_ready")
    out_done = sem("m_out_done")
    b_bank, c_bank = [bank(0), bank(1)], bank(2)
    ring_bank, sum_bank = [bank(3), bank(6)], [bank(4), bank(5)]

    def unit(buffer, slot):
        return buffer[:, slot, :].rearrange("p (j t) -> p j t", j=G)[:, :, 1:L]

    def by_sequence(columns):
        return columns.rearrange("p (j t) -> p j t", j=G)

    def number(h, name):
        return h * NE + ENTRIES.index(name)

    def run(fori, front, group, tail):
        front(0)
        group(0, 1, None)
        with fori(0, NG - 2) as r:
            group(r + 1, r + 2, r)
        group(NG - 1, None, NG - 2)
        tail(NG - 1)

    with nc.Block() as block:
        @block.sync
        def _(sp):
            sp_stage_ahead(c, sp, with_ctx=False)

        @block.gpsimd
        def _(pool):
            def add_linear(h):
                pool.wait_ge(lost_done, h + 1)
                pool.tensor_tensor(positive[:, :, :], positive[:, :, :], lost[:, :, :], ALU.subtract)\
                    .then_inc(linear_done, 1)

            def group(g, h, tail):
                for m in range(U):
                    n = m // TD
                    pool.wait_ge(scanned, g * U + (m + 1 + RD))
                    pool.wait_ge(c_copied, g * NS + (n + 2))
                    pool.wait_ge(summed, g * U + (m + 1))
                    pool.tensor_tensor(by_sequence(read[:, m % RR, :]), unit(state, m % R),
                                       by_sequence(c_wide[:, n % RC, :]), ALU.mult).then_inc(read_done, 1)
                    if m == 5 and tail is not None:
                        tail_pool(c, pool, tail + n0)
                    if m == 28 and h is not None:
                        add_linear(h)

            for buffer in (padded, decay, drive, dt_in, parts):
                last = pool.memset(buffer[:], 0.0)
            last.then_inc(zeros_set, 1)
            run(pool.Fori, add_linear, group, lambda g: tail_pool(c, pool, g + n0))

        @block.tensor
        def _(pe):
            def entry(h, name, products):
                pe.wait_ge(ring_free, number(h, name) + 1)
                out = ring_bank[ENTRIES.index(name) % 2]
                for i, (rows, weights, operand) in enumerate(products):
                    last = pe.matmul(out[0:rows, :], weights, operand, start=(i == 0), stop=(i == len(products) - 1))
                    if name == "dt" and i == 0:
                        last.then_inc(c.xTs_used, 1)
                last.then_inc(ring_done, 1)

            def front_step(h, n):
                if n == 0:
                    pe.wait_ge(c.xTs_loaded, (h + n0 + 1) * 16)
                    for t in range(TD):
                        entry(h, f"in{t}", [(P, c.w["m_in"][:, t * P:(t + 1) * P], c.xTs[:, :])])
                for t in range(TD):
                    if n == 4 + t:
                        entry(h, f"z{t}", [(P, c.w["m_in"][:, (TD + t) * P:(TD + t + 1) * P], c.xTs[:, :])])
                if n == 7:
                    pe.wait_ge(u_done, h * TD + TD)
                    entry(h, "dt", [(DR, c.w["m_x_proj"][:, t, 0:DR], u[:, t, :]) for t in range(TD)])
                if n == 8:
                    entry(h, "bc", [(3 * BC, c.w["m_x_proj"][:, t, DR:DR + 3 * BC], u[:, t, :]) for t in range(TD)])
                if n == 9:
                    pe.wait_ge(ring_free, number(h, "dt") + 3)
                for t in range(TD):
                    if n == 9 + t:
                        entry(h, f"delta{t}", [(P, c.w["m_dt"][:, t * P:(t + 1) * P], dt_in[:, :])])

            def broadcast_b(g, n):
                pe.wait_ge(drive_done, (g * NS + n + 1) * 2)
                pe.matmul(b_bank[n % 2][:, :], c.part_rows[:, n:n + 1].broadcast_to([P, P]), parts[:, :],
                          start=True, stop=True).then_inc(b_done, 1)

            def broadcast_c(g, n):
                pe.wait_ge(c_copied, g * NS + (n + 1))
                pe.matmul(c_bank[:, :], c.part_rows[:, NS + n:NS + n + 1].broadcast_to([P, P]), parts[:, :],
                          start=True, stop=True).then_inc(c_done, 1)

            def sum_state(g, n):
                for t in range(TD):
                    m = n * TD + t
                    pe.wait_ge(read_done, g * U + (m + 1 + 2 * R))
                    pe.matmul(sum_bank[t][:, :], c.w["ident"][:, :], read[:, m % RR, :],
                              start=False, stop=(n == NS - 1)).then_inc(summed, 1)

            def project_out(g):
                pe.wait_ge(y_ready, g * TD + 4)
                pe.wait_ge(c.resid_done, g + n0 + 1)
                if not c.last:
                    pe.wait_ge(c.yT_copied, g + n0 + 1)
                for j in range(G):
                    for t in range(TD):
                        last = pe.matmul(c.y_bank[:, j * P:(j + 1) * P], y[:, t, j * P:(j + 1) * P],
                                         c.w["m_out"][:, t, :], start=(t == 0), stop=(t == TD - 1))
                last.then_inc(out_done, 1)

            def front(h):
                for n in range(NS):
                    front_step(h, n)

            def group(g, h, tail):
                pe.wait_ge(parts_ready, g + 1)
                broadcast_b(g, 0)
                broadcast_c(g, 0)
                broadcast_b(g, 1)
                if h is not None:
                    front_step(h, 0)
                broadcast_c(g, 1)
                pe.wait_ge(y_ready, g * TD + 2)
                for t in range(TD):
                    pe.matmul(sum_bank[t][:, :], diagonal[:, t, :], u[:, t, :], start=True, stop=False)
                for n in range(NS):
                    if n + 2 < NS:
                        broadcast_c(g, n + 2)
                        broadcast_b(g, n + 2)
                    if n > 0 and h is not None:
                        front_step(h, n)
                    if n > 0:
                        sum_state(g, n - 1)
                    if n == 5 and tail is not None:
                        tail_pe(c, pe, tail + n0, c.y_bank)
                    if n == 0 and tail is not None:
                        project_out(tail)
                sum_state(g, NS - 1)

            def tail(g):
                project_out(g)
                tail_pe(c, pe, g + n0, c.y_bank)

            pe.wait_ge(zeros_set, 1)
            pe.wait_ge(setup_done, 1)
            run(pe.Fori, front, group, tail)

        @block.scalar
        def _(act):
            def taken(h, name):
                act.wait_ge(ring_done, number(h, name) + 1)
                return ring_bank[ENTRIES.index(name) % 2]

            def front_step(h, n):
                if n == 3:
                    for t in range(TD):
                        src = taken(h, f"in{t}")
                        act.activation(conv[:, t, :], src[:, :], ACT.Identity, scale=c.w["m_conv"][:, t, KC - 1:KC],
                                       bias=c.w["m_conv_bias"][:, t:t + 1])
                        act.activation(padded[:, t, :, KC - 1:], by_sequence(src[:, :]), ACT.Copy).then_inc(ring_free, 1)
                if n == 8:
                    for t in range(TD):
                        act.wait_ge(conv_done, h * TD + (t + 1))
                        act.activation(u[:, t, :], conv[:, t, :], ACT.Silu).then_inc(u_done, 1)
                    act.preload_act_table_set(LOG_EXP)
                    for t in range(TD):
                        act.wait_ge(gate_done, h + 1)
                        act.activation(z[:, t, :], taken(h, f"z{t}")[:, :], ACT.Copy).then_inc(ring_free, 1)
                if n == 11:
                    act.activation(dt_in[0:DR, :], taken(h, "dt")[0:DR, :], ACT.Copy).then_inc(ring_free, 1)
                    src = taken(h, "bc")
                    act.activation(high[:, :], src[0:3 * BC, :], ACT.Copy)
                    act.activation(bc[:, :], src[0:3 * BC, :], ACT.Copy).then_inc(ring_free, 1)
                if n == 13:
                    for t in range(TD):
                        src = taken(h, f"delta{t}")
                        bias = c.w["m_dt_bias"][:, t:t + 1]
                        act.activation(exp_v[:, t, :], src[:, :], ACT.Abs, bias=bias).then_inc(abs_done, 1)
                        act.activation(positive[:, t, :], src[:, :], ACT.Relu, bias=bias).then_inc(ring_free, 1)
                    act.wait_ge(abs_done, h * TD + TD)
                    act.activation(exp_v[:, :, :], exp_v[:, :, :], ACT.Exp, scale=-1.0).then_inc(exp_v_done, 1)
                if n == 13:
                    act.wait_ge(rest_done, h + 1)
                    act.activation(mid[:, :], rest[:, :], ACT.Copy).then_inc(mid_done, 1)
                if n == 14:
                    act.wait_ge(lost_done, h + 1)
                    act.activation(log_part[:, :, :], one_plus[:, :, :], ACT.Ln).then_inc(log_done, 1)
                if n == 15:
                    act.wait_ge(rest2_done, h + 1)
                    act.wait_ge(b_done, h * NS + 1)
                    for rows, part in ((slice(0, BC), high), (slice(BC, 2 * BC), mid), (slice(2 * BC, 3 * BC), rest2)):
                        last = act.activation(parts[rows, :], part[rows, :], ACT.Copy)
                    last.then_inc(parts_ready, 1)

            def front(h):
                for n in range(NS):
                    front_step(h, n)

            def copy_c(g, n):
                act.wait_ge(c_done, g * NS + (n + 1))
                act.wait_ge(read_done, (g * NS + n) * TD + 2)
                act.activation(c_wide[:, n % RC, :], c_bank[:, :], ACT.Copy).then_inc(c_copied, 1)

            def group(g, h, tail):
                act.wait_ge(delta_done, g + 1)
                for n in range(NS):
                    if n >= 1:
                        copy_c(g, n - 1)
                    for t in range(TD):
                        m = n * TD + t
                        act.wait_ge(scanned, g * U + (m + 1))
                        act.activation(unit(decay, m % RD), by_sequence(delta[:, t, :]), ACT.Exp,
                                       scale=minus_a[:, t, n:n + 1]).then_inc(decay_done, 1)
                    if n == 9 and tail is not None:
                        tail_act(c, act, tail + n0, c.y_bank)
                    if n == 6:
                        act.wait_ge(summed, g * U + RR + 1)
                        act.wait_ge(y_ready, g * TD + 2)
                        act.activation(gate[:, :, :], z[:, :, :], ACT.Silu).then_inc(gate_done, 1)
                        if h is None:
                            act.preload_act_table_set(LOG_EXP)
                    if h is not None:
                        front_step(h, n)
                copy_c(g, NS - 1)

            act.preload_act_table_set(LOG_EXP)
            act.activation(minus_a[:, :, :], c.w["m_a_log"][:, :, :], ACT.Exp).then_inc(a_exp, 1)
            act.wait_ge(zeros_set, 1)
            act.wait_ge(setup_done, 1)
            ones_credit(act, [(ring_free, 2), (c_copied, 1), (gate_done, 1)])
            run(act.Fori, front, group, lambda g: tail_act(c, act, g + n0, c.y_bank))

        @block.vector
        def _(dve):
            def tap(h, k, t):
                if k == 1:
                    dve.wait_ge(ring_free, number(h, f"in{t}") + 3)
                first = KC - 1 - k
                src = padded[:, t, :, first:first + P]
                out = by_sequence(conv[:, t, :])
                weight = c.w["m_conv"][:, t, first:first + 1]
                last = dve.scalar_tensor_tensor(out, src, weight, out, ALU.mult, ALU.add)
                if k == KC - 1:
                    last.then_inc(conv_done, 1)

            def front_step(h, m):
                if 6 <= m < 4 + KC * TD:
                    tap(h, (m - 4) // TD, m % TD)
                    if m % TD == TD - 1:
                        dve.drain()
                if m == 22:
                    dve.wait_ge(ring_free, number(h, "bc") + 3)
                    dve.tensor_tensor(rest[:, :], bc[:, :], high[:, :], ALU.subtract).then_inc(rest_done, 1)
                if m == 25:
                    dve.wait_ge(exp_v_done, h + 1)
                    dve.tensor_scalar(one_plus[:, :, :], exp_v[:, :, :], 1.0, None, ALU.add).then_inc(one_plus_done, 1)
                if m == 26:
                    dve.wait_ge(mid_done, h + 1)
                    dve.tensor_tensor(rest2[:, :], rest[:, :], mid[:, :], ALU.subtract).then_inc(rest2_done, 1)
                if m == 26:
                    dve.wait_ge(one_plus_done, h + 1)
                    dve.scalar_tensor_tensor(lost[:, :, :], one_plus[:, :, :], -1.0, exp_v[:, :, :],
                                             ALU.add, ALU.subtract).then_inc(lost_done, 1)

            def make_delta(h):
                dve.wait_ge(linear_done, h + 1)
                dve.wait_ge(log_done, h + 1)
                dve.wait_ge(decay_done, h * U + 1)
                dve.tensor_tensor(delta[:, :, :], positive[:, :, :], log_part[:, :, :], ALU.add).then_inc(delta_done, 1)

            def make_du(h):
                dve.wait_ge(delta_done, h + 1)
                dve.tensor_tensor(du[:, :, :], delta[:, :, :], u[:, :, :], ALU.mult)
                dve.drain()

            def drive_unit(g, m):
                n, t = m // TD, m % TD
                dve.wait_ge(b_done, g * NS + (n + 2))
                dve.wait_ge(scanned, g * U + (m + 1 + RD - R))
                dve.tensor_tensor(unit(drive, m % R), by_sequence(b_bank[n % 2][:, :]), by_sequence(du[:, t, :]),
                                  ALU.mult).then_inc(drive_done, 1)

            def scan_unit(g, m):
                dve.wait_ge(decay_done, g * U + (m + 2))
                dve.wait_ge(drive_done, g * U + (m + 5))
                dve.wait_ge(read_done, g * U + (m + 1 + R))
                dve.tensor_tensor_scan(state[:, m % R, :], decay[:, m % RD, :], drive[:, m % R, :], 0.0,
                                       ALU.mult, ALU.add).then_inc(scanned, 1)

            def gated_output(g):
                for t in range(TD):
                    dve.wait_ge(summed, g * U + (U - TD + t + 1 + RR))
                    if t == 0:
                        dve.wait_ge(gate_done, g + 2)
                        dve.wait_ge(out_done, g + 1)
                    dve.tensor_tensor(y[:, t, :], sum_bank[t][:, :], gate[:, t, :], ALU.mult).then_inc(y_ready, 1)

            def tail_step(g, m):
                if m == 0:
                    gated_output(g)
                if m == 5:
                    dve.wait_ge(out_done, g + 2)
                    tail_dve_variance(c, dve, g + n0)
                if m == 9:
                    tail_dve_norm(c, dve, g + n0)

            def front(h):
                for m in range(U):
                    front_step(h, m)
                make_delta(h)
                make_du(h)

            def group(g, h, tail):
                drive_unit(g, 0)
                for m in range(U):
                    if m + 1 < U:
                        drive_unit(g, m + 1)
                    if m == U - 1 and h is not None:
                        make_delta(h)
                    scan_unit(g, m)
                    if h is not None:
                        front_step(h, m)
                    if tail is not None:
                        tail_step(tail, m)
                if h is not None:
                    make_du(h)

            def tail(g):
                for m in range(U):
                    tail_step(g, m)

            dve.wait_ge(a_exp, 1)
            dve.tensor_scalar(minus_a[:, :, :], minus_a[:, :, :], -1.0, None, ALU.mult)
            for t in range(TD):
                last = dve.tensor_scalar(diagonal[:, t, :], c.w["ident"][:, :], c.w["m_d"][:, t:t + 1], None, ALU.mult)
            last.then_inc(setup_done, 1)
            dve.wait_ge(zeros_set, 1)
            ones_credit(dve, [(drive_done, 4), (scanned, RD), (read_done, 2 * R), (summed, RR), (y_ready, 2), (out_done, 1),
                              (decay_done, 1), (b_done, 1)])
            run(dve.Fori, front, group, tail)
    memory.close()



KEPT = ["ident", "part_rows", "minus_half"]
EARLY = ["causal", "a_wq", "a_wk", "a_wv", "a_wo"]
WEIGHTS = {
    "ident": ([P, P], F32), "part_rows": ([P, 2 * NS], F32), "causal": ([P, P], F32), "minus_half": ([P, G], F32),
    "a_wq": ([P, AH * AD], F32), "a_wk": ([P, AH * AD], F32), "a_wv": ([P, AH * AD], F32),
    "a_wo": ([P, 8, P], F32),
    "earlier": ([P, E, E], F32), "e_router": ([P, E], F32), "e_experts": ([P, E, P], F32),
    "m_in": ([P, 2 * DI], F32), "m_conv": ([P, 2, KC], F32), "m_conv_bias": ([P, 2], F32),
    "m_x_proj": ([P, 2, DR + 6 * NS], F32), "m_dt": ([P, DI], F32), "m_dt_bias": ([P, 2], F32),
    "m_a_log": ([P, 2, NS], F32), "m_d": ([P, 2], F32), "m_out": ([P, 2, P], F32),
    "f_router": ([P, E], F32), "f_w1": ([P, E, P], F32), "f_w2": ([P, E, P], F32), "f_w3": ([P, E, P], F32),
    "f_b1": ([P, E], F32), "f_b2": ([P, E], F32), "f_b3": ([P, E], F32),
    "f_sw1": ([P, 2, P], F32), "f_sw2": ([P, 2, P], F32), "f_sw3": ([P, 2, P], F32),
    "ones_row": ([1, P], F32), "head_of": ([P, XH], F32),
    "own_head": ([P, 4], F32),
    "x0_wq": ([P, P], F32), "x0_wk": ([P, P], F32), "x0_wv": ([P, P], F32), "x0_wo": ([P, P], F32),
    "x0_bq": ([P, 1], F32), "x0_bk": ([P, 1], F32), "x0_bv": ([SC, P], F32), "x0_bo": ([1, P], F32),
    "x0_select": ([P, 3, 3], F32), "x0_feat_bias": ([3, 1], F32),
    "x0_w1": ([3, 64], F32), "x0_b1": ([64, 1], F32), "x0_w2": ([64, P], F32), "x0_b2": ([64, 1], F32),
    "x0_w3": ([64, P], F32), "x0_b3": ([P, 1], F32),
    "x1_wq": ([P, P], F32), "x1_wk": ([P, P], F32), "x1_wv": ([P, P], F32), "x1_wo": ([P, P], F32),
    "x1_bo": ([1, P], F32),
}


def decoder(nc, dram, out, stages=(0, 1, 2, 3, 4, 5)):
    c = Core()
    c.x_dram = dram["x"].rearrange("b p d -> p b d")
    c.xT_dram = dram["xT"]
    c.dram = dram
    c.out_dram = out.rearrange("b p d -> p b d")
    c.sem = nc.alloc_semaphore
    c.sb = lambda name, shape, dtype=F32: nc.alloc_sbuf_tensor(name, shape, dtype)
    psum = nc.alloc_psum_tensor("psum", [P, 8, 512], F32)
    c.psum = psum
    c.bank = lambda i: psum[:, i, :]
    c.y_bank = c.bank(7)
    early_memory = ExitStack()
    late = [name for name in WEIGHTS if name not in EARLY + KEPT]
    c.w = {name: c.sb("w_" + name, *WEIGHTS[name]) for name in KEPT + late}
    c.part_rows = c.sb("part_rows16", [P, 2 * NS], BF16)
    c.ident16, c.zeros16, c.causal16 = (c.sb(name, [P, n], BF16) for name, n in
                                        (("ident16", P), ("zeros16", W), ("causal16", W)))
    c.x_all = c.sb("x_all", [P, B, P])
    c.xT_all = c.sb("xT_all", [P, B * P])
    c.xs = c.sb("xs", [P, G, P])
    c.xTs = c.sb("xTs", [P, W])
    c.ctxTs = c.sb("ctxTs", [P, G * SC])
    c.ys = c.sb("ys", [P, G, P])
    c.yTs = c.sb("yTs", [P, W])
    c.resid = c.sb("resid", [P, G, P])
    c.bn = c.sb("bn", [P, G, 6])
    c.meanvar = c.sb("meanvar", [P, G, 2])
    c.var_eps = c.sb("var_eps", [P, G])
    c.rstd = c.sb("rstd", [P, G])
    c.w |= {name: early_memory.enter_context(nc.sbuf_tensor("w_" + name, *WEIGHTS[name])) for name in EARLY}

    c.early_loaded, c.late_loaded = c.sem("early_loaded"), c.sem("late_loaded")
    c.late = late
    c.resid_done = c.sem("resid_done")
    c.var_done, c.rstd_done = c.sem("var_done"), c.sem("rstd_done")
    c.y_normed, c.y_transposed = c.sem("y_normed"), c.sem("y_transposed")
    c.y_stored, c.yT_copied, c.yT_stored = c.sem("y_stored"), c.sem("yT_copied"), c.sem("yT_stored")
    c.xs_loaded, c.xTs_loaded, c.xTs_used = c.sem("xs_loaded"), c.sem("xTs_loaded"), c.sem("xTs_used")
    c.ctx_loaded = c.sem("ctx_loaded")

    with nc.Block() as block:
        @block.sync
        def _(sp):
            ones_credit(sp, [(c.resid_done, 1), (c.y_stored, 16), (c.yT_stored, 16), (c.y_transposed, 1),
                             (c.yT_copied, 1), (c.xTs_used, 1)])
            for name in KEPT + EARLY:
                sp.dma_start(c.w[name][:], dram[name]).then_inc(c.early_loaded, 16)
            sp.wait_ge(c.early_loaded, 16 * len(KEPT + EARLY))
            if stages[0] != 0:
                load_late(c, sp)
                sp.wait_ge(c.late_loaded, 16 * len(late))

        @block.gpsimd
        def _(pool):
            pool.memset(c.zeros16[:, :], 0.0)

        @block.vector
        def _(dve):
            dve.wait_ge(c.early_loaded, 16 * len(KEPT + EARLY))
            dve.tensor_copy(c.ident16[:, :], c.w["ident"][:, :])
            dve.tensor_copy(c.part_rows[:, :], c.w["part_rows"][:, :])
            dve.tensor_copy(c.causal16[:, :].rearrange("p (m t) -> p m t", m=G),
                            c.w["causal"][:, :].unsqueeze(1).broadcast_to([P, G, P]))

    for stage in stages:
        c.last = stage == stages[-1]
        c.n0 = stages.index(stage) * NG
        c.ctx0 = sum(x in (1, 4) for x in stages[:stages.index(stage)]) * NG
        STAGES[stage](c, nc, stage)
        if stage == 0:
            early_memory.close()


STAGES = {0: causal_attention, 1: cross_attention, 2: linear_experts, 3: mamba, 4: cross_attention,
          5: gated_experts}



def by_block(rows):
    return rows.reshape(2, P, *rows.shape[1:]).swapaxes(0, 1)


def block_diagonal(weight):
    import numpy as np
    out = np.zeros((P, P), weight.dtype)
    for h in range(XH):
        out[h * XD:(h + 1) * XD, h * XD:(h + 1) * XD] = weight
    return out


def statistics_weights():
    import numpy as np
    out = np.zeros((P, 3, 3), np.float32)
    out[:, 0, 0] = XD ** -0.5 / (P * SC)
    out[:, 1, 1] = XD ** -0.5 / P
    out[:, 2, 2] = 1.0 / (P * (SC - 1))
    return out


def layouts(a):
    import numpy as np
    f32 = np.float32
    token = np.arange(P)
    d = {
        "x": a["x"],
        "xT": a["x"].transpose(2, 0, 1).reshape(P, B * P),
        "ident": np.eye(P, dtype=f32),
        "causal": np.where(token[None, :] > token[:, None], f32(-1e30), f32(0.0)),
        "minus_half": np.full((P, G), -0.5, f32),
        "a_wq": a["L0_attn_w_q"].transpose(2, 0, 1).reshape(P, AH * AD),
        "a_wk": a["L0_attn_w_k"].transpose(2, 0, 1).reshape(P, AH * AD),
        "a_wv": a["L0_attn_w_v"].transpose(2, 0, 1).reshape(P, AH * AD),
        "a_wo": a["L0_attn_w_o"].T.reshape(8, P, P).transpose(1, 0, 2),
        "earlier": np.broadcast_to(np.arange(E)[None, :] < np.arange(E)[:, None], (P, E, E)).astype(f32),
        "e_router": a["L0_ffn_router_w"].T, "e_experts": a["L0_ffn_expert_weights"].transpose(1, 0, 2),
        "m_in": a["L1_attn_in_proj_w"].T, "m_conv": by_block(a["L1_attn_conv_w"][:, 0, :]),
        "m_conv_bias": by_block(a["L1_attn_conv_b"]), 
        "m_x_proj": by_block(np.concatenate([a["L1_attn_x_proj_w"].T] + [a["L1_attn_x_proj_w"][DR:].T] * 2, 1)),
        "part_rows": ((token[:, None] % (2 * NS) == np.arange(2 * NS)[None, :]) & (token[:, None] < 6 * NS)).astype(f32),
        "m_dt": np.concatenate([a["L1_attn_dt_proj_w"].T, np.zeros((P - DR, DI), f32)]),
        "m_dt_bias": by_block(a["L1_attn_dt_proj_b"]), "m_a_log": by_block(a["L1_attn_A_log"]),
        "m_d": by_block(a["L1_attn_D"]), "m_out": by_block(a["L1_attn_out_proj_w"].T),
        "f_router": a["L1_ffn_gate_w"].T, "f_w1": a["L1_ffn_w1"].transpose(2, 0, 1),
        "f_w2": a["L1_ffn_w2"].transpose(2, 0, 1), "f_w3": a["L1_ffn_w3"].transpose(2, 0, 1),
        "f_b1": a["L1_ffn_b1"].T, "f_b2": a["L1_ffn_b2"].T, "f_b3": a["L1_ffn_b3"].T,
        "f_sw1": a["L1_ffn_sw1"].T.reshape(P, 2, P), "f_sw2": a["L1_ffn_sw2"].T.reshape(P, 2, P),
        "f_sw3": by_block(a["L1_ffn_sw3"].T),
        "ones_row": np.ones((1, P), f32),
        "head_of": (token[:, None] // XD == np.arange(XH)[None, :]).astype(f32),
        "own_head": (token[:, None] // XD % 4 == np.arange(4)[None, :]).astype(f32),
        "ctxT": a["ctx_1024"].transpose(2, 0, 1).reshape(P, B * SC),
        "mask": np.broadcast_to(a["mask_Bx1x1xS2_if1"].reshape(1, B * SC), (P, B * SC)),
        "x0_wq": a["L0_xattn_Wq"].T, "x0_wk": a["L0_xattn_Wk"].T, "x0_wv": a["L0_xattn_Wv"].T,
        "x0_wo": a["L0_xattn_Wo"].T,
        "x0_bq": a["L0_xattn_bq"][:, None], "x0_bk": a["L0_xattn_bk"][:, None],
        "x0_bv": np.broadcast_to(a["L0_xattn_bv"][None, :], (SC, P)), "x0_bo": a["L0_xattn_bo"][None, :],
        "x0_select": statistics_weights(),
        "x0_feat_bias": np.array([[0.0], [0.0], [-1.0 / (SC * (SC - 1))]], f32),
        "x0_w1": a["L0_xattn_w1"].T, "x0_b1": a["L0_xattn_b1"][:, None],
        "x0_w2": np.concatenate([a["L0_xattn_w2"].T, np.zeros((64, 64), f32)], 1), "x0_b2": a["L0_xattn_b2"][:, None],
        "x0_w3": np.broadcast_to(a["L0_xattn_w3"].T, (64, P)),
        "x0_b3": np.broadcast_to(a["L0_xattn_b3"][None, :], (P, 1)),
        "x1_wq": block_diagonal(a["L1_xattn_Wq"]), "x1_wk": block_diagonal(a["L1_xattn_Wk"]),
        "x1_wv": block_diagonal(a["L1_xattn_Wv"].T), "x1_wo": a["L1_xattn_Wo"].T,
        "x1_bo": a["L1_xattn_bo"][None, :],
    }
    return {k: np.ascontiguousarray(v) for k, v in d.items()}


def kernel(**inputs):
    import numpy as np
    import concourse.bacc as bacc
    from concourse.bass_utils import run_bass_kernel_spmd

    arrays = layouts({name: np.asarray(value) for name, value in inputs.items()})
    nc = bacc.Bacc("TRN2", target_bir_lowering=False, num_devices=1)
    dram = {name: nc.dram_tensor("in_" + name, v.shape, mybir.dt.from_np(v.dtype), kind="ExternalInput").ap()
            for name, v in arrays.items()}
    out = nc.dram_tensor("out", (B, P, P), F32, kind="ExternalOutput").ap()
    decoder(nc, dram, out)
    result = run_bass_kernel_spmd(nc, [{"in_" + name: v for name, v in arrays.items()}], core_ids=[0])
    return result.results[0]["out"]
```
